# Optimizing a Trainium2 kernel written in Bass

```python
import numpy as np
import jax
import jax.numpy as jnp

def _softmax(x, axis=-1):
    return jax.nn.softmax(x, axis=axis)

def _gelu(x):
    return jax.nn.gelu(x, approximate=True)

def _silu(x):
    return jax.nn.silu(x)

def _sigmoid(x):
    return jax.nn.sigmoid(x)

def _layernorm(x, axis=-1, eps=1e-05):
    m = jnp.mean(x, axis=axis, keepdims=True)
    v = jnp.var(x, axis=axis, keepdims=True)
    return (x - m) / jnp.sqrt(v + eps)

def _scatter_add(tgt, idx, src, axis=0):
    return tgt.at[idx].add(src)

def _segment_sum(src, seg, n):
    return jax.ops.segment_sum(src, seg, n)
kernel_name = 'mk_gnn_resnorm_d4_gnn_r16_839b92'

def setup_inputs(seed: int=0):
    np.random.seed(seed)
    _w = jnp.asarray

    def _rec_inputs():
        import jax
        import jax.numpy as jnp
        _gk = jax.random.key(seed)
        x = -0.0002117 + 1 * jax.random.normal(jax.random.fold_in(_gk, 1), (6250, 256), jnp.float32)
        _s = jax.random.randint(jax.random.fold_in(_gk, 2), (50000,), 0, 6250, jnp.int32)
        _d = jax.random.randint(jax.random.fold_in(_gk, 3), (50000,), 0, 6250, jnp.int32)
        _loop = jnp.arange(6250, dtype=jnp.int32)
        src = jnp.concatenate([_s, _d, _loop])
        dst = jnp.concatenate([_d, _s, _loop])
        _o = jnp.argsort(dst, stable=True)
        src = src[_o]
        dst = dst[_o]
        edge_weight = jax.random.uniform(jax.random.fold_in(_gk, 13), (106250,), jnp.float32, 0.0, 1)
        return (x, src, dst, edge_weight)
    x, src, dst, edge_weight = _rec_inputs()

    def _L0_gnn_setup():
        import jax, jax.numpy as jnp
        import numpy as np
        N = 6250
        E = 200000
        D_IN = 256
        D_OUT = 256
        EPS = 1e-12
        key = jax.random.key(seed)
        k1, k2, k3, k4, k5, k6 = jax.random.split(key, 6)
        x = jax.random.normal(k1, (N, D_IN), dtype=jnp.float32)
        edge_src = jax.random.randint(k2, (E,), 0, N, dtype=jnp.int32)
        edge_dst = jax.random.randint(k3, (E,), 0, N, dtype=jnp.int32)
        edge_w = jax.random.uniform(k4, (E,), dtype=jnp.float32)
        w_self = jax.random.normal(k5, (D_OUT, D_IN), dtype=jnp.float32) * 0.05
        w_neigh = jax.random.normal(k6, (D_OUT, D_IN), dtype=jnp.float32) * 0.05
        return {'x': x, 'edge_src': edge_src, 'edge_dst': edge_dst, 'edge_w': edge_w, 'w_self': w_self, 'w_neigh': w_neigh}
    _L0_gnn_all = _L0_gnn_setup()
    _L0_gnn_in = {k: v for k, v in _L0_gnn_all.items() if k in ('w_self', 'w_neigh')}
    del _L0_gnn_all

    def _L1_gnn_setup():
        import jax, jax.numpy as jnp
        import numpy as np
        N_NODES = 6250
        N_EDGES = 18750
        HIDDEN = 256
        N_LAYERS = 3
        LN_EPS = 1e-05

        def _layer_norm(x, g, b):
            mu = jnp.mean(x, axis=-1, keepdims=True)
            var = jnp.mean(jnp.square(x - mu), axis=-1, keepdims=True)
            return (x - mu) * jax.lax.rsqrt(var + LN_EPS) * g + b

        def _gin_layer(h, src, dst, W1, b1, W2, b2, eps, gamma, beta):
            agg = jax.ops.segment_sum(h[src], dst, num_segments=N_NODES)
            z = (1.0 + eps) * h + agg
            m = jax.nn.relu(z @ W1 + b1) @ W2 + b2
            return jax.nn.relu(_layer_norm(m + h, gamma, beta))
        key = jax.random.key(seed)
        ks = jax.random.split(key, 6)
        h = jax.random.normal(ks[0], (N_NODES, HIDDEN), dtype=jnp.float32)
        edge_index = jax.random.randint(ks[1], (2, N_EDGES), 0, N_NODES, dtype=jnp.int64)
        scale = 1.0 / np.sqrt(HIDDEN)
        W1 = jax.random.normal(ks[2], (N_LAYERS, HIDDEN, HIDDEN), dtype=jnp.float32) * scale
        W2 = jax.random.normal(ks[3], (N_LAYERS, HIDDEN, HIDDEN), dtype=jnp.float32) * scale
        b1 = jnp.zeros((N_LAYERS, HIDDEN), dtype=jnp.float32)
        b2 = jnp.zeros((N_LAYERS, HIDDEN), dtype=jnp.float32)
        eps = jnp.zeros((N_LAYERS,), dtype=jnp.float32)
        gamma = jnp.ones((N_LAYERS, HIDDEN), dtype=jnp.float32)
        beta = jnp.zeros((N_LAYERS, HIDDEN), dtype=jnp.float32)
        return {'h': h, 'edge_index': edge_index, 'W1': W1, 'b1': b1, 'W2': W2, 'b2': b2, 'eps': eps, 'gamma': gamma, 'beta': beta}
    _L1_gnn_all = _L1_gnn_setup()
    _L1_gnn_in = {k: v for k, v in _L1_gnn_all.items() if k in ('W1', 'b1', 'W2', 'b2', 'eps', 'gamma', 'beta')}
    del _L1_gnn_all

    def _L2_gnn_setup():
        import jax, jax.numpy as jnp
        import numpy as np
        N_NODES = 1024
        N_EDGES = 16384
        D_IN = 256
        D = 256
        H = 512
        E = 64
        TOP_K = 2
        CAP = 1024
        BN_EPS = 1e-05

        def _moe_ff(x, Wg, bg, w1, b1, w2, b2):
            N = x.shape[0]
            logits = x @ Wg + bg
            vals, idx = jax.lax.top_k(logits, TOP_K)
            gates = jax.nn.softmax(vals, axis=-1)
            e_flat = idx.reshape(-1)
            g_flat = gates.reshape(-1)
            tok = jnp.arange(N * TOP_K) // TOP_K
            order = jnp.argsort(e_flat)
            e_s, tok_s, g_s = (e_flat[order], tok[order], g_flat[order])
            counts = jnp.bincount(e_flat, length=E)
            offs = jnp.concatenate([jnp.zeros((1,), counts.dtype), jnp.cumsum(counts)[:-1]])
            rank = jnp.arange(N * TOP_K) - offs[e_s]
            valid = rank < CAP
            slot = jnp.where(valid, e_s * CAP + rank, E * CAP)
            buf = jnp.zeros((E * CAP + 1, D), x.dtype).at[slot].set(x[tok_s])
            h = buf[:E * CAP].reshape(E, CAP, D)
            h1 = jax.nn.gelu(jnp.einsum('ecd,edh->ech', h, w1) + b1[:, None, :], approximate=False)
            h2 = jnp.einsum('ech,ehd->ecd', h1, w2) + b2[:, None, :]
            out_buf = h2.reshape(E * CAP, D)
            y_s = jnp.where(valid[:, None], out_buf[jnp.minimum(slot, E * CAP - 1)], 0.0)
            return jnp.zeros((N, D), x.dtype).at[tok_s].add(g_s[:, None] * y_s)

        def _forward(feats, W_gc, b_gc, W_res, b_res, Wg, bg, w1, b1, w2, b2, gamma, beta, src, dst):
            n = feats.shape[0]
            ones = jnp.ones((src.shape[0],), feats.dtype)
            deg_out = jnp.clip(jax.ops.segment_sum(ones, src, num_segments=n), 1.0)
            deg_in = jnp.clip(jax.ops.segment_sum(ones, dst, num_segments=n), 1.0)
            h = feats * jax.lax.rsqrt(deg_out)[:, None]
            m = jax.ops.segment_sum(h[src], dst, num_segments=n) * jax.lax.rsqrt(deg_in)[:, None]
            gc = m @ W_gc + b_gc
            x = gc + (feats @ W_res + b_res)
            core = _moe_ff(x, Wg, bg, w1, b1, w2, b2)
            y = x + core
            mean = jnp.mean(y, axis=0)
            var = jnp.mean((y - mean) ** 2, axis=0)
            return (y - mean) * jax.lax.rsqrt(var + BN_EPS) * gamma + beta
        key = jax.random.key(seed)
        ks = jax.random.split(key, 16)
        s = lambda d: 1.0 / np.sqrt(d)
        inp = {'feats': jax.random.normal(ks[0], (N_NODES, D_IN), jnp.float32), 'W_gc': jax.random.normal(ks[1], (D_IN, D), jnp.float32) * s(D_IN), 'b_gc': jnp.zeros((D,), jnp.float32), 'W_res': jax.random.normal(ks[2], (D_IN, D), jnp.float32) * s(D_IN), 'b_res': jnp.zeros((D,), jnp.float32), 'Wg': jax.random.normal(ks[3], (D, E), jnp.float32) * s(D), 'bg': jnp.zeros((E,), jnp.float32), 'w1': jax.random.normal(ks[4], (E, D, H), jnp.float32) * s(D), 'b1': jnp.zeros((E, H), jnp.float32), 'w2': jax.random.normal(ks[5], (E, H, D), jnp.float32) * s(H), 'b2': jnp.zeros((E, D), jnp.float32), 'gamma': jnp.ones((D,), jnp.float32), 'beta': jnp.zeros((D,), jnp.float32), 'src': jax.random.randint(ks[6], (N_EDGES,), 0, N_NODES), 'dst': jax.random.randint(ks[7], (N_EDGES,), 0, N_NODES)}
        return inp
    _L2_gnn_all = _L2_gnn_setup()
    _L2_gnn_in = {k: v for k, v in _L2_gnn_all.items() if k in ('W_gc', 'b_gc', 'W_res', 'b_res', 'Wg', 'bg', 'w1', 'b1', 'w2', 'b2', 'gamma', 'beta')}
    del _L2_gnn_all

    def _L3_gnn_setup():
        import jax, jax.numpy as jnp
        import numpy as np
        N_NODES = 6250
        key = jax.random.key(seed)
        k = jax.random.split(key, 7)
        N, E, F_IN, F_OUT = (N_NODES, 200000, 256, 256)
        stdv = 1.0 / np.sqrt(F_OUT)
        return {'x': jax.random.normal(k[0], (N, F_IN), dtype=jnp.float32), 'edge_row': jax.random.randint(k[1], (E,), 0, N, dtype=jnp.int32), 'edge_col': jax.random.randint(k[2], (E,), 0, N, dtype=jnp.int32), 'edge_val': jax.random.uniform(k[3], (E,), dtype=jnp.float32), 'weight': jax.random.uniform(k[4], (F_IN, F_OUT), dtype=jnp.float32, minval=-stdv, maxval=stdv), 'learnable_diag': 0.01 * jax.random.normal(k[5], (F_IN,), dtype=jnp.float32), 'bias': jax.random.uniform(k[6], (F_OUT,), dtype=jnp.float32, minval=-stdv, maxval=stdv)}
    _L3_gnn_all = _L3_gnn_setup()
    _L3_gnn_in = {k: v for k, v in _L3_gnn_all.items() if k in ('weight', 'learnable_diag', 'bias')}
    del _L3_gnn_all
    return {'x': x, 'src': src, 'dst': dst, 'edge_weight': edge_weight, 'L0_gnn_w_self': _L0_gnn_in['w_self'], 'L0_gnn_w_neigh': _L0_gnn_in['w_neigh'], 'L1_gnn_W1': _L1_gnn_in['W1'], 'L1_gnn_b1': _L1_gnn_in['b1'], 'L1_gnn_W2': _L1_gnn_in['W2'], 'L1_gnn_b2': _L1_gnn_in['b2'], 'L1_gnn_eps': _L1_gnn_in['eps'], 'L1_gnn_gamma': _L1_gnn_in['gamma'], 'L1_gnn_beta': _L1_gnn_in['beta'], 'L2_gnn_W_gc': _L2_gnn_in['W_gc'], 'L2_gnn_b_gc': _L2_gnn_in['b_gc'], 'L2_gnn_W_res': _L2_gnn_in['W_res'], 'L2_gnn_b_res': _L2_gnn_in['b_res'], 'L2_gnn_Wg': _L2_gnn_in['Wg'], 'L2_gnn_bg': _L2_gnn_in['bg'], 'L2_gnn_w1': _L2_gnn_in['w1'], 'L2_gnn_b1': _L2_gnn_in['b1'], 'L2_gnn_w2': _L2_gnn_in['w2'], 'L2_gnn_b2': _L2_gnn_in['b2'], 'L2_gnn_gamma': _L2_gnn_in['gamma'], 'L2_gnn_beta': _L2_gnn_in['beta'], 'L3_gnn_weight': _L3_gnn_in['weight'], 'L3_gnn_learnable_diag': _L3_gnn_in['learnable_diag'], 'L3_gnn_bias': _L3_gnn_in['bias']}

def reference(x, src, dst, edge_weight, L0_gnn_w_self, L0_gnn_w_neigh, L1_gnn_W1, L1_gnn_b1, L1_gnn_W2, L1_gnn_b2, L1_gnn_eps, L1_gnn_gamma, L1_gnn_beta, L2_gnn_W_gc, L2_gnn_b_gc, L2_gnn_W_res, L2_gnn_b_res, L2_gnn_Wg, L2_gnn_bg, L2_gnn_w1, L2_gnn_b1, L2_gnn_w2, L2_gnn_b2, L2_gnn_gamma, L2_gnn_beta, L3_gnn_weight, L3_gnn_learnable_diag, L3_gnn_bias):
    import jax
    import jax.numpy as jnp

    def _L0_gnn_ref(x, edge_src, edge_dst, edge_w, w_self, w_neigh):
        import jax, jax.numpy as jnp
        import numpy as np
        N = 6250
        E = 200000
        D_IN = 256
        D_OUT = 256
        EPS = 1e-12
        x_self = x @ w_self.T
        msgs = edge_w[:, None] * x[edge_src]
        x_neigh = jax.ops.segment_sum(msgs, edge_dst, num_segments=N)
        x_neigh = x_neigh @ w_neigh.T
        out = x_self + x_neigh
        norm = jnp.sqrt(jnp.sum(out * out, axis=1, keepdims=True))
        return out / jnp.maximum(norm, EPS)

    def _L1_gnn_ref(h, edge_index, W1, b1, W2, b2, eps, gamma, beta):
        import jax, jax.numpy as jnp
        import numpy as np
        N_NODES = 6250
        N_EDGES = 18750
        HIDDEN = 256
        N_LAYERS = 3
        LN_EPS = 1e-05

        def _layer_norm(x, g, b):
            mu = jnp.mean(x, axis=-1, keepdims=True)
            var = jnp.mean(jnp.square(x - mu), axis=-1, keepdims=True)
            return (x - mu) * jax.lax.rsqrt(var + LN_EPS) * g + b

        def _gin_layer(h, src, dst, W1, b1, W2, b2, eps, gamma, beta):
            agg = jax.ops.segment_sum(h[src], dst, num_segments=N_NODES)
            z = (1.0 + eps) * h + agg
            m = jax.nn.relu(z @ W1 + b1) @ W2 + b2
            return jax.nn.relu(_layer_norm(m + h, gamma, beta))
        src, dst = (edge_index[0], edge_index[1])
        for l in range(N_LAYERS):
            h = _gin_layer(h, src, dst, W1[l], b1[l], W2[l], b2[l], eps[l], gamma[l], beta[l])
        return h

    def _L2_gnn_ref(feats, W_gc, b_gc, W_res, b_res, Wg, bg, w1, b1, w2, b2, gamma, beta, src, dst):
        import jax, jax.numpy as jnp
        import numpy as np
        N_NODES = 1024
        N_EDGES = 16384
        D_IN = 256
        D = 256
        H = 512
        E = 64
        TOP_K = 2
        CAP = 1024
        BN_EPS = 1e-05

        def _moe_ff(x, Wg, bg, w1, b1, w2, b2):
            N = x.shape[0]
            logits = x @ Wg + bg
            vals, idx = jax.lax.top_k(logits, TOP_K)
            gates = jax.nn.softmax(vals, axis=-1)
            e_flat = idx.reshape(-1)
            g_flat = gates.reshape(-1)
            tok = jnp.arange(N * TOP_K) // TOP_K
            order = jnp.argsort(e_flat)
            e_s, tok_s, g_s = (e_flat[order], tok[order], g_flat[order])
            counts = jnp.bincount(e_flat, length=E)
            offs = jnp.concatenate([jnp.zeros((1,), counts.dtype), jnp.cumsum(counts)[:-1]])
            rank = jnp.arange(N * TOP_K) - offs[e_s]
            valid = rank < CAP
            slot = jnp.where(valid, e_s * CAP + rank, E * CAP)
            buf = jnp.zeros((E * CAP + 1, D), x.dtype).at[slot].set(x[tok_s])
            h = buf[:E * CAP].reshape(E, CAP, D)
            h1 = jax.nn.gelu(jnp.einsum('ecd,edh->ech', h, w1) + b1[:, None, :], approximate=False)
            h2 = jnp.einsum('ech,ehd->ecd', h1, w2) + b2[:, None, :]
            out_buf = h2.reshape(E * CAP, D)
            y_s = jnp.where(valid[:, None], out_buf[jnp.minimum(slot, E * CAP - 1)], 0.0)
            return jnp.zeros((N, D), x.dtype).at[tok_s].add(g_s[:, None] * y_s)

        def _forward(feats, W_gc, b_gc, W_res, b_res, Wg, bg, w1, b1, w2, b2, gamma, beta, src, dst):
            n = feats.shape[0]
            ones = jnp.ones((src.shape[0],), feats.dtype)
            deg_out = jnp.clip(jax.ops.segment_sum(ones, src, num_segments=n), 1.0)
            deg_in = jnp.clip(jax.ops.segment_sum(ones, dst, num_segments=n), 1.0)
            h = feats * jax.lax.rsqrt(deg_out)[:, None]
            m = jax.ops.segment_sum(h[src], dst, num_segments=n) * jax.lax.rsqrt(deg_in)[:, None]
            gc = m @ W_gc + b_gc
            x = gc + (feats @ W_res + b_res)
            core = _moe_ff(x, Wg, bg, w1, b1, w2, b2)
            y = x + core
            mean = jnp.mean(y, axis=0)
            var = jnp.mean((y - mean) ** 2, axis=0)
            return (y - mean) * jax.lax.rsqrt(var + BN_EPS) * gamma + beta
        return _forward(feats, W_gc, b_gc, W_res, b_res, Wg, bg, w1, b1, w2, b2, gamma, beta, src, dst)

    def _L3_gnn_ref(x, edge_row, edge_col, edge_val, weight, learnable_diag, bias):
        import jax, jax.numpy as jnp
        import numpy as np
        N_NODES = 6250
        gathered = edge_val[:, None] * x[edge_col]
        e1 = jax.ops.segment_sum(gathered, edge_row, num_segments=N_NODES)
        e2 = e1 * (learnable_diag + 1.0)
        e4 = x - e2
        out = e4 @ weight + bias
        return out
    edge_index = jnp.stack([src, dst])
    x = _layernorm(x + _L0_gnn_ref(x, src, dst, edge_weight, L0_gnn_w_self, L0_gnn_w_neigh), axis=-1)
    x = _layernorm(x + _L1_gnn_ref(x, edge_index, L1_gnn_W1, L1_gnn_b1, L1_gnn_W2, L1_gnn_b2, L1_gnn_eps, L1_gnn_gamma, L1_gnn_beta), axis=-1)
    x = _layernorm(x + _L2_gnn_ref(x, L2_gnn_W_gc, L2_gnn_b_gc, L2_gnn_W_res, L2_gnn_b_res, L2_gnn_Wg, L2_gnn_bg, L2_gnn_w1, L2_gnn_b1, L2_gnn_w2, L2_gnn_b2, L2_gnn_gamma, L2_gnn_beta, src, dst), axis=-1)
    x = _layernorm(x + _L3_gnn_ref(x, src, dst, edge_weight, L3_gnn_weight, L3_gnn_learnable_diag, L3_gnn_bias), axis=-1)
    return x

_drawn_inputs = setup_inputs


def setup_inputs(seed=0):
    import zlib

    import numpy as np

    out = dict(_drawn_inputs(seed))
    spreads = {'L1_gnn_b1': (0.0, 0.1),
     'L1_gnn_b2': (0.0, 0.1),
     'L1_gnn_eps': (0.0, 0.51),
     'L1_gnn_gamma': (1.0, 0.2),
     'L1_gnn_beta': (0.0, 0.1),
     'L2_gnn_b_gc': (0.0, 0.1),
     'L2_gnn_b_res': (0.0, 0.1),
     'L2_gnn_bg': (0.0, 0.1),
     'L2_gnn_b1': (0.0, 0.368),
     'L2_gnn_b2': (0.0, 0.267),
     'L2_gnn_gamma': (1.0, 0.2),
     'L2_gnn_beta': (0.0, 0.1)}
    factors = {'L3_gnn_learnable_diag': 6.308, 'L3_gnn_bias': 3.337}
    for name, (base, spread) in spreads.items():
        noise = np.random.default_rng([zlib.crc32(name.encode()), seed]).standard_normal(out[name].shape)
        drawn = base * np.exp(spread * noise) if base else spread * noise
        out[name] = jnp.asarray(drawn.astype(out[name].dtype))
    for name, factor in factors.items():
        out[name] = (out[name] * factor).astype(out[name].dtype)
    return out
```

```python
import concourse.bass as bass
from concourse import mybir
from contextlib import ExitStack

N = 6250
E = 106250
D = 256
P = 128
NT = -(-N // P)
LAST = N - (NT - 1) * P
NPAD = NT * P
QT = 4
NQ = -(-NT // QT)
QW = QT * D
EP = 125
EC = E // EP
HALF = 8
ROUND = 2 * HALF
EW = -(-EC // ROUND) * ROUND
ER = EW // ROUND
NCH = -(-((E + (P - 1) * NT) // P) // ROUND) * ROUND
NR = NCH // ROUND
REC_ROWS = NCH * P + P * EW
PASSES = 6
NE = 64
HID = 512
CAP = 1024
MC = -(-((2 * N + (P - 1) * NE) // P) // 3) * 3
MG = MC // 3
XS_ROWS = MC * P + 2 * NT * P
LN_EPS = 1e-5
BIG = 3.0e38


def gnn(nc, a, out):
    f32, i32, u32, bf16 = mybir.dt.float32, mybir.dt.int32, mybir.dt.uint32, mybir.dt.bfloat16
    ALU, ACT, AX = mybir.AluOpType, mybir.ActivationFunctionType, mybir.AxisListType
    DS = bass.DynSlice
    ctx = ExitStack()
    with ctx:
        def sb(name, cols, dt=f32, rows=P):
            return ctx.enter_context(nc.sbuf_tensor(name, [rows, cols], dt))

        def sem(name):
            return ctx.enter_context(nc.semaphore(name))

        def dram(name, shape, dt=f32):
            return nc.dram_tensor(name, shape, dt, kind="Internal").ap()

        recs = [dram(f"edge_records{b}", (REC_ROWS, 4)) for b in range(2)]
        tables = [a["x"]] + [dram(f"table{k}", (NPAD, D)) for k in range(1, PASSES)]
        xs_dram = dram("expert_inputs", (XS_ROWS, D))
        ys_dram = dram("expert_outputs", (MC * P, D))

        X = sb("X", NT * D)
        Hb = sb("Hb", NT * D)
        ACC = sb("ACC", NT * D)
        ring = sb("ring", ROUND * D)
        pick = sb("pick", ROUND * P)
        REC = sb("REC", NCH * 4)
        TTS = [sb(f"TT{b}", NCH, i32) for b in range(2)]
        WA = sb("WA", 2 * 2 * D)
        VEC = sb("VEC", 4 * D)
        B1C = sb("B1C", 2)
        EPS1 = sb("EPS1", 1)
        STG = sb("STG", ROUND * 4)
        IDX = sb("IDX", ROUND, u32)
        iota = sb("iota", P)
        ident = sb("ident", P)
        tri = sb("tri", P)
        trii = sb("trii", P)
        ones = sb("ones", P)
        onesl = sb("onesl", P)
        RIN = sb("RIN", NT)
        ROUT = sb("ROUT", NT)
        CNT = sb("CNT", NE)
        OFF = sb("OFF", NE)
        col = sb("col", 8)
        coli = sb("coli", 2, i32)
        nchb = sb("nchb", P)
        ST = sb("ST", QT * 6)
        MV = sb("MV", QT * 2)
        SM = sb("SM", QT * 6)
        WG = sb("WG", 2 * NE)
        BG = sb("BG", NE)
        IM = sb("IM", NE)
        iotam = sb("iotam", MC)
        DUMP = sb("DUMP", 2 * NT)
        G12 = sb("G12", 2 * NT)
        ET = sb("ET", MC, i32)
        PS = ctx.enter_context(nc.psum_tensor("PS", [P, 8 * 512], f32))

        def bank(b, w=512, off=0):
            return PS[:, b * 512 + off:b * 512 + off + w]

        Z = ring[:, 0:2 * QW]
        ZT = ring[:, 2 * QW:4 * QW]
        M1T = pick[:, 0:QW]
        U = pick[:, QW:2 * QW]

        s_const = sem("constants_made")
        s_clean = sem("buffers_cleared")
        s_in = sem("edges_loaded")
        s_x = sem("x_loaded")
        s_w = sem("weights_loaded")
        s_wt = sem("weights_transposed")
        s_wtc = sem("weight_transposes_copied")
        s_init = sem("records_initialised")
        s_zero = sem("expert_inputs_zeroed")
        s_dve = sem("vector_steps")
        s_act = sem("scalar_steps")
        s_cnt = sem("tile_counts_made")
        s_psort = sem("sort_products_done")
        s_pos = sem("edge_positions_made")
        s_stage = sem("indices_staged")
        s_slot = [sem(f"slot{j}_moved") for j in range(ROUND)]
        s_rec = sem("records_loaded")
        s_oh = sem("one_hots_built")
        s_hist = sem("histogram_halves_done")
        s_deg = sem("degrees_made")
        s_degq = sem("degree_roots_made")
        s_pick = sem("pick_halves_built")
        s_prod = sem("product_halves_done")
        s_acc = sem("chunks_accumulated")
        s_z = sem("operands_ready")
        s_t = sem("operands_transposed")
        s_zt = sem("transposes_copied")
        s_mm1 = sem("first_products_done")
        s_m1 = sem("hidden_ready")
        s_mm = sem("layer_products_done")
        s_nrm = sem("norms_made")
        s_u = sem("products_consumed")
        s_var = sem("variances_ready")
        s_sd = sem("deviations_ready")
        s_rs = sem("scales_ready")
        s_ln = sem("rows_normalised")
        s_aff = sem("affine_applied")
        s_fin = sem("outputs_final")
        s_tab = sem("tables_stored")
        s_gate = sem("gate_inputs_copied")
        s_t2 = sem("gate_inputs_transposed")
        s_t2c = sem("gate_transposes_copied")
        s_lg = sem("logits_done")
        s_lgc = sem("logits_copied")
        s_gap = sem("gate_gaps_made")
        s_exp = sem("gate_exponentials_made")
        s_route = sem("route_steps_made")
        s_rk = sem("rank_products_done")
        s_rkc = sem("ranks_copied")
        s_xsc = sem("expert_inputs_scattered")
        s_wl = [sem(f"expert_weights{j}_loaded") for j in range(3)]
        s_xl = [sem(f"expert_rows{j}_loaded") for j in range(3)]
        s_et = sem("expert_inputs_transposed")
        s_xt = sem("expert_transposes_copied")
        s_h = sem("expert_hidden_done")
        s_g = sem("expert_gelu_done")
        s_y = sem("expert_products_done")
        s_yc = sem("expert_outputs_copied")
        s_ys = [sem(f"expert_outputs{j}_stored") for j in range(3)]
        s_b1 = sem("expert_biases_loaded")
        s_b1t = sem("expert_biases_transposed")
        s_b1c = sem("expert_biases_copied")
        s_comb = [sem(f"combine_slot{j}_gathered") for j in range(8)]
        s_cu = sem("combined")
        s_bnv = sem("batch_vectors_loaded")
        s_cen = sem("rows_centred")
        s_csq = sem("centred_rows_squared")
        s_bnm = sem("batch_sums_done")
        s_bns = sem("batch_root_made")
        s_out = sem("output_stored")
        s_idle = sem("waits_that_stood_alone")

        def hcols(n, dt=f32):
            v = Hb[:, n * EW:(n + 1) * EW]
            return v.bitcast(dt) if dt != f32 else v

        SRC, DST, TMI = hcols(0, i32), hcols(1, i32), hcols(2, i32)
        WE, HI, LO, SHI, SLO, RK, TMP, OH, CUM = (hcols(n) for n in range(3, 12))
        TMJ = hcols(13, i32)
        POS = [hcols(12, u32), hcols(11, u32)]
        EDUMP = pick[:, 0:EW]
        IOTC = pick[:, EW:EW + NCH]
        RECE = ring[:, 0:EW * 4].rearrange("p (c f) -> p c f", f=4)
        RECV = REC[:, :].rearrange("p (c f) -> p c f", f=4)
        OHL = [pick[:, h * 512:(h + 1) * 512].bitcast(bf16).rearrange("p (c m) -> p c m", c=HALF) for h in range(2)]
        OHH = [pick[:, 1024 + h * 256:1024 + h * 256 + HALF * NT // 2].bitcast(bf16).rearrange("p (c m) -> p c m", c=HALF)
               for h in range(2)]

        GW = NT * NE
        LOG, OH1, OH2, MM = (Hb[:, n * GW:(n + 1) * GW] for n in range(4))
        W1B = [Hb[:, j * 2048:j * 2048 + 1024] for j in range(3)]
        W2B = [Hb[:, j * 2048 + 1024:j * 2048 + 2048] for j in range(3)]
        HT = [Hb[:, 6144 + j * 512:6656 + j * 512] for j in range(3)]
        XSB = [Hb[:, 7680 + j * 256:7936 + j * 256] for j in range(3)]
        XTB = [Hb[:, 8448 + j * 256:8704 + j * 256] for j in range(3)]
        YB = [Hb[:, 9216 + j * 256:9472 + j * 256] for j in range(3)]
        B2B = [Hb[0:1, 9984 + j * 256:10240 + j * 256] for j in range(3)]
        B1T = Hb[:, 11008:11264]
        B1R = pick[0:NE, 0:HID]
        RNK = ring[:, 0:GW]
        RT = ring[:, GW:GW + 4 * NT]
        SI = ring[:, GW + 4 * NT:GW + 6 * NT].bitcast(u32)
        GI = ring[:, GW + 6 * NT:GW + 8 * NT].bitcast(u32)
        RB = 448

        block = ctx.enter_context(nc.Block())

        def wait(e, s, value):
            e.wait_ge(s, value)
            if not isinstance(value, int):
                e.sem_inc(s_idle, 1)

        class Steps:

            def __init__(self, e, s):
                self.e, self.s, self.at, self.n, self.alone = e, s, 0, 0, False

            def link(self, ins):
                ins.then_inc(self.s, 1)
                self.at = self.at + 1
                self.n += 1
                wait(self.e, self.s, self.at) if self.alone else self.e.wait_ge(self.s, self.at)
                self.alone = False

            def loop(self, start, end, per):
                base, n = self.at, self.n
                with self.e.Fori(start, end) as i:
                    self.at = (i - start) * per + base if per else base
                    yield i
                assert self.n - n == per, (self.n - n, per)
                self.at = base + (end - start) * per

        def groups(e, steps=None, per=0):
            last = NT - (NQ - 1) * QT
            yield 0, QT, QT
            if steps is None:
                with e.Fori(1, NQ - 2) as q:
                    yield q, QT, QT
            else:
                yield from ((q, QT, QT) for q in steps.loop(1, NQ - 2, per))
            yield NQ - 2, QT, last
            yield NQ - 1, last, 0

        def chunks(e):
            for j in range(3):
                yield 0, j, j
            with e.Fori(1, MG - 1) as g:
                for j in range(3):
                    yield g, j, g * 3 + j
            for j in range(3):
                yield MG - 1, j, (MG - 1) * 3 + j

        def fixed(v):
            return isinstance(v, int)

        def at(buf, c, w=1):
            return buf[:, c:c + w] if fixed(c) else buf[:, DS(c, w)]

        def part(buf, q, nt):
            return at(buf, q * QW, nt * D)

        def tiles(v, nt):
            return v.rearrange("p (t d) -> p t d", t=nt)

        def vec(n, nt):
            return VEC[:, n * D:(n + 1) * D].unsqueeze(1).broadcast_to((P, nt, D))

        def wmat(m, k):
            return WA[:, (m * 2 + k) * D:(m * 2 + k + 1) * D]

        def ln_count(k, q, second=0):
            base = {0: 0, 1: NQ, 2: 2 * NQ, 3: 3 * NQ, "bn": 5 * NQ, 5: 6 * NQ}[k]
            return base + (2 * q + second if k == 3 else q) + 1

        W_DMAS = [2, 7, 7, 7, 6, 3]

        def w_count(k):
            return 16 * sum(W_DMAS[:k + 1])

        def operands(k):
            return 2 if k in (0, 4) else 1

        w1_rows = a["L2_gnn_w1"].rearrange("e d h -> (e d) h")
        w2_rows = a["L2_gnn_w2"].rearrange("e h d -> (e h) d")
        SQ = VEC[:, 0:D]
        CMAP = Hb[:, 9 * EW:9 * EW + NCH]

        def expert_moves(pool):
            pool.wait_ge(s_zero, 64)
            pool.wait_ge(s_route, 3)
            for n in range(2 * NT):
                t, s = n // 2, n % 2
                pool.indirect_dma_start(xs_dram, bass.IndirectOffsetOnAxis(ap=SI[:, s * NT + t:s * NT + t + 1], axis=0),
                                        ACC[:, t * D:(t + 1) * D], None).then_inc(s_xsc, 16)
            for g, j, c in chunks(pool):
                wait(pool, s_yc, c + 1)
                rows = ys_dram[c * P:(c + 1) * P, :] if fixed(c) else ys_dram[DS(c * P, P), :]
                pool.dma_start(rows, YB[j]).then_inc(s_ys[j], 16)
            for j in range(3):
                pool.wait_ge(s_ys[j], 16 * MG)
            for n in range(2 * NT):
                t, s = n // 2, n % 2
                if n >= 8:
                    pool.wait_ge(s_cu, n - 7)
                pool.indirect_dma_start(ring[:, n % 8 * D:(n % 8 + 1) * D], None, ys_dram,
                                        bass.IndirectOffsetOnAxis(ap=GI[:, s * NT + t:s * NT + t + 1], axis=0)).then_inc(s_comb[n % 8], 16)

        def expert_products(pe):
            mm = nc.tensor.matmul
            pe.wait_ge(s_route, 1)
            for b in range(GW // RB):
                mm(bank(b, RB), tri[:, :], MM[:, b * RB:(b + 1) * RB], start=True, stop=False)
                mm(bank(b, RB), ones[:, :], LOG[:, b * RB:(b + 1) * RB], start=False, stop=True)
            mm(bank(7, 1)[0:NE, :], CNT[:, :], ones[:, 0:1], start=True, stop=True).then_inc(s_rk, 1)
            pe.wait_ge(s_route, 2)
            mm(bank(7, NE, 64), nchb[0:NE, :], tri[0:NE, 0:NE], start=True, stop=True)
            mm(bank(7, 1, 192)[0:NE, :], trii[0:NE, 0:NE], col[0:NE, 1:2], start=True, stop=True).then_inc(s_rk, 1)
            pe.wait_ge(s_gap, 2)
            mm(bank(7, MC, 256)[0:1, :], ones[0:NE, 0:1], pick[0:NE, 0:MC], start=True, stop=True).then_inc(s_rk, 1)
            pe.wait_ge(s_route, 3)
            pe.wait_ge(s_b1, 16)
            for m in range(4):
                last = nc.tensor.transpose(bank(6, NE, m * NE), B1R[:, m * P:(m + 1) * P], ident[0:NE, 0:NE])
            last.then_inc(s_b1t, 1)

            def transpose(g, j, c):
                pe.wait_ge(s_xl[j], g * 16 + 16)
                if not (fixed(c) and c == 0):
                    pe.wait_ge(s_xt, c)
                for b in range(2):
                    last = nc.tensor.transpose(bank(0, P, b * P), XSB[j][:, b * P:(b + 1) * P], ident[:, :])
                last.then_inc(s_et, 1)

            def hidden(g, j, c):
                pe.wait_ge(s_xt, c + 1)
                pe.wait_ge(s_wl[j], g * 48 + 48)
                if not (fixed(c) and c < 3):
                    pe.wait_ge(s_g, c - 2)
                for m in range(4):
                    for b in range(2):
                        last = mm(bank(3 + j, P, m * P), W1B[j][:, b * HID + m * P:b * HID + (m + 1) * P],
                                  XTB[j][:, b * P:(b + 1) * P], start=b == 0, stop=b == 1)
                last.then_inc(s_h, 1)

            def output(j, c):
                pe.wait_ge(s_g, c + 1)
                if not (fixed(c) and c == 0):
                    pe.wait_ge(s_yc, c)
                for m in range(4):
                    mm(bank(1, D), HT[j][:, m * P:(m + 1) * P], W2B[j][:, m * D:(m + 1) * D], start=m == 0, stop=False)
                mm(bank(1, D), ones[0:1, :], B2B[j], start=False, stop=True).then_inc(s_y, 1)

            transpose(0, 0, 0)
            for g, j, c in chunks(pe):
                if not (fixed(c) and c == MC - 1):
                    transpose(g + (j == 2), (j + 1) % 3, c + 1)
                hidden(g, j, c)
                if not (fixed(c) and c == 0):
                    output((j + 2) % 3, c - 1)
            output((MC - 1) % 3, MC - 1)

            pe.wait_ge(s_cu, 2 * NT)
            mm(bank(0, D), ones[:, :], ACC[:, 0:D], start=True, stop=False)
            with pe.Fori(1, NT - 1) as t:
                mm(bank(0, D), ones[:, :], ACC[:, DS(t * D, D)], start=False, stop=False, skip_group_check=True)
            mm(bank(0, D), onesl[:, :], ACC[:, (NT - 1) * D:NT * D], start=False, stop=True).then_inc(s_bnm, 1)
            for q, nt, nxt in groups(pe):
                pe.wait_ge(s_csq, q + 1)
                for t in range(nt):
                    last = mm(bank(1, D), ones[:, :] if nxt else onesl[:, :], Z[:, t * D:(t + 1) * D],
                              start=fixed(q) and q == 0 and t == 0, stop=not nxt, skip_group_check=True)
                last.then_inc(s_bnm, 1)

        def expert_scalar(act, S, normalise):
            fn = nc.scalar.activation
            act.wait_ge(s_gap, 1)
            fn(RT[:, 0:NT], RT[:, 0:NT], ACT.Exp).then_inc(s_exp, 1)
            act.wait_ge(s_rk, 1)
            for b in range(GW // RB):
                last = fn(RNK[:, b * RB:(b + 1) * RB], bank(b, RB), ACT.Copy)
            last.then_inc(s_rkc, 1)
            act.wait_ge(s_b1t, 1)
            fn(B1T, bank(6, 4 * NE), ACT.Copy).then_inc(s_b1c, 1)
            act.wait_ge(s_b1c, 1)
            for g, j, c in chunks(act):
                wait(act, s_h, c + 1)
                if not (fixed(c) and c < 3):
                    wait(act, s_y, c - 2)
                e = act.value_load(ET[0:1, c:c + 1] if fixed(c) else ET[0:1, DS(c, 1)], min_val=0, max_val=NE - 1)
                for m in range(4):
                    last = fn(HT[j][:, m * P:(m + 1) * P], bank(3 + j, P, m * P), ACT.Gelu, bias=Hb[:, DS(e + (11008 + m * NE), 1)])
                last.then_inc(s_g, 1)
            for q, nt, _ in groups(act):
                wait(act, s_cen, q + 1)
                if not (fixed(q) and q == 0):
                    wait(act, s_bnm, q + 1)
                fn(Z[:, 0:nt * D], part(ACC, q, nt), ACT.Square).then_inc(s_csq, 1)
            act.wait_ge(s_bns, 1)
            fn(VEC[:, 2 * D:3 * D], VEC[:, 2 * D:3 * D], ACT.Sqrt).then_inc(s_bns, 1)
            for q, nt, _ in groups(act):
                normalise("bn", q, nt, part(X, q, nt)).then_inc(s_fin, 1)

        def expert_vector(dve, V, statistics):
            v = nc.vector
            dve.wait_ge(s_lgc, NQ)
            g3 = lambda b: b.rearrange("p (t e) -> p t e", e=NE)
            over_e = lambda c: c.unsqueeze(2).broadcast_to((P, NT, NE))
            over_t = lambda c: c.unsqueeze(1).broadcast_to((P, NT, NE))
            best, second, sel = RT[:, NT:2 * NT], RT[:, 2 * NT:3 * NT], RT[:, 3 * NT:4 * NT]

            def top(value, oh):
                V.link(v.tensor_reduce(value, g3(LOG), AX.X, ALU.max))
                V.link(v.tensor_tensor(g3(MM), g3(LOG), over_e(value), ALU.is_equal))
                V.link(v.tensor_tensor(g3(MM), g3(MM), over_t(IM[:, :]), ALU.mult))
                V.link(v.tensor_reduce(sel, g3(MM), AX.X, ALU.min))
                V.link(v.tensor_tensor(g3(oh), over_t(IM[:, :]), over_e(sel), ALU.is_equal))

            top(best, OH1)
            V.link(v.scalar_tensor_tensor(LOG, OH1, -BIG, LOG, ALU.mult, ALU.add))
            top(second, OH2)
            v.tensor_tensor(RT[:, 0:NT], second, best, ALU.subtract).then_inc(s_gap, 1)
            dve.wait_ge(s_exp, 1)
            V.link(v.tensor_scalar(G12[:, 0:NT], RT[:, 0:NT], 1.0, None, ALU.add))
            V.link(v.reciprocal(G12[:, 0:NT], G12[:, 0:NT]))
            V.link(v.tensor_tensor(G12[:, NT:2 * NT], G12[:, 0:NT], RT[:, 0:NT], ALU.mult))
            V.link(v.tensor_tensor(MM, OH1, OH2, ALU.add))
            v.tensor_scalar(MM[:, (NT - 1) * NE:], MM[:, (NT - 1) * NE:], onesl[:, 0:1], None, ALU.mult)
            V.link(v.memset(LOG[:, 0:NE], 0.0))
            for t in V.loop(1, NT, 1):
                V.link(v.tensor_tensor(Hb[:, DS(t * NE, NE)], Hb[:, DS(t * NE - NE, NE)], Hb[:, DS(t * NE + (3 * GW - NE), NE)], ALU.add))
            v.tensor_tensor(CNT[:, :], LOG[:, (NT - 1) * NE:], MM[:, (NT - 1) * NE:], ALU.add).then_inc(s_route, 1)
            dve.wait_ge(s_rk, 1)
            V.link(v.tensor_scalar(coli[0:NE, 0:1], bank(7, 1)[0:NE, :], float(CAP), float(P - 1), ALU.min, ALU.add))
            V.link(v.tensor_scalar(coli[0:NE, 1:2], coli[0:NE, 0:1], 7, None, ALU.arith_shift_right))
            V.link(v.tensor_copy(col[0:NE, 1:2], coli[0:NE, 1:2]))
            v.tensor_scalar(nchb[0:NE, :], ones[0:NE, :], col[0:NE, 1:2], float(P), ALU.mult, ALU.mult).then_inc(s_route, 1)
            dve.wait_ge(s_rk, 2)
            v.tensor_copy(OFF[:, :], bank(7, NE, 64))
            V.link(v.tensor_copy(col[0:NE, 2:3], bank(7, 1, 192)[0:NE, :]))
            v.tensor_scalar(pick[0:NE, 0:MC], iotam[0:NE, :], col[0:NE, 2:3], None, ALU.is_ge).then_inc(s_gap, 1)
            dve.wait_ge(s_rk, 3)
            V.link(v.tensor_scalar(ET[0:1, :], bank(7, MC, 256)[0:1, :], float(NE - 1), None, ALU.min))
            dve.wait_ge(s_rkc, 1)
            rank, ok = best, second
            for s, oh in enumerate((OH1, OH2)):
                c = slice(s * NT, (s + 1) * NT)
                V.link(v.tensor_tensor(LOG, oh, RNK, ALU.mult))
                V.link(v.tensor_reduce(rank, g3(LOG), AX.X, ALU.add))
                V.link(v.tensor_scalar(ok, rank, float(CAP), None, ALU.is_lt))
                V.link(v.tensor_scalar(ok[:, NT - 1:NT], ok[:, NT - 1:NT], onesl[:, 0:1], None, ALU.mult))
                V.link(v.tensor_tensor(g3(LOG), g3(oh), over_t(OFF[:, :]), ALU.mult))
                V.link(v.tensor_reduce(sel, g3(LOG), AX.X, ALU.add))
                V.link(v.tensor_tensor(sel, sel, rank, ALU.add))
                v.tensor_tensor(G12[:, c], G12[:, c], ok, ALU.mult)
                v.tensor_tensor(GI[:, c], sel, ok, ALU.mult)
                V.link(v.tensor_tensor(sel, sel, DUMP[:, c], ALU.subtract))
                V.link(v.tensor_tensor(sel, sel, ok, ALU.mult))
                last = v.tensor_tensor(SI[:, c], sel, DUMP[:, c], ALU.add)
                if s == 0:
                    V.link(last)
            last.then_inc(s_route, 1)

            def copy_in(g, j, c):
                dve.wait_ge(s_et, c + 1)
                if not (fixed(c) and c < 3):
                    dve.wait_ge(s_h, c - 2)
                v.tensor_copy(XTB[j], bank(0, D)).then_inc(s_xt, 1)

            dve.wait_ge(s_b1c, 1)
            copy_in(0, 0, 0)
            for g, j, c in chunks(dve):
                if not (fixed(c) and c == MC - 1):
                    copy_in(g + (j == 2), (j + 1) % 3, c + 1)
                dve.wait_ge(s_y, c + 1)
                if not (fixed(g) and g == 0):
                    dve.wait_ge(s_ys[j], g * 16)
                v.tensor_copy(YB[j], bank(1, D)).then_inc(s_yc, 1)
            for n in range(2 * NT):
                t, s = n // 2, n % 2
                dve.wait_ge(s_comb[n % 8], 16 * (n // 8 + 1))
                if n:
                    dve.wait_ge(s_cu, n)
                acc = ACC[:, t * D:(t + 1) * D]
                v.scalar_tensor_tensor(acc, ring[:, n % 8 * D:(n % 8 + 1) * D], G12[:, s * NT + t:s * NT + t + 1], acc,
                                       ALU.mult, ALU.add).then_inc(s_cu, 1)
            dve.wait_ge(s_bnm, 1)
            V.link(v.tensor_scalar(VEC[:, 3 * D:4 * D], bank(0, D), 1.0 / N, None, ALU.mult))
            for q, nt, _ in groups(dve):
                acc = tiles(part(ACC, q, nt), nt)
                v.tensor_tensor(acc, acc, vec(3, nt), ALU.subtract).then_inc(s_cen, 1)
            dve.wait_ge(s_bnm, NQ + 1)
            dve.wait_ge(s_bnv, 32)
            v.tensor_scalar(VEC[:, 2 * D:3 * D], bank(1, D), 1.0 / N, LN_EPS, ALU.mult, ALU.add).then_inc(s_bns, 1)
            dve.wait_ge(s_bns, 2)
            V.link(v.reciprocal(VEC[:, 2 * D:3 * D], VEC[:, 2 * D:3 * D]))
            V.link(v.tensor_tensor(VEC[:, 2 * D:3 * D], VEC[:, 2 * D:3 * D], VEC[:, 0:D], ALU.mult))
            dve.wait_ge(s_cen, NQ)
            for q, nt, _ in groups(dve, V, 6):
                if not (fixed(q) and q == 0):
                    dve.wait_ge(s_fin, q + NQ * 4)
                u = tiles(U[:, 0:nt * D], nt)
                V.link(v.tensor_tensor(u, tiles(part(ACC, q, nt), nt), vec(2, nt), ALU.mult))
                V.link(v.tensor_tensor(u, u, vec(1, nt), ALU.add))
                V.link(v.tensor_tensor(U[:, 0:nt * D], U[:, 0:nt * D], part(X, q, nt), ALU.add))
                statistics("bn", q, nt)

        @block.sync
        def _(sp):
            sp.wait_ge(s_clean, 1)
            for dst, name in ((SRC, "src"), (DST, "dst"), (WE, "edge_weight")):
                sp.dma_start(dst[0:EP, 0:EC], a[name].rearrange("(p c) -> p c", c=EC)).then_inc(s_in, 16)
            sp.dma_start(tiles(X[:, 0:(NT - 1) * D], NT - 1),
                         a["x"][0:(NT - 1) * P, :].rearrange("(t p) d -> p t d", p=P)).then_inc(s_x, 16)
            sp.dma_start(X[0:LAST, (NT - 1) * D:NT * D], a["x"][(NT - 1) * P:N, :]).then_inc(s_x, 16)

            def weights(k):
                def mat(slot, src):
                    sp.dma_start(WA[:, slot * 2 * D:(slot + 1) * 2 * D].rearrange("p (k n) -> p k n", k=2),
                                 src.rearrange("(k p) n -> p k n", p=P)).then_inc(s_w, 16)

                def row(slot, src):
                    sp.dma_start(VEC[:, slot * D:(slot + 1) * D], src.partition_broadcast(P)).then_inc(s_w, 16)

                if k == 0:
                    mat(0, a["L0_gnn_w_neigh"])
                    mat(1, a["L0_gnn_w_self"])
                elif k <= 3:
                    mat(0, a["L1_gnn_W1"][k - 1])
                    mat(1, a["L1_gnn_W2"][k - 1])
                    row(0, a["L1_gnn_b2"][k - 1])
                    row(1, a["L1_gnn_gamma"][k - 1])
                    row(2, a["L1_gnn_beta"][k - 1])
                    sp.dma_start(B1C[:, :], a["L1_gnn_b1"][k - 1].rearrange("(k p) -> p k", p=P),
                                 allow_slow_non_contiguous=True).then_inc(s_w, 16)
                    sp.dma_start(EPS1[:, :], a["L1_gnn_eps"][k - 1:k].partition_broadcast(P)).then_inc(s_w, 16)
                elif k == 4:
                    mat(0, a["L2_gnn_W_gc"])
                    mat(1, a["L2_gnn_W_res"])
                    row(0, a["L2_gnn_b_gc"])
                    row(1, a["L2_gnn_b_res"])
                    sp.dma_start(WG[:, :].rearrange("p (k n) -> p k n", k=2),
                                 a["L2_gnn_Wg"].rearrange("(k p) n -> p k n", p=P)).then_inc(s_w, 16)
                    sp.dma_start(BG[:, :], a["L2_gnn_bg"].partition_broadcast(P)).then_inc(s_w, 16)
                else:
                    mat(0, a["L3_gnn_weight"])
                    row(0, a["L3_gnn_bias"])
                    row(1, a["L3_gnn_learnable_diag"])

            weights(0)
            sp.wait_ge(s_clean, 2)
            for rec in recs:
                sp.dma_start(rec[0:NCH * P, :].rearrange("(p c) f -> p (c f)", p=P), REC[:, :]).then_inc(s_init, 16)
            xz = xs_dram[0:MC * P, :].rearrange("(p r) d -> p (r d)", p=P)
            for r in range(0, MC, NT):
                w = min(NT, MC - r) * D
                sp.dma_start(xz[:, r * D:r * D + w], ACC[:, 0:w]).then_inc(s_zero, 16)
            for j in range(ROUND):
                sp.wait_ge(s_slot[j], 16 * ER)
            sp.wait_ge(s_init, 32)
            sp.dma_start(REC[:, :], recs[0][0:NCH * P, :].rearrange("(p c) f -> p (c f)", p=P)).then_inc(s_rec, 16)

            def store_rows(k):
                for q, nt, _ in groups(sp):
                    src = Z[:, QW:QW + nt * D] if k == 3 else part(Hb if k in (1, 2) else X, q, nt)
                    sp.wait_ge(s_fin, q + NQ * k + 1)
                    if k == PASSES - 1 and fixed(q) and q == NQ - 1:
                        sp.dma_start(out[(NT - 1) * P:N, :], src[0:LAST, :]).then_inc(s_out, 16)
                        continue
                    table, s = (out, s_out) if k == PASSES - 1 else (tables[k + 1], s_tab)
                    rows = table[q * QT * P:(q * QT + nt) * P, :] if fixed(q) else table[DS(q * (QT * P), nt * P), :]
                    sp.dma_start(rows.rearrange("(t p) d -> p t d", p=P), tiles(src, nt)).then_inc(s, 16)

            for k in range(4):
                store_rows(k)
                weights(k + 1)
            for j in range(ROUND):
                sp.wait_ge(s_slot[j], 16 * 2 * ER)
            sp.wait_ge(s_acc, 5 * NCH)
            sp.wait_ge(s_stage, 4 * ER + 10 * NR)
            sp.dma_start(REC[:, :], recs[1][0:NCH * P, :].rearrange("(p c) f -> p (c f)", p=P)).then_inc(s_rec, 16)
            sp.wait_ge(s_xsc, 16 * 2 * NT)
            sp.wait_ge(s_route, 3)
            sp.dma_start(B1R, a["L2_gnn_b1"]).then_inc(s_b1, 16)
            for g, j, c in chunks(sp):
                e = sp.value_load(ET[0:1, c:c + 1] if fixed(c) else ET[0:1, DS(c, 1)], min_val=0, max_val=NE - 1)
                if not (fixed(g) and g == 0):
                    sp.wait_ge(s_y, c - 2)
                sp.dma_start(W1B[j].rearrange("p (k n) -> p k n", k=2),
                             w1_rows[DS(e * D, D), :].rearrange("(k p) n -> p k n", p=P)).then_inc(s_wl[j], 16)
                sp.dma_start(W2B[j].rearrange("p (k n) -> p k n", k=4),
                             w2_rows[DS(e * HID, HID), :].rearrange("(k p) n -> p k n", p=P)).then_inc(s_wl[j], 16)
                sp.dma_start(B2B[j], a["L2_gnn_b2"][DS(e, 1), :]).then_inc(s_wl[j], 16)
                sp.dma_start(XSB[j], xs_dram[c * P:(c + 1) * P, :] if fixed(c) else xs_dram[DS(c * P, P), :]).then_inc(s_xl[j], 16)
            sp.wait_ge(s_mm, 5 * NQ)
            sp.dma_start(VEC[:, 0:D], a["L2_gnn_gamma"].partition_broadcast(P)).then_inc(s_bnv, 16)
            sp.dma_start(VEC[:, D:2 * D], a["L2_gnn_beta"].partition_broadcast(P)).then_inc(s_bnv, 16)
            store_rows(4)
            weights(5)
            store_rows(5)
            sp.wait_ge(s_out, 16 * NQ)

        @block.gpsimd
        def _(pool):
            imprecise = dict(allow_small_or_imprecise_dtypes=True)
            pool.iota(iota[:, :], pattern=[[1, P]], base=0, channel_multiplier=0, **imprecise)
            pool.iota(iotam[:, :], pattern=[[1, MC]], base=0, channel_multiplier=0, **imprecise)
            pool.iota(IM[:, :], pattern=[[1, NE]], base=-NE, channel_multiplier=0, **imprecise)
            pool.iota(IOTC, pattern=[[1, NCH]], base=0, channel_multiplier=0, **imprecise)
            pool.iota(EDUMP, pattern=[[1, EW]], base=NCH * P, channel_multiplier=EW, **imprecise)
            pool.iota(DUMP[:, :], pattern=[[P, 2 * NT]], base=MC * P, channel_multiplier=1, **imprecise)
            pool.memset(ident[:, :], 0.0)
            pool.memset(ones[:, :], 1.0).then_inc(s_const, 1)
            pool.wait_ge(s_const, 1)
            pool.affine_select(out=ident[:, :], in_=ident[:, :], compare_op=ALU.not_equal, fill=1.0, base=0,
                               pattern=[[-1, P]], channel_multiplier=1)
            pool.affine_select(out=tri[:, :], in_=ones[:, :], compare_op=ALU.is_gt, fill=0.0, base=0,
                               pattern=[[1, P]], channel_multiplier=-1)
            pool.affine_select(out=trii[:, :], in_=ones[:, :], compare_op=ALU.is_ge, fill=0.0, base=0,
                               pattern=[[1, P]], channel_multiplier=-1)
            pool.affine_select(out=onesl[:, :], in_=ones[:, :], compare_op=ALU.is_ge, fill=0.0, base=LAST - 1,
                               pattern=[[0, P]], channel_multiplier=-1).then_inc(s_const, 1)

            def scatter_half(b, i, h):
                wait(pool, s_stage, i * 2 + 2 * ER * b + h + 1)
                for j in range(h * HALF, (h + 1) * HALF):
                    pool.indirect_dma_start(recs[b], bass.IndirectOffsetOnAxis(ap=IDX[:, j:j + 1], axis=0),
                                            STG[:, j * 4:j * 4 + 4], None).then_inc(s_slot[j], 16)

            pool.wait_ge(s_init, 32)
            for b in range(2):
                with pool.Fori(0, ER) as i:
                    for h in range(2):
                        scatter_half(b, i, h)

            def gather_half(k, i, h, first):
                n = i * 2 + 2 * NR * k + h
                wait(pool, s_stage, n + 4 * ER + 1)
                if not (first and k == 0):
                    wait(pool, s_prod, n - 1)
                for j in range(h * HALF, (h + 1) * HALF):
                    pool.indirect_dma_start(ring[:, j * D:(j + 1) * D], None, tables[k],
                                            bass.IndirectOffsetOnAxis(ap=IDX[:, j:j + 1], axis=0)).then_inc(s_slot[j], 16)

            for k in range(PASSES):
                if k == 5:
                    expert_moves(pool)
                if k:
                    wait(pool, s_tab, 16 * NQ * k)
                for h in range(2):
                    gather_half(k, 0, h, True)
                with pool.Fori(1, NR) as i:
                    for h in range(2):
                        gather_half(k, i, h, False)

        @block.tensor
        def _(pe):
            mm = nc.tensor.matmul
            pe.wait_ge(s_const, 2)
            for b in range(2):
                pe.wait_ge(s_cnt, 3 * b + 1)
                mm(bank(0, 1)[0:NT, :], CNT[:, 0:NT], ones[:, 0:1], start=True, stop=True).then_inc(s_psort, 1)
                pe.wait_ge(s_cnt, 3 * b + 2)
                mm(bank(1, NT), tri[:, :], CNT[:, 0:NT], start=True, stop=False)
                mm(bank(1, NT), nchb[0:NT, :], tri[0:NT, 0:NT], start=False, stop=True)
                mm(bank(2, 1)[0:NT, :], trii[0:NT, 0:NT], col[0:NT, 1:2], start=True, stop=True).then_inc(s_psort, 1)
                pe.wait_ge(s_cnt, 3 * b + 3)
                for c in range(2):
                    last = mm(bank(3 + c, NCH // 2)[0:1, :], ones[0:NT, 0:1], CMAP[0:NT, c * (NCH // 2):(c + 1) * (NCH // 2)],
                              start=True, stop=True)
                last.then_inc(s_psort, 1)

            def hist_half(b, i, h, start, stop):
                pe.wait_ge(s_oh, i * 2 + 2 * ER * b + h + 1)
                for j in range(HALF):
                    last = mm(bank(6 + b, NT), OHL[h][:, j, :], OHH[h][:, j, :], start=start and j == 0,
                              stop=stop and j == HALF - 1, skip_group_check=True)
                last.then_inc(s_hist, 1)

            for b in range(2):
                hist_half(b, 0, 0, True, False)
                hist_half(b, 0, 1, False, False)
                with pe.Fori(1, ER - 1) as i:
                    for h in range(2):
                        hist_half(b, i, h, False, False)
                hist_half(b, ER - 1, 0, False, False)
                hist_half(b, ER - 1, 1, False, True)

            pe.wait_ge(s_w, w_count(0))
            for m in range(2):
                for k in range(2):
                    for o in range(2):
                        last = nc.tensor.transpose(bank(m, P, k * D + o * P), wmat(m, o)[:, k * P:(k + 1) * P], ident[:, :])
            last.then_inc(s_wt, 1)
            pe.wait_ge(s_wtc, 1)
            pe.wait_ge(s_deg, 1)

            def prod_half(k, i, h, first):
                n = i * 2 + 2 * NR * k + h
                pe.wait_ge(s_pick, n + 1)
                if not (first and k == 0):
                    pe.wait_ge(s_acc, n * HALF - HALF)
                for j in range(h * HALF, (h + 1) * HALF):
                    pe.wait_ge(s_slot[j], i * 16 + 16 * (2 * ER + NR * k + 1))
                    last = mm(PS[:, j * D:(j + 1) * D], pick[:, j * P:(j + 1) * P], ring[:, j * D:(j + 1) * D],
                              start=True, stop=True)
                last.then_inc(s_prod, 1)

            def transposes(k, q, nt):
                pe.wait_ge(s_z, q + NQ * k + 1)
                if not (fixed(q) and q == 0 and k == 0):
                    pe.wait_ge(s_zt, q + NQ * k)
                for o in range(operands(k)):
                    for b in range(2):
                        for t in range(nt):
                            last = nc.tensor.transpose(bank(2 * o + b, P, t * P), Z[:, o * QW + t * D + b * P:o * QW + t * D + (b + 1) * P],
                                                       ident[:, :])
                last.then_inc(s_t, 1)

            def layer(k, q, nt, nxt):
                if k in (1, 2, 3):
                    pe.wait_ge(s_zt, q + NQ * k + 1)
                    if not (fixed(q) and q == 0 and k == 1):
                        pe.wait_ge(s_m1, q + NQ * (k - 1))
                    for b in range(2):
                        for d in range(2):
                            last = mm(bank(2 + b, nt * P), wmat(0, d)[:, b * P:(b + 1) * P], ZT[:, d * 512:d * 512 + nt * P],
                                      start=d == 0, stop=d == 1)
                    last.then_inc(s_mm1, 1)
                    if nxt:
                        transposes(k, q + 1, nxt)
                    pe.wait_ge(s_m1, q + NQ * (k - 1) + 1)
                    pairs = [(M1T, 0, 1, b) for b in range(2)]
                else:
                    pe.wait_ge(s_zt, q + NQ * k + 1)
                    if nxt:
                        transposes(k, q + 1, nxt)
                    pairs = [(ZT, o * 1024, o, b) for o in range(operands(k)) for b in range(2)]
                if not (fixed(q) and q == 0 and k == 0):
                    pe.wait_ge(s_u, q + NQ * k)
                biases = {0: 0, 4: 2}.get(k, 1)
                for t in range(nt):
                    o = bank(4 + t // 2, D, t % 2 * D)
                    for n, (src, base, m, b) in enumerate(pairs):
                        last = mm(o, src[:, base + b * 512 + t * P:base + b * 512 + (t + 1) * P], wmat(m, b), start=n == 0,
                                  stop=n == len(pairs) - 1 and not biases)
                    for v in range(biases):
                        last = mm(o, ones[0:1, :], VEC[0:1, v * D:(v + 1) * D], start=False, stop=v == biases - 1)
                last.then_inc(s_mm, 1)
                if k == 4:
                    pe.wait_ge(s_gate, q + 1)
                    if not (fixed(q) and q == 0):
                        pe.wait_ge(s_lgc, q)
                    for b in range(2):
                        for t in range(nt):
                            last = nc.tensor.transpose(bank(6 + b, P, t * P), U[:, t * D + b * P:t * D + (b + 1) * P], ident[:, :])
                    last.then_inc(s_t2, 1)
                    pe.wait_ge(s_t2c, q + 1)
                    for t in range(nt):
                        o = bank(6, NE, t * NE)
                        for b in range(2):
                            mm(o, M1T[:, b * 512 + t * P:b * 512 + (t + 1) * P], WG[:, b * NE:(b + 1) * NE], start=b == 0, stop=False)
                        last = mm(o, ones[0:1, :], BG[0:1, :], start=False, stop=True)
                    last.then_inc(s_lg, 1)

            for k in range(PASSES):
                if k == 5:
                    expert_products(pe)
                for h in range(2):
                    prod_half(k, 0, h, True)
                with pe.Fori(1, NR) as i:
                    for h in range(2):
                        prod_half(k, i, h, False)
                pe.wait_ge(s_w, w_count(k))
                transposes(k, 0, QT)
                for q, nt, nxt in groups(pe):
                    layer(k, q, nt, nxt)

        @block.scalar
        def _(act):
            S = Steps(act, s_act)
            fn = nc.scalar.activation

            def stage_scatter(b, i, h):
                if not (fixed(i) and i == 0 and b == 0):
                    for j in range(h * HALF, (h + 1) * HALF):
                        wait(act, s_slot[j], i * 16 + 16 * ER * b)
                c = i * ROUND + h * HALF
                fn(IDX[:, h * HALF:(h + 1) * HALF], at(POS[b], c, HALF), ACT.Copy)
                src = ring[:, c * 4:(c + HALF) * 4] if fixed(c) else ring[:, DS(c * 4, HALF * 4)]
                fn(STG[:, h * HALF * 4:(h + 1) * HALF * 4], src, ACT.Copy).then_inc(s_stage, 1)

            for b in range(2):
                act.wait_ge(s_pos, b + 1)
                for h in range(2):
                    stage_scatter(b, 0, h)
                with act.Fori(1, ER) as i:
                    for h in range(2):
                        stage_scatter(b, i, h)

            act.wait_ge(s_wt, 1)
            for m in range(2):
                last = fn(WA[:, m * 512:(m + 1) * 512], bank(m), ACT.Copy)
            last.then_inc(s_wtc, 1)
            act.wait_ge(s_deg, 1)
            fn(RIN[:, :], RIN[:, :], ACT.Sqrt)
            fn(ROUT[:, :], ROUT[:, :], ACT.Sqrt).then_inc(s_degq, 1)
            act.wait_ge(s_rec, 16)

            def stage_gather(k, i, h, first):
                if first and k == 0:
                    for j in range(h * HALF, (h + 1) * HALF):
                        act.wait_ge(s_slot[j], 16 * 2 * ER)
                else:
                    wait(act, s_prod, i * 2 + 2 * NR * k + h - 1)
                c = i * ROUND + h * HALF
                src = RECV[:, c:c + HALF, 0] if fixed(c) else RECV[:, DS(c, HALF), 0]
                fn(IDX[:, h * HALF:(h + 1) * HALF], src, ACT.Copy).then_inc(s_stage, 1)

            def copy_transposes(k, q, nt):
                act.wait_ge(s_t, q + NQ * k + 1)
                if not (fixed(q) and q == 0):
                    if k in (1, 2, 3):
                        act.wait_ge(s_mm1, q + NQ * (k - 1))
                    else:
                        act.wait_ge(s_mm, q + NQ * k)
                for b in range(2 * operands(k)):
                    last = fn(ZT[:, b * 512:b * 512 + nt * P], bank(b, nt * P), ACT.Copy)
                last.then_inc(s_zt, 1)

            def normalise(key, q, nt, dst, second=0):
                n = ln_count(key, q, second)
                act.wait_ge(s_var, n)
                fn(SM[:, 4:4 + nt], SM[:, 0:nt], ACT.Sqrt).then_inc(s_sd, 1)
                wait(act, s_rs, n)
                for t in range(nt):
                    last = fn(dst[:, t * D:(t + 1) * D], U[:, t * D:(t + 1) * D], ACT.Identity, bias=SM[:, 12 + t:13 + t],
                              scale=SM[:, 8 + t:9 + t])
                return last

            def finish(k, q, nt, nxt):
                if k == 0:
                    act.wait_ge(s_mm, q + 1)
                    if not (fixed(q) and q == 0):
                        act.wait_ge(s_u, q)
                    for t in range(nt):
                        last = fn(SQ[:, 0:D], bank(4 + t // 2, D, t % 2 * D), ACT.Square, accum_out=SM[:, 16 + t:17 + t])
                        S.link(last)
                    fn(SM[:, 20:20 + nt], SM[:, 16:16 + nt], ACT.Sqrt).then_inc(s_nrm, 1)
                if k in (1, 2, 3):
                    act.wait_ge(s_mm1, q + NQ * (k - 1) + 1)
                    if not (fixed(q) and q == 0 and k == 1):
                        act.wait_ge(s_mm, q + NQ * k)
                    for b in range(2):
                        last = fn(M1T[:, b * 512:b * 512 + nt * P], bank(2 + b, nt * P), ACT.Relu, bias=B1C[:, b:b + 1])
                    last.then_inc(s_m1, 1)
                if k == 4:
                    act.wait_ge(s_mm, q + NQ * 4 + 1)
                    if not (fixed(q) and q == 0):
                        act.wait_ge(s_t2, q)
                        act.wait_ge(s_u, q + NQ * 4)
                    for b in range(-(-nt // 2)):
                        w = min(2, nt - 2 * b) * D
                        last = fn(U[:, b * 512:b * 512 + w], bank(4 + b, w), ACT.Copy)
                    last.then_inc(s_gate, 1)
                if nxt:
                    copy_transposes(k, q + 1, nxt)
                if k == 4:
                    act.wait_ge(s_t2, q + 1)
                    for b in range(2):
                        last = fn(M1T[:, b * 512:b * 512 + nt * P], bank(6 + b, nt * P), ACT.Copy)
                    last.then_inc(s_t2c, 1)
                elif k in (0, 5):
                    normalise(k, q, nt, part(X, q, nt)).then_inc(s_fin, 1)
                else:
                    normalise(k, q, nt, U).then_inc(s_ln, 1)
                    if k < 3:
                        wait(act, s_aff, q + NQ * (k - 1) + 1)
                        fn(part(Hb, q, nt), U[:, 0:nt * D], ACT.Relu).then_inc(s_fin, 1)
                    else:
                        S.link(normalise(3, q, nt, part(X, q, nt), 1))
                        if not (fixed(q) and q == 0):
                            wait(act, s_tab, q * 16 + 16 * NQ * 3)
                        for t in range(nt):
                            last = fn(Z[:, QW + t * D:QW + (t + 1) * D], at(X, q * QW + t * D, D), ACT.Copy,
                                      scale=at(ROUT, q * QT + t))
                        last.then_inc(s_fin, 1)

            for k in range(PASSES):
                if k == 5:
                    expert_scalar(act, S, normalise)
                    act.wait_ge(s_rec, 32)
                for h in range(2):
                    stage_gather(k, 0, h, True)
                with act.Fori(1, NR) as i:
                    for h in range(2):
                        stage_gather(k, i, h, False)
                act.wait_ge(s_w, w_count(k))
                if k == 3:
                    act.wait_ge(s_deg, 2)
                copy_transposes(k, 0, QT)
                for q, nt, nxt in groups(act, S, {0: QT, 3: 1}.get(k, 0)):
                    finish(k, q, nt, nxt)

        @block.vector
        def _(dve):
            V = Steps(dve, s_dve)
            v = nc.vector
            v.memset(Hb[:, 0:2 * EW].bitcast(i32), -1)
            v.memset(WE, 0.0)
            v.memset(X[:, (NT - 1) * D:NT * D], 0.0).then_inc(s_clean, 1)
            v.memset(ACC[:, :], 0.0)
            V.link(v.memset(REC[:, :], 0.0))
            v.memset(RECV[:, :, 1], -1.0).then_inc(s_clean, 1)
            v.memset(ring[:, :], 0.0)
            V.link(v.memset(RK, 0.0))
            dve.wait_ge(s_const, 2)
            dve.wait_ge(s_in, 48)

            for src, hi, lo in ((DST, HI, LO), (SRC, SHI, SLO)):
                V.link(v.tensor_scalar(TMI, src, 7, None, ALU.arith_shift_right))
                V.link(v.tensor_copy(hi, TMI))
                V.link(v.tensor_scalar(TMI, src, P - 1, None, ALU.bitwise_and))
                V.link(v.tensor_copy(lo, TMI))

            def sort(b, hi):
                if b:
                    V.link(v.memset(RK, 0.0))
                for h in V.loop(0, NT, 4):
                    V.link(v.tensor_scalar(OH, hi, at(iota, h), None, ALU.is_equal))
                    V.link(v.tensor_tensor_scan(CUM, OH, OH, 0.0, ALU.add, ALU.max))
                    v.tensor_copy(at(CNT, h), CUM[:, EW - 1:EW])
                    V.link(v.tensor_tensor(TMP, OH, CUM, ALU.mult))
                    V.link(v.tensor_tensor(RK, RK, TMP, ALU.add))
                v.memset(col[:, 0:1], 0.0).then_inc(s_cnt, 1)

                dve.wait_ge(s_psort, 3 * b + 1)
                V.link(v.tensor_scalar(coli[0:NT, 0:1], bank(0, 1)[0:NT, :], float(P - 1), None, ALU.add))
                V.link(v.tensor_scalar(coli[0:NT, 1:2], coli[0:NT, 0:1], 7, None, ALU.arith_shift_right))
                V.link(v.tensor_copy(col[0:NT, 1:2], coli[0:NT, 1:2]))
                v.tensor_scalar(nchb[0:NT, :], ones[0:NT, :], col[0:NT, 1:2], float(P), ALU.mult, ALU.mult).then_inc(s_cnt, 1)
                dve.wait_ge(s_psort, 3 * b + 2)
                v.tensor_copy(OFF[:, 0:NT], bank(1, NT))
                V.link(v.tensor_copy(col[0:NT, 2:3], bank(2, 1)[0:NT, :]))
                v.tensor_scalar(CMAP[0:NT, :], IOTC[0:NT, :], col[0:NT, 2:3], None, ALU.is_ge).then_inc(s_cnt, 1)
                dve.wait_ge(s_psort, 3 * b + 3)
                for c in range(2):
                    w = NCH // 2
                    V.link(v.tensor_scalar(TTS[b][0:1, c * w:(c + 1) * w], bank(3 + c, w)[0:1, :], float(NT - 1), float(D),
                                           ALU.min, ALU.mult))

                for h in V.loop(0, NT, 2):
                    V.link(v.tensor_scalar(OH, hi, at(iota, h), at(OFF, h), ALU.is_equal, ALU.mult))
                    V.link(v.tensor_tensor(RK, RK, OH, ALU.add))
                V.link(v.tensor_scalar(TMI, RK, -1.0, 0.0, ALU.add, ALU.max))
                V.link(v.tensor_scalar(TMJ, TMI, 7, None, ALU.arith_shift_right))
                V.link(v.tensor_copy(TMP, TMJ))
                V.link(v.tensor_scalar(TMJ, TMI, P - 1, None, ALU.bitwise_and))
                V.link(v.tensor_copy(OH, TMJ))
                V.link(v.scalar_tensor_tensor(RK, OH, float(NCH), TMP, ALU.mult, ALU.add))
                V.link(v.tensor_tensor(RK, RK, EDUMP, ALU.subtract))
                V.link(v.tensor_scalar(OH, hi, 0.0, None, ALU.is_ge))
                V.link(v.tensor_tensor(RK, RK, OH, ALU.mult))
                V.link(v.tensor_tensor(POS[b], RK, EDUMP, ALU.add))

            def records(b, other, lo):
                v.tensor_copy(RECE[:, :, 0], other)
                v.tensor_copy(RECE[:, :, 1], lo)
                v.tensor_copy(RECE[:, :, 2], WE).then_inc(s_pos, 1)

            sort(0, HI)
            records(0, SRC, LO)
            sort(1, SHI)

            def one_hot_half(b, i, h, hi, lo):
                n = i * 2 + 2 * ER * b + h
                if not (fixed(i) and i == 0 and b == 0):
                    dve.wait_ge(s_hist, n - 1)
                c = i * ROUND + h * HALF
                l3 = at(lo, c, HALF).unsqueeze(2).broadcast_to((P, HALF, P))
                h3 = at(hi, c, HALF).unsqueeze(2).broadcast_to((P, HALF, NT))
                v.tensor_tensor(OHL[h], iota[:, :].unsqueeze(1).broadcast_to((P, HALF, P)), l3, ALU.is_equal)
                v.tensor_tensor(OHH[h], iota[:, 0:NT].unsqueeze(1).broadcast_to((P, HALF, NT)), h3, ALU.is_equal).then_inc(s_oh, 1)

            for b, (hi, lo) in enumerate(((HI, LO), (SHI, SLO))):
                for h in range(2):
                    one_hot_half(b, 0, h, hi, lo)
                with dve.Fori(1, ER) as i:
                    for h in range(2):
                        one_hot_half(b, i, h, hi, lo)
            for j in range(ROUND):
                dve.wait_ge(s_slot[j], 16 * ER)
            records(1, DST, SLO)
            dve.wait_ge(s_hist, 4 * ER)
            v.tensor_scalar(RIN[:, :], bank(6, NT), 1.0, None, ALU.max)
            v.tensor_scalar(ROUT[:, :], bank(7, NT), 1.0, None, ALU.max).then_inc(s_deg, 1)
            dve.wait_ge(s_degq, 1)
            V.link(v.reciprocal(RIN[:, :], RIN[:, :]))
            v.reciprocal(ROUT[:, :], ROUT[:, :]).then_inc(s_deg, 1)
            dve.wait_ge(s_deg, 2)
            dve.wait_ge(s_rec, 16)

            def pick_half(k, i, h):
                for j in range(HALF):
                    c = i * ROUND + h * HALF + j
                    p = pick[:, (h * HALF + j) * P:(h * HALF + j + 1) * P]
                    lo = RECV[:, c, 1:2] if fixed(c) else REC[:, DS(c * 4 + 1, 1)]
                    we = RECV[:, c, 2:3] if fixed(c) else REC[:, DS(c * 4 + 2, 1)]
                    if k in (0, 5):
                        last = v.tensor_scalar(p, iota[:, :], lo, we, ALU.is_equal, ALU.mult)
                    else:
                        last = v.tensor_scalar(p, iota[:, :], lo, None, ALU.is_equal)
                last.then_inc(s_pick, 1)

            def add_half(k, i, h):
                n = i * 2 + 2 * NR * k + h
                dve.wait_ge(s_prod, n + 1)
                for j in range(HALF):
                    c = i * ROUND + h * HALF + j
                    tt = TTS[k == 5]
                    t = dve.value_load(tt[0:1, c:c + 1] if fixed(c) else tt[0:1, DS(c, 1)], min_val=0, max_val=(NT - 1) * D)
                    if not (fixed(n) and n + j == 0):
                        dve.wait_ge(s_acc, n * HALF + j)
                    slot = h * HALF + j
                    v.tensor_tensor(ACC[:, DS(t, D)], ACC[:, DS(t, D)], PS[:, slot * D:(slot + 1) * D], ALU.add).then_inc(s_acc, 1)

            def prepare(k, q, nt):
                if not (fixed(q) and q == 0):
                    dve.wait_ge(s_t, q + NQ * k)
                acc, x = part(ACC, q, nt), part(X, q, nt)
                if k == 0:
                    v.tensor_copy(Z[:, 0:nt * D], acc)
                    last = v.tensor_copy(Z[:, QW:QW + nt * D], x)
                elif k <= 3:
                    last = v.scalar_tensor_tensor(Z[:, 0:nt * D], x if k == 1 else part(Hb, q, nt), EPS1[:, :], acc, ALU.mult, ALU.add)
                elif k == 4:
                    for t in range(nt):
                        v.tensor_scalar(Z[:, t * D:(t + 1) * D], at(ACC, q * QW + t * D, D), at(RIN, q * QT + t), None, ALU.mult)
                    last = v.tensor_copy(Z[:, QW:QW + nt * D], x)
                else:
                    V.link(v.tensor_tensor(tiles(Z[:, QW:QW + nt * D], nt), tiles(acc, nt), vec(1, nt), ALU.mult))
                    last = v.tensor_tensor(Z[:, 0:nt * D], x, Z[:, QW:QW + nt * D], ALU.subtract)
                last.then_inc(s_z, 1)

            def statistics(key, q, nt, second=0):
                for t in range(nt):
                    last = v.bn_stats(ST[:, t * 6:(t + 1) * 6], U[:, t * D:(t + 1) * D])
                V.alone = True
                V.link(last)
                for t in range(nt):
                    last = v.bn_aggr(MV[:, t * 2:t * 2 + 2], ST[:, t * 6:(t + 1) * 6])
                V.link(last)
                mv = MV[:, 0:2 * nt].rearrange("p (t s) -> p t s", s=2)
                v.tensor_scalar(SM[:, 0:nt], mv[:, :, 1], LN_EPS, None, ALU.add).then_inc(s_var, 1)
                n = ln_count(key, q, second)
                dve.wait_ge(s_sd, n)
                V.link(v.reciprocal(SM[:, 8:8 + nt], SM[:, 4:4 + nt]))
                v.scalar_tensor_tensor(SM[:, 12:12 + nt], mv[:, :, 0], -1.0, SM[:, 8:8 + nt], ALU.mult, ALU.mult).then_inc(s_rs, 1)

            def consume(k, q, nt):
                dve.wait_ge(s_mm, q + NQ * k + 1)
                if k == 4:
                    dve.wait_ge(s_gate, q + 1)
                    v.tensor_copy(part(ACC, q, nt), U[:, 0:nt * D]).then_inc(s_u, 1)
                    dve.wait_ge(s_lg, q + 1)
                    v.tensor_copy(at(Hb, q * (QT * NE), nt * NE), bank(6, nt * NE)).then_inc(s_lgc, 1)
                    return
                if not (fixed(q) and q == 0):
                    dve.wait_ge(s_fin, q + NQ * k)
                if k == 0:
                    dve.wait_ge(s_nrm, q + 1)
                    V.link(v.tensor_scalar(SM[:, 20:20 + nt], SM[:, 20:20 + nt], 1e-12, None, ALU.max))
                    V.link(v.reciprocal(SM[:, 20:20 + nt], SM[:, 20:20 + nt]))
                    for t in range(nt):
                        last = v.scalar_tensor_tensor(U[:, t * D:(t + 1) * D], bank(4 + t // 2, D, t % 2 * D), SM[:, 20 + t:21 + t],
                                                      at(X, q * QW + t * D, D), ALU.mult, ALU.add)
                else:
                    last = v.tensor_tensor(U[:, 0:nt * D], PS[:, 2048:2048 + nt * D], part(Hb if k in (2, 3) else X, q, nt), ALU.add)
                last.then_inc(s_u, 1)
                dve.wait_ge(s_u, q + NQ * k + 1)
                statistics(k, q, nt)
                if k in (1, 2, 3):
                    dve.wait_ge(s_ln, q + NQ * (k - 1) + 1)
                    u = tiles(U[:, 0:nt * D], nt)
                    V.link(v.tensor_tensor(u, u, vec(1, nt), ALU.mult))
                    last = v.tensor_tensor(u, u, vec(2, nt), ALU.add)
                    if k < 3:
                        last.then_inc(s_aff, 1)
                    else:
                        V.link(last)
                        V.link(v.scalar_tensor_tensor(U[:, 0:nt * D], U[:, 0:nt * D], 0.0, part(X, q, nt), ALU.max, ALU.add))
                        statistics(3, q, nt, 1)

            PER = {0: 5, 1: 4, 2: 4, 3: 9, 4: 0, 5: 4}
            for k in range(PASSES):
                if k == 5:
                    expert_vector(dve, V, statistics)
                    dve.wait_ge(s_rec, 32)
                if k:
                    dve.wait_ge(s_fin, NQ * k)
                    V.link(v.memset(ACC[:, :], 0.0))
                pick_half(k, 0, 0)
                pick_half(k, 0, 1)
                add_half(k, 0, 0)
                with dve.Fori(1, NR) as i:
                    pick_half(k, i, 0)
                    add_half(k, i - 1, 1)
                    pick_half(k, i, 1)
                    add_half(k, i, 0)
                add_half(k, NR - 1, 1)
                dve.wait_ge(s_acc, NCH * (k + 1))
                dve.wait_ge(s_w, w_count(k))
                if k == 0:
                    dve.wait_ge(s_x, 32)
                if k in (1, 2, 3):
                    V.link(v.tensor_scalar(EPS1[:, :], EPS1[:, :], 1.0, None, ALU.add))
                if k == 5:
                    V.link(v.tensor_scalar(VEC[:, D:2 * D], VEC[:, D:2 * D], 1.0, None, ALU.add))
                prepare(k, 0, QT)
                for q, nt, nxt in groups(dve, V, PER[k]):
                    if nxt:
                        prepare(k, q + 1, nxt)
                    consume(k, q, nt)


_INS = [
    "x", "src", "dst", "edge_weight", "L0_gnn_w_self", "L0_gnn_w_neigh", "L1_gnn_W1", "L1_gnn_b1",
    "L1_gnn_W2", "L1_gnn_b2", "L1_gnn_eps", "L1_gnn_gamma", "L1_gnn_beta", "L2_gnn_W_gc", "L2_gnn_b_gc",
    "L2_gnn_W_res", "L2_gnn_b_res", "L2_gnn_Wg", "L2_gnn_bg", "L2_gnn_w1", "L2_gnn_b1", "L2_gnn_w2",
    "L2_gnn_b2", "L2_gnn_gamma", "L2_gnn_beta", "L3_gnn_weight", "L3_gnn_learnable_diag", "L3_gnn_bias",
]


def kernel(**inputs):
    import numpy as np
    import concourse.bacc as bacc
    from concourse.bass_utils import run_bass_kernel_spmd as run

    nc = bacc.Bacc("TRN2", target_bir_lowering=False, num_devices=1)
    arrays, aps = {}, {}
    for name in _INS:
        v = np.ascontiguousarray(inputs[name])
        arrays[f"in_{name}"] = v
        aps[name] = nc.dram_tensor(f"in_{name}", v.shape, mybir.dt.from_np(v.dtype), kind="ExternalInput").ap()
    out = nc.dram_tensor("out", (N, D), mybir.dt.float32, kind="ExternalOutput").ap()
    gnn(nc, aps, out)
    return run(nc, [arrays], core_ids=[0]).results[0]["out"]
```

```python
import concourse.bass as bass
from concourse import mybir
from contextlib import ExitStack

N = 6250
E = 106250
D = 256
P = 128
NT = -(-N // P)
LAST = N - (NT - 1) * P
NPAD = NT * P
QT = 4
NQ = -(-NT // QT)
QW = QT * D
EP = 125
EC = E // EP
HALF = 8
ROUND = 2 * HALF
EW = -(-EC // ROUND) * ROUND
ER = EW // ROUND
NCH = -(-((E + (P - 1) * NT) // P) // ROUND) * ROUND
NR = NCH // ROUND
REC_ROWS = NCH * P + P * EW
PASSES = 6
LOTS = [8, 46]
NE = 64
HID = 512
CAP = 1024
MB = 4
MC = -(-((2 * N + (P - 1) * NE) // P) // MB) * MB
MG = MC // MB
XS_ROWS = MC * P + 2 * NT * P
LN_EPS = 1e-5
BIG = 3.0e38


def gnn(nc, a, out):
    f32, i32, u32, bf16 = mybir.dt.float32, mybir.dt.int32, mybir.dt.uint32, mybir.dt.bfloat16
    ALU, ACT, AX = mybir.AluOpType, mybir.ActivationFunctionType, mybir.AxisListType
    DS = bass.DynSlice
    ctx = ExitStack()
    with ctx:
        def sb(name, cols, dt=f32, rows=P):
            return ctx.enter_context(nc.sbuf_tensor(name, [rows, cols], dt))

        def sem(name):
            return ctx.enter_context(nc.semaphore(name))

        def dram(name, shape, dt=f32):
            return nc.dram_tensor(name, shape, dt, kind="Internal").ap()

        recs = [dram(f"edge_records{b}", (REC_ROWS, 4)) for b in range(2)]
        pend = dram("edges_by_source", (P, EW * 4))
        tables = [a["x"]] + [dram(f"table{k}", (NPAD, D)) for k in range(1, PASSES)]
        xs_dram = dram("expert_inputs", (XS_ROWS, D))
        ys_dram = dram("expert_outputs", (MC * P, D))

        X = sb("X", NT * D)
        Hb = sb("Hb", NT * D)
        ACC = sb("ACC", NT * D)
        ring = sb("ring", ROUND * D)
        pick = sb("pick", ROUND * P)
        REC = sb("REC", NCH * 4)
        TTS = [sb(f"TT{b}", NCH, i32) for b in range(2)]
        WA = sb("WA", 2 * 2 * D)
        VEC = sb("VEC", 4 * D)
        B1C = sb("B1C", 2)
        EPS1 = sb("EPS1", 1)
        STG = sb("STG", ROUND * 4)
        IDX = sb("IDX", ROUND, u32)
        LOT = sb("LOT", 2 * ROUND * 4)
        iota = sb("iota", P)
        ident = sb("ident", P)
        tri = sb("tri", P)
        trii = sb("trii", P)
        ones = sb("ones", P)
        onesl = sb("onesl", P)
        RIN = sb("RIN", NT)
        ROUT = sb("ROUT", NT)
        CNT = sb("CNT", NE)
        OFF = sb("OFF", NE)
        col = sb("col", 8)
        coli = sb("coli", 2, i32)
        nchb = sb("nchb", P)
        ST = sb("ST", QT * 6)
        MV = sb("MV", QT * 2)
        SM = sb("SM", QT * 6)
        WG = sb("WG", 2 * NE)
        BG = sb("BG", NE)
        IM = sb("IM", NE)
        iotam = sb("iotam", MC)
        DUMP = sb("DUMP", 2 * NT)
        G12 = sb("G12", 2 * NT)
        ET = TTS[0][:, 0:MC]
        PS = ctx.enter_context(nc.psum_tensor("PS", [P, 8 * 512], f32))

        def bank(b, w=512, off=0):
            return PS[:, b * 512 + off:b * 512 + off + w]

        Z = ring[:, 0:2 * QW]
        ZT = ring[:, 2 * QW:4 * QW]
        M1T = pick[:, 0:QW]
        U = pick[:, QW:2 * QW]

        s_const = sem("constants_made")
        s_clean = sem("buffers_cleared")
        s_in = sem("edges_loaded")
        s_x = sem("x_loaded")
        s_w = sem("weights_loaded")
        s_wt = sem("weights_transposed")
        s_wtc = sem("weight_transposes_copied")
        s_init = sem("records_initialised")
        s_zero = sem("expert_inputs_zeroed")
        s_dve = sem("vector_steps")
        s_act = sem("scalar_steps")
        s_cnt = sem("tile_counts_made")
        s_psort = sem("sort_products_done")
        s_pos = sem("edge_positions_made")
        s_stage = sem("indices_staged")
        s_slot = [sem(f"slot{j}_moved") for j in range(ROUND)]
        s_pend = sem("records_by_source_kept")
        s_lot = [sem(f"record_lot{j}_loaded") for j in range(2)]
        s_win = [sem(f"record_lot{j}_scattered") for j in range(2)]
        s_rec = sem("records_loaded")
        s_oh = sem("one_hots_built")
        s_hist = sem("histogram_halves_done")
        s_deg = sem("degrees_made")
        s_degq = sem("degree_roots_made")
        s_pick = sem("pick_halves_built")
        s_prod = sem("product_halves_done")
        s_acc = sem("chunks_accumulated")
        s_vec = sem("vectors_prepared")
        s_prep = sem("operand_steps")
        s_z = sem("operands_ready")
        s_t = sem("operands_transposed")
        s_zt = sem("transposes_copied")
        s_mm1 = sem("first_products_done")
        s_m1 = sem("hidden_ready")
        s_mm = sem("layer_products_done")
        s_nrm = sem("norms_made")
        s_u = sem("products_consumed")
        s_var = sem("variances_ready")
        s_sd = sem("deviations_ready")
        s_rs = sem("scales_ready")
        s_ln = sem("rows_normalised")
        s_fin = sem("outputs_final")
        s_tab = sem("tables_stored")
        s_gate = sem("gate_inputs_copied")
        s_t2 = sem("gate_inputs_transposed")
        s_t2c = sem("gate_transposes_copied")
        s_lg = sem("logits_done")
        s_lgc = sem("logits_copied")
        s_gap = sem("gate_gaps_made")
        s_exp = sem("gate_exponentials_made")
        s_route = sem("route_steps_made")
        s_rk = sem("rank_products_done")
        s_rkc = sem("ranks_copied")
        s_xsc = sem("expert_inputs_scattered")
        s_wl = [sem(f"expert_weights{j}_loaded") for j in range(MB)]
        s_xl = [sem(f"expert_rows{j}_loaded") for j in range(MB)]
        s_et = sem("expert_inputs_transposed")
        s_xt = sem("expert_transposes_copied")
        s_h = sem("expert_hidden_done")
        s_g = sem("expert_gelu_done")
        s_y = sem("expert_products_done")
        s_yc = sem("expert_outputs_copied")
        s_ys = [sem(f"expert_outputs{j}_stored") for j in range(MB)]
        s_b1 = sem("expert_biases_loaded")
        s_b1t = sem("expert_biases_transposed")
        s_b1c = sem("expert_biases_copied")
        s_comb = [sem(f"combine_slot{j}_gathered") for j in range(8)]
        s_cu = sem("combined")
        s_bnv = sem("batch_vectors_loaded")
        s_cen = sem("rows_centred")
        s_csq = sem("centred_rows_squared")
        s_bnm = sem("batch_sums_done")
        s_bns = sem("batch_root_made")
        s_out = sem("output_stored")
        s_idle = sem("waits_that_stood_alone")

        def hcols(n, dt=f32):
            v = Hb[:, n * EW:(n + 1) * EW]
            return v.bitcast(dt) if dt != f32 else v

        SRC, DST, TMI = hcols(0, i32), hcols(1, i32), hcols(2, i32)
        WE, HI, LO, SHI, SLO, RK, TMP, OH, CUM = (hcols(n) for n in range(3, 12))
        TMJ = hcols(13, i32)
        POS = [hcols(12, u32), hcols(13, u32)]
        EDUMP = pick[:, 0:EW]
        IOTC = pick[:, EW:EW + NCH]
        RECE = [v.rearrange("p (c f) -> p c f", f=4) for v in (ring[:, 0:EW * 4], Hb[:, 8 * EW:12 * EW])]
        RECV = REC[:, :].rearrange("p (c f) -> p c f", f=4)
        OHL = [pick[:, h * 512:(h + 1) * 512].bitcast(bf16).rearrange("p (c m) -> p c m", c=HALF) for h in range(2)]
        OHH = [pick[:, 1024 + h * 256:1024 + h * 256 + HALF * NT // 2].bitcast(bf16).rearrange("p (c m) -> p c m", c=HALF)
               for h in range(2)]

        GW = NT * NE
        LOG, OH1, OH2, MM = (Hb[:, n * GW:(n + 1) * GW] for n in range(4))
        W1B = [Hb[:, j * 2048:j * 2048 + 1024] for j in range(MB)]
        W2B = [Hb[:, j * 2048 + 1024:j * 2048 + 2048] for j in range(MB)]
        HT = [Hb[:, 8192 + j * 512:8704 + j * 512] for j in range(MB)]
        B1T0 = 10240
        B1T = Hb[:, B1T0:B1T0 + 256]
        B2B = [Hb[:, 10496 + j * 256:10752 + j * 256] for j in range(MB)]
        XSB, XTB, YB = ([ring[:, (m * MB + j) * 256:(m * MB + j + 1) * 256] for j in range(MB)] for m in range(3))
        B1R = pick[0:NE, 0:HID]
        RNK = ring[:, 0:GW]
        RT = ring[:, GW:GW + 4 * NT]
        SI = ring[:, GW + 4 * NT:GW + 6 * NT].bitcast(u32)
        GI = ring[:, GW + 6 * NT:GW + 8 * NT].bitcast(u32)
        RB = 448

        block = ctx.enter_context(nc.Block())

        def wait(e, s, value):
            e.wait_ge(s, value)
            if not isinstance(value, int):
                e.sem_inc(s_idle, 1)

        class Steps:

            def __init__(self, e, s):
                self.e, self.s, self.at, self.n, self.alone = e, s, 0, 0, False

            def link(self, ins):
                ins.then_inc(self.s, 1)
                self.at = self.at + 1
                self.n += 1
                wait(self.e, self.s, self.at) if self.alone else self.e.wait_ge(self.s, self.at)
                self.alone = False

            def loop(self, start, end, per):
                base, n = self.at, self.n
                with self.e.Fori(start, end) as i:
                    self.at = (i - start) * per + base if per else base
                    yield i
                assert self.n - n == per, (self.n - n, per)
                self.at = base + (end - start) * per

        def groups(e, steps=None, per=0):
            last = NT - (NQ - 1) * QT
            yield 0, QT, QT
            if steps is None:
                with e.Fori(1, NQ - 2) as q:
                    yield q, QT, QT
            else:
                yield from ((q, QT, QT) for q in steps.loop(1, NQ - 2, per))
            yield NQ - 2, QT, last
            yield NQ - 1, last, 0

        def chunks(e):
            for j in range(MB):
                yield 0, j, j
            with e.Fori(1, MG - 1) as g:
                for j in range(MB):
                    yield g, j, g * MB + j
            for j in range(MB):
                yield MG - 1, j, (MG - 1) * MB + j

        def fixed(v):
            return isinstance(v, int)

        def at(buf, c, w=1):
            return buf[:, c:c + w] if fixed(c) else buf[:, DS(c, w)]

        def load_values(e, row, c, w, most):
            return nc.values_load_multi_w_load_instructions(
                row[0:1, c:c + w] if fixed(c) else row[0:1, DS(c, w)], engines=(e.engine,), min_val=0, max_val=most,
                skip_runtime_bounds_check_because="the row's numbers are clamped where it is made")[1]

        def part(buf, q, nt):
            return at(buf, q * QW, nt * D)

        def tiles(v, nt):
            return v.rearrange("p (t d) -> p t d", t=nt)

        def vec(n, nt):
            return VEC[:, n * D:(n + 1) * D].unsqueeze(1).broadcast_to((P, nt, D))

        def wmat(m, k):
            return WA[:, (m * 2 + k) * D:(m * 2 + k + 1) * D]

        def ln_count(k, q, second=0):
            base = {0: 0, 1: NQ, 2: 2 * NQ, 3: 3 * NQ, "bn": 5 * NQ, 5: 6 * NQ}[k]
            return base + (2 * q + second if k == 3 else q) + 1

        W_DMAS = [2, 7, 7, 7, 6, 3]

        def w_count(k):
            return 16 * sum(W_DMAS[:k + 1])

        def rounds(k):
            return ER + NR * k

        def operands(k):
            return 2 if k in (0, 4) else 1

        w1_rows = a["L2_gnn_w1"].rearrange("e d h -> (e d) h")
        w2_rows = a["L2_gnn_w2"].rearrange("e h d -> (e h) d")
        SQ = VEC[:, 0:D]
        CMAP = Hb[:, 9 * EW:9 * EW + NCH]

        def expert_moves(pool, lot_rounds):
            lot_rounds(0)
            pool.wait_ge(s_zero, 64)
            pool.wait_ge(s_route, 3)
            for n in range(2 * NT):
                t, s = n // 2, n % 2
                pool.indirect_dma_start(xs_dram, bass.IndirectOffsetOnAxis(ap=SI[:, s * NT + t:s * NT + t + 1], axis=0),
                                        ACC[:, t * D:(t + 1) * D], None).then_inc(s_xsc, 16)
            lot_rounds(1)
            for j in range(MB):
                pool.wait_ge(s_ys[j], 16 * MG)
            for n in range(2 * NT):
                t, s = n // 2, n % 2
                if n >= 8:
                    pool.wait_ge(s_cu, n - 7)
                pool.indirect_dma_start(ring[:, n % 8 * D:(n % 8 + 1) * D], None, ys_dram,
                                        bass.IndirectOffsetOnAxis(ap=GI[:, s * NT + t:s * NT + t + 1], axis=0)).then_inc(s_comb[n % 8], 16)

        def expert_products(pe):
            mm = nc.tensor.matmul
            pe.wait_ge(s_route, 1)
            for b in range(GW // RB):
                mm(bank(b, RB), tri[:, :], MM[:, b * RB:(b + 1) * RB], start=True, stop=False)
                mm(bank(b, RB), ones[:, :], LOG[:, b * RB:(b + 1) * RB], start=False, stop=True)
            mm(bank(7, 1)[0:NE, :], CNT[:, :], ones[:, 0:1], start=True, stop=True).then_inc(s_rk, 1)
            pe.wait_ge(s_route, 2)
            mm(bank(7, NE, 64), nchb[0:NE, :], tri[0:NE, 0:NE], start=True, stop=True)
            mm(bank(7, 1, 192)[0:NE, :], trii[0:NE, 0:NE], col[0:NE, 1:2], start=True, stop=True).then_inc(s_rk, 1)
            pe.wait_ge(s_gap, 2)
            mm(bank(7, MC, 256)[0:1, :], ones[0:NE, 0:1], pick[0:NE, 0:MC], start=True, stop=True).then_inc(s_rk, 1)
            pe.wait_ge(s_route, 3)
            pe.wait_ge(s_b1, 16)
            for m in range(4):
                last = nc.tensor.transpose(bank(2, NE, m * NE), B1R[:, m * P:(m + 1) * P], ident[0:NE, 0:NE])
            last.then_inc(s_b1t, 1)

            def transpose(g, j, c):
                pe.wait_ge(s_xl[j], g * 16 + 16)
                if not (fixed(c) and c == 0):
                    pe.wait_ge(s_xt, c)
                for b in range(2):
                    last = nc.tensor.transpose(bank(0, P, b * P), XSB[j][:, b * P:(b + 1) * P], ident[:, :])
                last.then_inc(s_et, 1)

            def hidden(g, j, c):
                pe.wait_ge(s_xt, c + 1)
                pe.wait_ge(s_wl[j], g * 48 + 48)
                if not (fixed(c) and c < MB):
                    pe.wait_ge(s_g, c - (MB - 1))
                for m in range(4):
                    for b in range(2):
                        last = mm(bank(3 + j, P, m * P), W1B[j][:, b * HID + m * P:b * HID + (m + 1) * P],
                                  XTB[j][:, b * P:(b + 1) * P], start=b == 0, stop=b == 1)
                last.then_inc(s_h, 1)

            def output(j, c):
                pe.wait_ge(s_g, c + 1)
                if not (fixed(c) and c == 0):
                    pe.wait_ge(s_yc, c)
                for m in range(4):
                    last = mm(bank(1, D), HT[j][:, m * P:(m + 1) * P], W2B[j][:, m * D:(m + 1) * D], start=m == 0, stop=m == 3)
                last.then_inc(s_y, 1)

            transpose(0, 0, 0)
            for g, j, c in chunks(pe):
                if not (fixed(c) and c == MC - 1):
                    transpose(g + (j == MB - 1), (j + 1) % MB, c + 1)
                hidden(g, j, c)
                if not (fixed(c) and c == 0):
                    output((j + MB - 1) % MB, c - 1)
            output((MC - 1) % MB, MC - 1)

            pe.wait_ge(s_cu, 2 * NT)
            mm(bank(0, D), ones[:, :], ACC[:, 0:D], start=True, stop=False)
            with pe.Fori(1, NT - 1) as t:
                mm(bank(0, D), ones[:, :], ACC[:, DS(t * D, D)], start=False, stop=False, skip_group_check=True)
            mm(bank(0, D), onesl[:, :], ACC[:, (NT - 1) * D:NT * D], start=False, stop=True).then_inc(s_bnm, 1)
            for q, nt, nxt in groups(pe):
                pe.wait_ge(s_csq, q + 1)
                for t in range(nt):
                    last = mm(bank(1, D), ones[:, :] if nxt else onesl[:, :], Z[:, t * D:(t + 1) * D],
                              start=fixed(q) and q == 0 and t == 0, stop=not nxt, skip_group_check=True)
                last.then_inc(s_bnm, 1)

        def expert_scalar(act, S, normalise):
            fn = nc.scalar.activation
            act.wait_ge(s_gap, 1)
            fn(RT[:, 0:NT], RT[:, 0:NT], ACT.Exp).then_inc(s_exp, 1)
            act.wait_ge(s_rk, 1)
            for b in range(GW // RB):
                last = fn(RNK[:, b * RB:(b + 1) * RB], bank(b, RB), ACT.Copy)
            last.then_inc(s_rkc, 1)
            act.wait_ge(s_b1t, 1)
            fn(B1T, bank(2, 4 * NE), ACT.Copy).then_inc(s_b1c, 1)
            act.wait_ge(s_b1c, 1)
            for g, j, c in chunks(act):
                if j == 0:
                    experts = load_values(act, ET, c, MB, NE - 1)
                wait(act, s_h, c + 1)
                if not (fixed(c) and c < MB):
                    wait(act, s_y, c - (MB - 1))
                e = experts[j]
                for m in range(4):
                    last = fn(HT[j][:, m * P:(m + 1) * P], bank(3 + j, P, m * P), ACT.Gelu, bias=Hb[:, DS(e + (B1T0 + m * NE), 1)])
                last.then_inc(s_g, 1)
            for q, nt, _ in groups(act):
                wait(act, s_cen, q + 1)
                if not (fixed(q) and q == 0):
                    wait(act, s_bnm, q + 1)
                fn(Z[:, 0:nt * D], part(ACC, q, nt), ACT.Square).then_inc(s_csq, 1)
            act.wait_ge(s_bns, 1)
            fn(VEC[:, 2 * D:3 * D], VEC[:, 2 * D:3 * D], ACT.Sqrt).then_inc(s_bns, 1)
            for q, nt, _ in groups(act):
                normalise("bn", q, nt, part(X, q, nt)).then_inc(s_fin, 1)

        def expert_vector(dve, V, statistics):
            v = nc.vector
            dve.wait_ge(s_lgc, NQ)
            g3 = lambda b: b.rearrange("p (t e) -> p t e", e=NE)
            over_e = lambda c: c.unsqueeze(2).broadcast_to((P, NT, NE))
            over_t = lambda c: c.unsqueeze(1).broadcast_to((P, NT, NE))
            best, second, sel = RT[:, NT:2 * NT], RT[:, 2 * NT:3 * NT], RT[:, 3 * NT:4 * NT]

            def top(value, oh):
                V.link(v.tensor_reduce(value, g3(LOG), AX.X, ALU.max))
                V.link(v.tensor_tensor(g3(MM), g3(LOG), over_e(value), ALU.is_equal))
                V.link(v.tensor_tensor(g3(MM), g3(MM), over_t(IM[:, :]), ALU.mult))
                V.link(v.tensor_reduce(sel, g3(MM), AX.X, ALU.min))
                V.link(v.tensor_tensor(g3(oh), over_t(IM[:, :]), over_e(sel), ALU.is_equal))

            top(best, OH1)
            V.link(v.scalar_tensor_tensor(LOG, OH1, -BIG, LOG, ALU.mult, ALU.add))
            top(second, OH2)
            v.tensor_tensor(RT[:, 0:NT], second, best, ALU.subtract).then_inc(s_gap, 1)
            dve.wait_ge(s_exp, 1)
            V.link(v.tensor_scalar(G12[:, 0:NT], RT[:, 0:NT], 1.0, None, ALU.add))
            V.link(v.reciprocal(G12[:, 0:NT], G12[:, 0:NT]))
            V.link(v.tensor_tensor(G12[:, NT:2 * NT], G12[:, 0:NT], RT[:, 0:NT], ALU.mult))
            V.link(v.tensor_tensor(MM, OH1, OH2, ALU.add))
            v.tensor_scalar(MM[:, (NT - 1) * NE:], MM[:, (NT - 1) * NE:], onesl[:, 0:1], None, ALU.mult)
            V.link(v.memset(LOG[:, 0:NE], 0.0))
            for t in V.loop(1, NT, 1):
                V.link(v.tensor_tensor(Hb[:, DS(t * NE, NE)], Hb[:, DS(t * NE - NE, NE)], Hb[:, DS(t * NE + (3 * GW - NE), NE)], ALU.add))
            v.tensor_tensor(CNT[:, :], LOG[:, (NT - 1) * NE:], MM[:, (NT - 1) * NE:], ALU.add).then_inc(s_route, 1)
            dve.wait_ge(s_rk, 1)
            V.link(v.tensor_scalar(coli[0:NE, 0:1], bank(7, 1)[0:NE, :], float(CAP), float(P - 1), ALU.min, ALU.add))
            V.link(v.tensor_scalar(coli[0:NE, 1:2], coli[0:NE, 0:1], 7, None, ALU.arith_shift_right))
            V.link(v.tensor_copy(col[0:NE, 1:2], coli[0:NE, 1:2]))
            v.tensor_scalar(nchb[0:NE, :], ones[0:NE, :], col[0:NE, 1:2], float(P), ALU.mult, ALU.mult).then_inc(s_route, 1)
            dve.wait_ge(s_rk, 2)
            v.tensor_copy(OFF[:, :], bank(7, NE, 64))
            V.link(v.tensor_copy(col[0:NE, 2:3], bank(7, 1, 192)[0:NE, :]))
            v.tensor_scalar(pick[0:NE, 0:MC], iotam[0:NE, :], col[0:NE, 2:3], None, ALU.is_ge).then_inc(s_gap, 1)
            dve.wait_ge(s_rk, 3)
            V.link(v.tensor_scalar(ET[0:1, :], bank(7, MC, 256)[0:1, :], float(NE - 1), None, ALU.min))
            dve.wait_ge(s_rkc, 1)
            rank, ok = best, second
            for s, oh in enumerate((OH1, OH2)):
                c = slice(s * NT, (s + 1) * NT)
                V.link(v.tensor_tensor(LOG, oh, RNK, ALU.mult))
                V.link(v.tensor_reduce(rank, g3(LOG), AX.X, ALU.add))
                V.link(v.tensor_scalar(ok, rank, float(CAP), None, ALU.is_lt))
                V.link(v.tensor_scalar(ok[:, NT - 1:NT], ok[:, NT - 1:NT], onesl[:, 0:1], None, ALU.mult))
                V.link(v.tensor_tensor(g3(LOG), g3(oh), over_t(OFF[:, :]), ALU.mult))
                V.link(v.tensor_reduce(sel, g3(LOG), AX.X, ALU.add))
                V.link(v.tensor_tensor(sel, sel, rank, ALU.add))
                v.tensor_tensor(G12[:, c], G12[:, c], ok, ALU.mult)
                v.tensor_tensor(GI[:, c], sel, ok, ALU.mult)
                V.link(v.tensor_tensor(sel, sel, DUMP[:, c], ALU.subtract))
                V.link(v.tensor_tensor(sel, sel, ok, ALU.mult))
                last = v.tensor_tensor(SI[:, c], sel, DUMP[:, c], ALU.add)
                if s == 0:
                    V.link(last)
            last.then_inc(s_route, 1)

            def copy_in(g, j, c):
                dve.wait_ge(s_et, c + 1)
                if not (fixed(c) and c < MB):
                    dve.wait_ge(s_h, c - (MB - 1))
                v.tensor_copy(XTB[j], bank(0, D)).then_inc(s_xt, 1)

            dve.wait_ge(s_b1c, 1)
            copy_in(0, 0, 0)
            for g, j, c in chunks(dve):
                if not (fixed(c) and c == MC - 1):
                    copy_in(g + (j == MB - 1), (j + 1) % MB, c + 1)
                dve.wait_ge(s_y, c + 1)
                if not (fixed(g) and g == 0):
                    dve.wait_ge(s_ys[j], g * 16)
                v.tensor_tensor(YB[j], bank(1, D), B2B[j], ALU.add).then_inc(s_yc, 1)
            for n in range(2 * NT):
                t, s = n // 2, n % 2
                dve.wait_ge(s_comb[n % 8], 16 * (n // 8 + 1))
                if n:
                    dve.wait_ge(s_cu, n)
                acc = ACC[:, t * D:(t + 1) * D]
                v.scalar_tensor_tensor(acc, ring[:, n % 8 * D:(n % 8 + 1) * D], G12[:, s * NT + t:s * NT + t + 1], acc,
                                       ALU.mult, ALU.add).then_inc(s_cu, 1)
            dve.wait_ge(s_bnm, 1)
            V.link(v.tensor_scalar(VEC[:, 3 * D:4 * D], bank(0, D), 1.0 / N, None, ALU.mult))
            for q, nt, _ in groups(dve):
                acc = tiles(part(ACC, q, nt), nt)
                v.tensor_tensor(acc, acc, vec(3, nt), ALU.subtract).then_inc(s_cen, 1)
            dve.wait_ge(s_bnm, NQ + 1)
            dve.wait_ge(s_bnv, 32)
            v.tensor_scalar(VEC[:, 2 * D:3 * D], bank(1, D), 1.0 / N, LN_EPS, ALU.mult, ALU.add).then_inc(s_bns, 1)
            dve.wait_ge(s_bns, 2)
            V.link(v.reciprocal(VEC[:, 2 * D:3 * D], VEC[:, 2 * D:3 * D]))
            V.link(v.tensor_tensor(VEC[:, 2 * D:3 * D], VEC[:, 2 * D:3 * D], VEC[:, 0:D], ALU.mult))
            dve.wait_ge(s_cen, NQ)
            for q, nt, _ in groups(dve, V, 6):
                if not (fixed(q) and q == 0):
                    dve.wait_ge(s_fin, q + NQ * 4)
                u = tiles(U[:, 0:nt * D], nt)
                V.link(v.tensor_tensor(u, tiles(part(ACC, q, nt), nt), vec(2, nt), ALU.mult))
                V.link(v.tensor_tensor(u, u, vec(1, nt), ALU.add))
                V.link(v.tensor_tensor(U[:, 0:nt * D], U[:, 0:nt * D], part(X, q, nt), ALU.add))
                statistics("bn", q, nt)

        @block.sync
        def _(sp):
            sp.wait_ge(s_clean, 1)
            for dst, name in ((SRC, "src"), (DST, "dst"), (WE, "edge_weight")):
                sp.dma_start(dst[0:EP, 0:EC], a[name].rearrange("(p c) -> p c", c=EC)).then_inc(s_in, 16)
            sp.dma_start(tiles(X[:, 0:(NT - 1) * D], NT - 1),
                         a["x"][0:(NT - 1) * P, :].rearrange("(t p) d -> p t d", p=P)).then_inc(s_x, 16)
            sp.dma_start(X[0:LAST, (NT - 1) * D:NT * D], a["x"][(NT - 1) * P:N, :]).then_inc(s_x, 16)

            def weights(k):
                def mat(slot, src):
                    sp.dma_start(WA[:, slot * 2 * D:(slot + 1) * 2 * D].rearrange("p (k n) -> p k n", k=2),
                                 src.rearrange("(k p) n -> p k n", p=P)).then_inc(s_w, 16)

                def row(slot, src):
                    sp.dma_start(VEC[:, slot * D:(slot + 1) * D], src.partition_broadcast(P)).then_inc(s_w, 16)

                if k == 0:
                    mat(0, a["L0_gnn_w_neigh"])
                    mat(1, a["L0_gnn_w_self"])
                elif k <= 3:
                    mat(0, a["L1_gnn_W1"][k - 1])
                    mat(1, a["L1_gnn_W2"][k - 1])
                    row(0, a["L1_gnn_b2"][k - 1])
                    row(1, a["L1_gnn_gamma"][k - 1])
                    row(2, a["L1_gnn_beta"][k - 1])
                    sp.dma_start(B1C[:, :], a["L1_gnn_b1"][k - 1].rearrange("(k p) -> p k", p=P),
                                 allow_slow_non_contiguous=True).then_inc(s_w, 16)
                    sp.dma_start(EPS1[:, :], a["L1_gnn_eps"][k - 1:k].partition_broadcast(P)).then_inc(s_w, 16)
                elif k == 4:
                    mat(0, a["L2_gnn_W_gc"])
                    mat(1, a["L2_gnn_W_res"])
                    row(0, a["L2_gnn_b_gc"])
                    row(1, a["L2_gnn_b_res"])
                    sp.dma_start(WG[:, :].rearrange("p (k n) -> p k n", k=2),
                                 a["L2_gnn_Wg"].rearrange("(k p) n -> p k n", p=P)).then_inc(s_w, 16)
                    sp.dma_start(BG[:, :], a["L2_gnn_bg"].partition_broadcast(P)).then_inc(s_w, 16)
                else:
                    mat(0, a["L3_gnn_weight"])
                    row(0, a["L3_gnn_bias"])
                    row(1, a["L3_gnn_learnable_diag"])

            weights(0)
            sp.wait_ge(s_clean, 2)
            for rec in recs:
                sp.dma_start(rec[0:NCH * P, :].rearrange("(p c) f -> p (c f)", p=P), REC[:, :]).then_inc(s_init, 16)
            xz = xs_dram[0:MC * P, :].rearrange("(p r) d -> p (r d)", p=P)
            for r in range(0, MC, NT):
                w = min(NT, MC - r) * D
                sp.dma_start(xz[:, r * D:r * D + w], ACC[:, 0:w]).then_inc(s_zero, 16)
            sp.wait_ge(s_pos, 2)
            sp.dma_start(pend, Hb[:, 8 * EW:12 * EW]).then_inc(s_pend, 16)
            for j in range(ROUND):
                sp.wait_ge(s_slot[j], 16 * ER)
            sp.wait_ge(s_init, 32)
            sp.dma_start(REC[:, :], recs[0][0:NCH * P, :].rearrange("(p c) f -> p (c f)", p=P)).then_inc(s_rec, 16)

            def store_rows(k):
                for q, nt, _ in groups(sp):
                    src = Z[:, QW:QW + nt * D] if k == 3 else part(Hb if k in (1, 2) else X, q, nt)
                    sp.wait_ge(s_fin, q + NQ * k + 1)
                    if k == PASSES - 1 and fixed(q) and q == NQ - 1:
                        sp.dma_start(out[(NT - 1) * P:N, :], src[0:LAST, :]).then_inc(s_out, 16)
                        continue
                    table, s = (out, s_out) if k == PASSES - 1 else (tables[k + 1], s_tab)
                    rows = table[q * QT * P:(q * QT + nt) * P, :] if fixed(q) else table[DS(q * (QT * P), nt * P), :]
                    sp.dma_start(rows.rearrange("(t p) d -> p t d", p=P), tiles(src, nt)).then_inc(s, 16)

            for k in range(4):
                store_rows(k)
                weights(k + 1)
            sp.wait_ge(s_xsc, 16 * 2 * NT)
            sp.wait_ge(s_route, 3)
            sp.dma_start(B1R, a["L2_gnn_b1"]).then_inc(s_b1, 16)

            def store_outputs(j, c):
                rows = ys_dram[c * P:(c + 1) * P, :] if fixed(c) else ys_dram[DS(c * P, P), :]
                sp.dma_start(rows, YB[j]).then_inc(s_ys[j], 16)

            for g, j, c in chunks(sp):
                if j == 0:
                    experts = load_values(sp, ET, c, MB, NE - 1)
                e = experts[j]
                if not (fixed(g) and g == 0):
                    sp.wait_ge(s_et, c - (MB - 1))
                sp.dma_start(XSB[j], xs_dram[c * P:(c + 1) * P, :] if fixed(c) else xs_dram[DS(c * P, P), :]).then_inc(s_xl[j], 16)
                if not (fixed(g) and g == 0):
                    sp.wait_ge(s_yc, c - (MB - 1))
                    store_outputs(j, c - MB)
                sp.dma_start(W1B[j].rearrange("p (k n) -> p k n", k=2),
                             w1_rows[DS(e * D, D), :].rearrange("(k p) n -> p k n", p=P)).then_inc(s_wl[j], 16)
                sp.dma_start(W2B[j].rearrange("p (k n) -> p k n", k=4),
                             w2_rows[DS(e * HID, HID), :].rearrange("(k p) n -> p k n", p=P)).then_inc(s_wl[j], 16)
                sp.dma_start(B2B[j], a["L2_gnn_b2"][DS(e, 1), :].broadcast_to((P, D))).then_inc(s_wl[j], 16)
            for j in range(MB):
                sp.wait_ge(s_yc, MC - MB + j + 1)
                store_outputs(j, MC - MB + j)
            for j in range(2):
                sp.wait_ge(s_win[j], 16 * ROUND * sum(LOTS) // 2)
            sp.wait_ge(s_acc, 5 * NCH)
            sp.wait_ge(s_stage, 2 * ER + 10 * NR)
            sp.dma_start(REC[:, :], recs[1][0:NCH * P, :].rearrange("(p c) f -> p (c f)", p=P)).then_inc(s_rec, 16)
            sp.wait_ge(s_mm, 5 * NQ)
            sp.dma_start(VEC[:, 0:D], a["L2_gnn_gamma"].partition_broadcast(P)).then_inc(s_bnv, 16)
            sp.dma_start(VEC[:, D:2 * D], a["L2_gnn_beta"].partition_broadcast(P)).then_inc(s_bnv, 16)
            store_rows(4)
            weights(5)
            store_rows(5)
            sp.wait_ge(s_out, 16 * NQ)

        @block.gpsimd
        def _(pool):
            imprecise = dict(allow_small_or_imprecise_dtypes=True)
            pool.iota(iota[:, :], pattern=[[1, P]], base=0, channel_multiplier=0, **imprecise)
            pool.iota(iotam[:, :], pattern=[[1, MC]], base=0, channel_multiplier=0, **imprecise)
            pool.iota(IM[:, :], pattern=[[1, NE]], base=-NE, channel_multiplier=0, **imprecise)
            pool.iota(IOTC, pattern=[[1, NCH]], base=0, channel_multiplier=0, **imprecise)
            pool.iota(EDUMP, pattern=[[1, EW]], base=NCH * P, channel_multiplier=EW, **imprecise)
            pool.iota(DUMP[:, :], pattern=[[P, 2 * NT]], base=MC * P, channel_multiplier=1, **imprecise)
            pool.memset(ident[:, :], 0.0)
            pool.memset(ones[:, :], 1.0).then_inc(s_const, 1)
            pool.wait_ge(s_const, 1)
            pool.affine_select(out=ident[:, :], in_=ident[:, :], compare_op=ALU.not_equal, fill=1.0, base=0,
                               pattern=[[-1, P]], channel_multiplier=1)
            pool.affine_select(out=tri[:, :], in_=ones[:, :], compare_op=ALU.is_gt, fill=0.0, base=0,
                               pattern=[[1, P]], channel_multiplier=-1)
            pool.affine_select(out=trii[:, :], in_=ones[:, :], compare_op=ALU.is_ge, fill=0.0, base=0,
                               pattern=[[1, P]], channel_multiplier=-1)
            pool.affine_select(out=onesl[:, :], in_=ones[:, :], compare_op=ALU.is_ge, fill=0.0, base=LAST - 1,
                               pattern=[[0, P]], channel_multiplier=-1).then_inc(s_const, 1)

            def scatter_half(i, h):
                wait(pool, s_stage, i * 2 + h + 1)
                for j in range(h * HALF, (h + 1) * HALF):
                    pool.indirect_dma_start(recs[0], bass.IndirectOffsetOnAxis(ap=IDX[:, j:j + 1], axis=0),
                                            STG[:, j * 4:j * 4 + 4], None).then_inc(s_slot[j], 16)

            pool.wait_ge(s_init, 32)
            with pool.Fori(0, ER) as i:
                for h in range(2):
                    scatter_half(i, h)
            pool.wait_ge(s_pend, 16)

            def lot_round(k, i):
                r = i * 2 + sum(LOTS[:k])
                for b in range(2):
                    if not (fixed(r) and r == 0):
                        wait(pool, s_win[b], (i + sum(LOTS[:k]) // 2) * (16 * ROUND))
                    src = pend[:, (r + b) * W:(r + b + 1) * W] if fixed(r) else pend[:, DS((r + b) * W, W)]
                    pool.dma_start(LOT[:, b * W:(b + 1) * W], src).then_inc(s_lot[b], 16)
                for b in range(2):
                    wait(pool, s_lot[b], (i + sum(LOTS[:k]) // 2) * 16 + 16)
                    for j in range(ROUND):
                        o = b * W + j * 4
                        pool.indirect_dma_start(recs[1], bass.IndirectOffsetOnAxis(ap=LOT[:, o + 3:o + 4].bitcast(u32), axis=0),
                                                LOT[:, o:o + 4], None).then_inc(s_win[b], 16)

            W = ROUND * 4

            def lot_rounds(k):
                lot_round(k, 0)
                with pool.Fori(1, LOTS[k] // 2) as i:
                    lot_round(k, i)


            def gather_half(k, i, h, first):
                n = i * 2 + 2 * NR * k + h
                wait(pool, s_stage, n + 2 * ER + 1)
                if not (first and k == 0):
                    wait(pool, s_prod, n - 1)
                for j in range(h * HALF, (h + 1) * HALF):
                    pool.indirect_dma_start(ring[:, j * D:(j + 1) * D], None, tables[k],
                                            bass.IndirectOffsetOnAxis(ap=IDX[:, j:j + 1], axis=0)).then_inc(s_slot[j], 16)

            prep = Steps(pool, s_prep)

            def prepare(k, q, nt):
                if not (fixed(q) and q == 0):
                    wait(pool, s_t, q + NQ * k)
                acc, x = part(ACC, q, nt), part(X, q, nt)
                tt = nc.gpsimd.tensor_tensor
                z, z2 = Z[:, 0:nt * D], Z[:, QW:QW + nt * D]
                prep.alone = True
                if k == 0:
                    pool.tensor_copy(z, acc)
                    last = pool.tensor_copy(z2, x)
                elif k <= 3:
                    prep.link(tt(z, x if k == 1 else part(Hb, q, nt), EPS1[:, :].broadcast_to((P, nt * D)), ALU.mult))
                    last = tt(z, z, acc, ALU.add)
                elif k == 4:
                    prep.link(tt(tiles(z, nt), tiles(acc, nt), at(RIN, q * QT, nt).unsqueeze(2).broadcast_to((P, nt, D)), ALU.mult))
                    last = pool.tensor_copy(z2, x)
                else:
                    prep.link(tt(tiles(z, nt), tiles(acc, nt), vec(1, nt), ALU.mult))
                    last = tt(z, x, z, ALU.subtract)
                last.then_inc(s_z, 1)

            for k in range(PASSES):
                if k == 5:
                    expert_moves(pool, lot_rounds)
                if k:
                    wait(pool, s_tab, 16 * NQ * k)
                for h in range(2):
                    gather_half(k, 0, h, True)
                with pool.Fori(1, NR) as i:
                    for h in range(2):
                        gather_half(k, i, h, False)
                pool.wait_ge(s_acc, NCH * (k + 1))
                if k == 0:
                    pool.wait_ge(s_x, 32)
                else:
                    pool.wait_ge(s_vec, k)
                if k == 4:
                    pool.wait_ge(s_deg, 2)
                for q, nt, _ in groups(pool, prep, 1 if k else 0):
                    prepare(k, q, nt)

        @block.tensor
        def _(pe):
            mm = nc.tensor.matmul
            pe.wait_ge(s_const, 2)
            for b in range(2):
                pe.wait_ge(s_cnt, 3 * b + 1)
                mm(bank(0, 1)[0:NT, :], CNT[:, 0:NT], ones[:, 0:1], start=True, stop=True).then_inc(s_psort, 1)
                pe.wait_ge(s_cnt, 3 * b + 2)
                mm(bank(1, NT), tri[:, :], CNT[:, 0:NT], start=True, stop=False)
                mm(bank(1, NT), nchb[0:NT, :], tri[0:NT, 0:NT], start=False, stop=True)
                mm(bank(2, 1)[0:NT, :], trii[0:NT, 0:NT], col[0:NT, 1:2], start=True, stop=True).then_inc(s_psort, 1)
                pe.wait_ge(s_cnt, 3 * b + 3)
                for c in range(2):
                    last = mm(bank(3 + c, NCH // 2)[0:1, :], ones[0:NT, 0:1], CMAP[0:NT, c * (NCH // 2):(c + 1) * (NCH // 2)],
                              start=True, stop=True)
                last.then_inc(s_psort, 1)

            def hist_half(b, i, h, start, stop):
                pe.wait_ge(s_oh, i * 2 + 2 * ER * b + h + 1)
                for j in range(HALF):
                    last = mm(bank(6 + b, NT), OHL[h][:, j, :], OHH[h][:, j, :], start=start and j == 0,
                              stop=stop and j == HALF - 1, skip_group_check=True)
                last.then_inc(s_hist, 1)

            for b in range(2):
                hist_half(b, 0, 0, True, False)
                hist_half(b, 0, 1, False, False)
                with pe.Fori(1, ER - 1) as i:
                    for h in range(2):
                        hist_half(b, i, h, False, False)
                hist_half(b, ER - 1, 0, False, False)
                hist_half(b, ER - 1, 1, False, True)

            pe.wait_ge(s_w, w_count(0))
            for m in range(2):
                for k in range(2):
                    for o in range(2):
                        last = nc.tensor.transpose(bank(m, P, k * D + o * P), wmat(m, o)[:, k * P:(k + 1) * P], ident[:, :])
            last.then_inc(s_wt, 1)
            pe.wait_ge(s_wtc, 1)
            pe.wait_ge(s_deg, 1)

            def prod_half(k, i, h, first):
                n = i * 2 + 2 * NR * k + h
                pe.wait_ge(s_pick, n + 1)
                if not (first and k == 0):
                    pe.wait_ge(s_acc, n * HALF - HALF)
                for j in range(h * HALF, (h + 1) * HALF):
                    pe.wait_ge(s_slot[j], i * 16 + 16 * (rounds(k) + 1))
                    last = mm(PS[:, j * D:(j + 1) * D], pick[:, j * P:(j + 1) * P], ring[:, j * D:(j + 1) * D],
                              start=True, stop=True)
                last.then_inc(s_prod, 1)

            def transposes(k, q, nt):
                pe.wait_ge(s_z, q + NQ * k + 1)
                if not (fixed(q) and q == 0 and k == 0):
                    pe.wait_ge(s_zt, q + NQ * k)
                for o in range(operands(k)):
                    for b in range(2):
                        for t in range(nt):
                            last = nc.tensor.transpose(bank(2 * o + b, P, t * P), Z[:, o * QW + t * D + b * P:o * QW + t * D + (b + 1) * P],
                                                       ident[:, :])
                last.then_inc(s_t, 1)

            def layer(k, q, nt, nxt):
                if k in (1, 2, 3):
                    pe.wait_ge(s_zt, q + NQ * k + 1)
                    if not (fixed(q) and q == 0 and k == 1):
                        pe.wait_ge(s_m1, q + NQ * (k - 1))
                    for b in range(2):
                        for d in range(2):
                            last = mm(bank(2 + b, nt * P), wmat(0, d)[:, b * P:(b + 1) * P], ZT[:, d * 512:d * 512 + nt * P],
                                      start=d == 0, stop=d == 1)
                    last.then_inc(s_mm1, 1)
                    if nxt:
                        transposes(k, q + 1, nxt)
                    pe.wait_ge(s_m1, q + NQ * (k - 1) + 1)
                    pairs = [(M1T, 0, 1, b) for b in range(2)]
                else:
                    pe.wait_ge(s_zt, q + NQ * k + 1)
                    if nxt:
                        transposes(k, q + 1, nxt)
                    pairs = [(ZT, o * 1024, o, b) for o in range(operands(k)) for b in range(2)]
                if not (fixed(q) and q == 0 and k == 0):
                    pe.wait_ge(s_u, q + NQ * k)
                biases = 1 if k == 4 else 0
                for t in range(nt):
                    o = bank(4 + t // 2, D, t % 2 * D)
                    for n, (src, base, m, b) in enumerate(pairs):
                        last = mm(o, src[:, base + b * 512 + t * P:base + b * 512 + (t + 1) * P], wmat(m, b), start=n == 0,
                                  stop=n == len(pairs) - 1 and not biases)
                    for v in range(biases):
                        last = mm(o, ones[0:1, :], VEC[0:1, v * D:(v + 1) * D], start=False, stop=v == biases - 1)
                last.then_inc(s_mm, 1)
                if k == 4:
                    pe.wait_ge(s_gate, q + 1)
                    if not (fixed(q) and q == 0):
                        pe.wait_ge(s_lgc, q)
                    for b in range(2):
                        for t in range(nt):
                            last = nc.tensor.transpose(bank(6 + b, P, t * P), U[:, t * D + b * P:t * D + (b + 1) * P], ident[:, :])
                    last.then_inc(s_t2, 1)
                    pe.wait_ge(s_t2c, q + 1)
                    for t in range(nt):
                        o = bank(6, NE, t * NE)
                        for b in range(2):
                            mm(o, M1T[:, b * 512 + t * P:b * 512 + (t + 1) * P], WG[:, b * NE:(b + 1) * NE], start=b == 0, stop=False)
                        last = mm(o, ones[0:1, :], BG[0:1, :], start=False, stop=True)
                    last.then_inc(s_lg, 1)

            for k in range(PASSES):
                if k == 5:
                    expert_products(pe)
                for h in range(2):
                    prod_half(k, 0, h, True)
                with pe.Fori(1, NR) as i:
                    for h in range(2):
                        prod_half(k, i, h, False)
                pe.wait_ge(s_w, w_count(k))
                if k == 4:
                    pe.wait_ge(s_vec, 4)
                transposes(k, 0, QT)
                for q, nt, nxt in groups(pe):
                    layer(k, q, nt, nxt)

        @block.scalar
        def _(act):
            S = Steps(act, s_act)
            fn = nc.scalar.activation

            def stage_scatter(i, h):
                if not (fixed(i) and i == 0):
                    for j in range(h * HALF, (h + 1) * HALF):
                        wait(act, s_slot[j], i * 16)
                c = i * ROUND + h * HALF
                fn(IDX[:, h * HALF:(h + 1) * HALF], at(POS[0], c, HALF), ACT.Copy)
                src = ring[:, c * 4:(c + HALF) * 4] if fixed(c) else ring[:, DS(c * 4, HALF * 4)]
                fn(STG[:, h * HALF * 4:(h + 1) * HALF * 4], src, ACT.Copy).then_inc(s_stage, 1)

            act.wait_ge(s_pos, 1)
            for h in range(2):
                stage_scatter(0, h)
            with act.Fori(1, ER) as i:
                for h in range(2):
                    stage_scatter(i, h)

            act.wait_ge(s_wt, 1)
            for m in range(2):
                last = fn(WA[:, m * 512:(m + 1) * 512], bank(m), ACT.Copy)
            last.then_inc(s_wtc, 1)
            act.wait_ge(s_deg, 1)
            fn(RIN[:, :], RIN[:, :], ACT.Sqrt)
            fn(ROUT[:, :], ROUT[:, :], ACT.Sqrt).then_inc(s_degq, 1)
            act.wait_ge(s_rec, 16)

            def stage_gather(k, i, h, first):
                if first and k == 0:
                    for j in range(h * HALF, (h + 1) * HALF):
                        act.wait_ge(s_slot[j], 16 * ER)
                else:
                    wait(act, s_prod, i * 2 + 2 * NR * k + h - 1)
                c = i * ROUND + h * HALF
                src = RECV[:, c:c + HALF, 0] if fixed(c) else RECV[:, DS(c, HALF), 0]
                fn(IDX[:, h * HALF:(h + 1) * HALF], src, ACT.Copy).then_inc(s_stage, 1)

            def copy_transposes(k, q, nt):
                act.wait_ge(s_t, q + NQ * k + 1)
                if not (fixed(q) and q == 0):
                    if k in (1, 2, 3):
                        act.wait_ge(s_mm1, q + NQ * (k - 1))
                    else:
                        act.wait_ge(s_mm, q + NQ * k)
                for b in range(2 * operands(k)):
                    last = fn(ZT[:, b * 512:b * 512 + nt * P], bank(b, nt * P), ACT.Copy)
                last.then_inc(s_zt, 1)

            def normalise(key, q, nt, dst, second=0):
                n = ln_count(key, q, second)
                act.wait_ge(s_var, n)
                fn(SM[:, 4:4 + nt], SM[:, 0:nt], ACT.Sqrt).then_inc(s_sd, 1)
                wait(act, s_rs, n)
                for t in range(nt):
                    last = fn(dst[:, t * D:(t + 1) * D], U[:, t * D:(t + 1) * D], ACT.Identity, bias=SM[:, 12 + t:13 + t],
                              scale=SM[:, 8 + t:9 + t])
                return last

            def early(k, q, nt, nxt):
                if k == 0:
                    act.wait_ge(s_mm, q + 1)
                    if not (fixed(q) and q == 0):
                        act.wait_ge(s_u, q)
                    for t in range(nt):
                        last = fn(SQ[:, 0:D], bank(4 + t // 2, D, t % 2 * D), ACT.Square, accum_out=SM[:, 16 + t:17 + t])
                        S.link(last)
                    fn(SM[:, 20:20 + nt], SM[:, 16:16 + nt], ACT.Sqrt).then_inc(s_nrm, 1)
                if k in (1, 2, 3):
                    act.wait_ge(s_mm1, q + NQ * (k - 1) + 1)
                    if not (fixed(q) and q == 0 and k == 1):
                        act.wait_ge(s_mm, q + NQ * k)
                    for b in range(2):
                        last = fn(M1T[:, b * 512:b * 512 + nt * P], bank(2 + b, nt * P), ACT.Relu, bias=B1C[:, b:b + 1])
                    last.then_inc(s_m1, 1)
                if k == 4:
                    act.wait_ge(s_mm, q + NQ * 4 + 1)
                    if not (fixed(q) and q == 0):
                        act.wait_ge(s_t2, q)
                        act.wait_ge(s_u, q + NQ * 4)
                    for b in range(-(-nt // 2)):
                        w = min(2, nt - 2 * b) * D
                        last = fn(U[:, b * 512:b * 512 + w], bank(4 + b, w), ACT.Copy)
                    last.then_inc(s_gate, 1)
                if nxt:
                    copy_transposes(k, q + 1, nxt)
                if k == 4:
                    act.wait_ge(s_t2, q + 1)
                    for b in range(2):
                        last = fn(M1T[:, b * 512:b * 512 + nt * P], bank(6 + b, nt * P), ACT.Copy)
                    last.then_inc(s_t2c, 1)

            def late(k, q, nt):
                if k in (0, 5):
                    normalise(k, q, nt, part(X, q, nt)).then_inc(s_fin, 1)
                elif k < 4:
                    normalise(k, q, nt, U).then_inc(s_ln, 1)
                    if k == 3:
                        S.link(normalise(3, q, nt, part(X, q, nt), 1))
                        if not (fixed(q) and q == 0):
                            wait(act, s_tab, q * 16 + 16 * NQ * 3)
                        for t in range(nt):
                            last = fn(Z[:, QW + t * D:QW + (t + 1) * D], at(X, q * QW + t * D, D), ACT.Copy,
                                      scale=at(ROUT, q * QT + t))
                        last.then_inc(s_fin, 1)

            for k in range(PASSES):
                if k == 5:
                    expert_scalar(act, S, normalise)
                    act.wait_ge(s_rec, 32)
                for h in range(2):
                    stage_gather(k, 0, h, True)
                with act.Fori(1, NR) as i:
                    for h in range(2):
                        stage_gather(k, i, h, False)
                act.wait_ge(s_w, w_count(k))
                if k == 3:
                    act.wait_ge(s_deg, 2)
                copy_transposes(k, 0, QT)
                for q, nt, nxt in groups(act, S, {0: QT, 3: 1}.get(k, 0)):
                    early(k, q, nt, nxt)
                    if not (fixed(q) and q == 0):
                        late(k, q - 1, QT)
                late(k, NQ - 1, NT - (NQ - 1) * QT)

        @block.vector
        def _(dve):
            V = Steps(dve, s_dve)
            v = nc.vector
            v.memset(Hb[:, 0:2 * EW].bitcast(i32), -1)
            v.memset(WE, 0.0)
            v.memset(X[:, (NT - 1) * D:NT * D], 0.0).then_inc(s_clean, 1)
            v.memset(ACC[:, :], 0.0)
            V.link(v.memset(REC[:, :], 0.0))
            v.memset(RECV[:, :, 1], -1.0).then_inc(s_clean, 1)
            v.memset(ring[:, :], 0.0)
            V.link(v.memset(RK, 0.0))
            dve.wait_ge(s_const, 2)
            dve.wait_ge(s_in, 48)

            for src, hi, lo in ((DST, HI, LO), (SRC, SHI, SLO)):
                V.link(v.tensor_scalar(TMI, src, 7, None, ALU.arith_shift_right))
                V.link(v.tensor_copy(hi, TMI))
                V.link(v.tensor_scalar(TMI, src, P - 1, None, ALU.bitwise_and))
                V.link(v.tensor_copy(lo, TMI))

            def sort(b, hi):
                if b:
                    V.link(v.memset(RK, 0.0))
                for h in V.loop(0, NT, 4):
                    V.link(v.tensor_scalar(OH, hi, at(iota, h), None, ALU.is_equal))
                    V.link(v.tensor_tensor_scan(CUM, OH, OH, 0.0, ALU.add, ALU.max))
                    v.tensor_copy(at(CNT, h), CUM[:, EW - 1:EW])
                    V.link(v.tensor_tensor(TMP, OH, CUM, ALU.mult))
                    V.link(v.tensor_tensor(RK, RK, TMP, ALU.add))
                v.memset(col[:, 0:1], 0.0).then_inc(s_cnt, 1)

                dve.wait_ge(s_psort, 3 * b + 1)
                V.link(v.tensor_scalar(coli[0:NT, 0:1], bank(0, 1)[0:NT, :], float(P - 1), None, ALU.add))
                V.link(v.tensor_scalar(coli[0:NT, 1:2], coli[0:NT, 0:1], 7, None, ALU.arith_shift_right))
                V.link(v.tensor_copy(col[0:NT, 1:2], coli[0:NT, 1:2]))
                v.tensor_scalar(nchb[0:NT, :], ones[0:NT, :], col[0:NT, 1:2], float(P), ALU.mult, ALU.mult).then_inc(s_cnt, 1)
                dve.wait_ge(s_psort, 3 * b + 2)
                v.tensor_copy(OFF[:, 0:NT], bank(1, NT))
                V.link(v.tensor_copy(col[0:NT, 2:3], bank(2, 1)[0:NT, :]))
                v.tensor_scalar(CMAP[0:NT, :], IOTC[0:NT, :], col[0:NT, 2:3], None, ALU.is_ge).then_inc(s_cnt, 1)
                dve.wait_ge(s_psort, 3 * b + 3)
                for c in range(2):
                    w = NCH // 2
                    V.link(v.tensor_scalar(TTS[b][0:1, c * w:(c + 1) * w], bank(3 + c, w)[0:1, :], float(NT - 1), float(D),
                                           ALU.min, ALU.mult))

                for h in V.loop(0, NT, 2):
                    V.link(v.tensor_scalar(OH, hi, at(iota, h), at(OFF, h), ALU.is_equal, ALU.mult))
                    V.link(v.tensor_tensor(RK, RK, OH, ALU.add))
                V.link(v.tensor_scalar(TMI, RK, -1.0, 0.0, ALU.add, ALU.max))
                V.link(v.tensor_scalar(TMJ, TMI, 7, None, ALU.arith_shift_right))
                V.link(v.tensor_copy(TMP, TMJ))
                V.link(v.tensor_scalar(TMJ, TMI, P - 1, None, ALU.bitwise_and))
                V.link(v.tensor_copy(OH, TMJ))
                V.link(v.scalar_tensor_tensor(RK, OH, float(NCH), TMP, ALU.mult, ALU.add))
                V.link(v.tensor_tensor(RK, RK, EDUMP, ALU.subtract))
                V.link(v.tensor_scalar(OH, hi, 0.0, None, ALU.is_ge))
                V.link(v.tensor_tensor(RK, RK, OH, ALU.mult))
                V.link(v.tensor_tensor(POS[b], RK, EDUMP, ALU.add))
                assert b == 0 or sum(LOTS) == ER

            def records(b, other, lo):
                v.tensor_copy(RECE[b][:, :, 0], other)
                v.tensor_copy(RECE[b][:, :, 1], lo)
                if b:
                    v.tensor_copy(Hb[:, 8 * EW:12 * EW].bitcast(u32).rearrange("p (c f) -> p c f", f=4)[:, :, 3], POS[b])
                v.tensor_copy(RECE[b][:, :, 2], WE).then_inc(s_pos, 1)

            sort(0, HI)
            records(0, SRC, LO)
            sort(1, SHI)
            records(1, DST, SLO)

            def one_hot_half(b, i, h, hi, lo):
                n = i * 2 + 2 * ER * b + h
                if not (fixed(i) and i == 0 and b == 0):
                    dve.wait_ge(s_hist, n - 1)
                c = i * ROUND + h * HALF
                l3 = at(lo, c, HALF).unsqueeze(2).broadcast_to((P, HALF, P))
                h3 = at(hi, c, HALF).unsqueeze(2).broadcast_to((P, HALF, NT))
                v.tensor_tensor(OHL[h], iota[:, :].unsqueeze(1).broadcast_to((P, HALF, P)), l3, ALU.is_equal)
                v.tensor_tensor(OHH[h], iota[:, 0:NT].unsqueeze(1).broadcast_to((P, HALF, NT)), h3, ALU.is_equal).then_inc(s_oh, 1)

            for b, (hi, lo) in enumerate(((HI, LO), (SHI, SLO))):
                for h in range(2):
                    one_hot_half(b, 0, h, hi, lo)
                with dve.Fori(1, ER) as i:
                    for h in range(2):
                        one_hot_half(b, i, h, hi, lo)
            dve.wait_ge(s_hist, 4 * ER)
            v.tensor_scalar(RIN[:, :], bank(6, NT), 1.0, None, ALU.max)
            v.tensor_scalar(ROUT[:, :], bank(7, NT), 1.0, None, ALU.max).then_inc(s_deg, 1)
            dve.wait_ge(s_degq, 1)
            V.link(v.reciprocal(RIN[:, :], RIN[:, :]))
            v.reciprocal(ROUT[:, :], ROUT[:, :]).then_inc(s_deg, 1)
            dve.wait_ge(s_deg, 2)
            dve.wait_ge(s_rec, 16)

            def pick_half(k, i, h):
                for j in range(HALF):
                    c = i * ROUND + h * HALF + j
                    p = pick[:, (h * HALF + j) * P:(h * HALF + j + 1) * P]
                    lo = RECV[:, c, 1:2] if fixed(c) else REC[:, DS(c * 4 + 1, 1)]
                    we = RECV[:, c, 2:3] if fixed(c) else REC[:, DS(c * 4 + 2, 1)]
                    if k in (0, 5):
                        last = v.tensor_scalar(p, iota[:, :], lo, we, ALU.is_equal, ALU.mult)
                    else:
                        last = v.tensor_scalar(p, iota[:, :], lo, None, ALU.is_equal)
                last.then_inc(s_pick, 1)

            def add_half(k, i, h):
                n = i * 2 + 2 * NR * k + h
                c = i * ROUND + h * HALF
                at_tile = load_values(dve, TTS[k == 5], c, HALF, (NT - 1) * D)
                dve.wait_ge(s_prod, n + 1)
                for j, t in enumerate(at_tile):
                    if not (fixed(n) and n + j == 0):
                        dve.wait_ge(s_acc, n * HALF + j)
                    slot = h * HALF + j
                    v.tensor_tensor(ACC[:, DS(t, D)], ACC[:, DS(t, D)], PS[:, slot * D:(slot + 1) * D], ALU.add).then_inc(s_acc, 1)

            def statistics(key, q, nt, second=0):
                for t in range(nt):
                    last = v.bn_stats(ST[:, t * 6:(t + 1) * 6], U[:, t * D:(t + 1) * D])
                V.alone = True
                V.link(last)
                for t in range(nt):
                    last = v.bn_aggr(MV[:, t * 2:t * 2 + 2], ST[:, t * 6:(t + 1) * 6])
                V.link(last)
                mv = MV[:, 0:2 * nt].rearrange("p (t s) -> p t s", s=2)
                v.tensor_scalar(SM[:, 0:nt], mv[:, :, 1], LN_EPS, None, ALU.add).then_inc(s_var, 1)
                n = ln_count(key, q, second)
                dve.wait_ge(s_sd, n)
                V.link(v.reciprocal(SM[:, 8:8 + nt], SM[:, 4:4 + nt]))
                v.scalar_tensor_tensor(SM[:, 12:12 + nt], mv[:, :, 0], -1.0, SM[:, 8:8 + nt], ALU.mult, ALU.mult).then_inc(s_rs, 1)

            def consume(k, q, nt):
                dve.wait_ge(s_mm, q + NQ * k + 1)
                if k == 4:
                    dve.wait_ge(s_gate, q + 1)
                    v.tensor_copy(part(ACC, q, nt), U[:, 0:nt * D]).then_inc(s_u, 1)
                    dve.wait_ge(s_lg, q + 1)
                    v.tensor_copy(at(Hb, q * (QT * NE), nt * NE), bank(6, nt * NE)).then_inc(s_lgc, 1)
                    return
                if not (fixed(q) and q == 0):
                    dve.wait_ge(s_fin, q + NQ * k)
                if k == 0:
                    dve.wait_ge(s_nrm, q + 1)
                    V.link(v.tensor_scalar(SM[:, 20:20 + nt], SM[:, 20:20 + nt], 1e-12, None, ALU.max))
                    V.link(v.reciprocal(SM[:, 20:20 + nt], SM[:, 20:20 + nt]))
                    for t in range(nt):
                        last = v.scalar_tensor_tensor(U[:, t * D:(t + 1) * D], bank(4 + t // 2, D, t % 2 * D), SM[:, 20 + t:21 + t],
                                                      at(X, q * QW + t * D, D), ALU.mult, ALU.add)
                else:
                    last = v.tensor_tensor(U[:, 0:nt * D], PS[:, 2048:2048 + nt * D], part(Hb if k in (2, 3) else X, q, nt), ALU.add)
                last.then_inc(s_u, 1)
                dve.wait_ge(s_u, q + NQ * k + 1)
                if k:
                    V.link(v.tensor_tensor(tiles(U[:, 0:nt * D], nt), tiles(U[:, 0:nt * D], nt), vec(0, nt), ALU.add))
                statistics(k, q, nt)
                if k in (1, 2, 3):
                    dve.wait_ge(s_ln, q + NQ * (k - 1) + 1)
                    u = tiles(U[:, 0:nt * D], nt)
                    V.link(v.tensor_tensor(u, u, vec(1, nt), ALU.mult))
                    V.link(v.tensor_tensor(u, u, vec(2, nt), ALU.add))
                    if k < 3:
                        v.tensor_scalar(part(Hb, q, nt), U[:, 0:nt * D], 0.0, None, ALU.max).then_inc(s_fin, 1)
                    else:
                        V.link(v.scalar_tensor_tensor(U[:, 0:nt * D], U[:, 0:nt * D], 0.0, part(X, q, nt), ALU.max, ALU.add))
                        statistics(3, q, nt, 1)

            PER = {0: 5, 1: 6, 2: 6, 3: 10, 4: 0, 5: 4}
            for k in range(PASSES):
                if k == 5:
                    expert_vector(dve, V, statistics)
                    dve.wait_ge(s_rec, 32)
                if k:
                    dve.wait_ge(s_fin, NQ * k)
                    V.link(v.memset(ACC[:, :], 0.0))
                pick_half(k, 0, 0)
                pick_half(k, 0, 1)
                add_half(k, 0, 0)
                with dve.Fori(1, NR) as i:
                    pick_half(k, i, 0)
                    add_half(k, i - 1, 1)
                    pick_half(k, i, 1)
                    add_half(k, i, 0)
                add_half(k, NR - 1, 1)
                dve.wait_ge(s_acc, NCH * (k + 1))
                dve.wait_ge(s_w, w_count(k))
                if k == 0:
                    dve.wait_ge(s_x, 32)
                if k in (1, 2, 3):
                    v.tensor_scalar(EPS1[:, :], EPS1[:, :], 1.0, None, ALU.add).then_inc(s_vec, 1)
                if k == 4:
                    v.tensor_tensor(VEC[:, 0:D], VEC[:, 0:D], VEC[:, D:2 * D], ALU.add).then_inc(s_vec, 1)
                if k == 5:
                    v.tensor_scalar(VEC[:, D:2 * D], VEC[:, D:2 * D], 1.0, None, ALU.add).then_inc(s_vec, 1)
                for q, nt, nxt in groups(dve, V, PER[k]):
                    consume(k, q, nt)


_INS = [
    "x", "src", "dst", "edge_weight", "L0_gnn_w_self", "L0_gnn_w_neigh", "L1_gnn_W1", "L1_gnn_b1",
    "L1_gnn_W2", "L1_gnn_b2", "L1_gnn_eps", "L1_gnn_gamma", "L1_gnn_beta", "L2_gnn_W_gc", "L2_gnn_b_gc",
    "L2_gnn_W_res", "L2_gnn_b_res", "L2_gnn_Wg", "L2_gnn_bg", "L2_gnn_w1", "L2_gnn_b1", "L2_gnn_w2",
    "L2_gnn_b2", "L2_gnn_gamma", "L2_gnn_beta", "L3_gnn_weight", "L3_gnn_learnable_diag", "L3_gnn_bias",
]


def kernel(**inputs):
    import numpy as np
    import concourse.bacc as bacc
    from concourse.bass_utils import run_bass_kernel_spmd as run

    nc = bacc.Bacc("TRN2", target_bir_lowering=False, num_devices=1)
    arrays, aps = {}, {}
    for name in _INS:
        v = np.ascontiguousarray(inputs[name])
        arrays[f"in_{name}"] = v
        aps[name] = nc.dram_tensor(f"in_{name}", v.shape, mybir.dt.from_np(v.dtype), kind="ExternalInput").ap()
    out = nc.dram_tensor("out", (N, D), mybir.dt.float32, kind="ExternalOutput").ap()
    gnn(nc, aps, out)
    return run(nc, [arrays], core_ids=[0]).results[0]["out"]
```

```python
import concourse.bass as bass
from concourse import mybir
from contextlib import ExitStack

N = 6250
E = 106250
D = 256
P = 128
NT = -(-N // P)
LAST = N - (NT - 1) * P
NPAD = NT * P
QT = 4
NQ = -(-NT // QT)
QW = QT * D
EP = 125
EC = E // EP
HALF = 6
ROUND = 2 * HALF
ER = -(-EC // (2 * ROUND)) * 2
NCH = (-(-((E + (P - 1) * NT) // P) // HALF) | 1) * HALF
NH = NCH // HALF
NR = (NH + 1) // 2
EW = NCH
REC_ROWS = NCH * P + P * EW
PASSES = 6
EB = -(-E // (P * P))
RW = EB * P
LOTS = [8, 64]
NE = 64
HID = 512
CAP = 1024
MB = 4
MC = -(-((2 * N + (P - 1) * NE) // P) // MB) * MB
MG = MC // MB
XS_ROWS = MC * P + 2 * NT * P
LN_EPS = 1e-5
BIG = 3.0e38


def gnn(nc, a, out):
    f32, i32, u32, bf16 = mybir.dt.float32, mybir.dt.int32, mybir.dt.uint32, mybir.dt.bfloat16
    ALU, ACT, AX = mybir.AluOpType, mybir.ActivationFunctionType, mybir.AxisListType
    DS = bass.DynSlice
    ctx = ExitStack()
    with ctx:
        def sb(name, cols, dt=f32, rows=P):
            return ctx.enter_context(nc.sbuf_tensor(name, [rows, cols], dt))

        def sem(name):
            return ctx.enter_context(nc.semaphore(name))

        def dram(name, shape, dt=f32):
            return nc.dram_tensor(name, shape, dt, kind="Internal").ap()

        recs = [dram(f"edge_records{b}", (REC_ROWS, 4)) for b in range(2)]
        pend = dram("edges_by_source", (P, EW * 4))
        tables = [a["x"]] + [dram(f"table{k}", (NPAD, D)) for k in range(1, PASSES)]
        xs_dram = dram("expert_inputs", (XS_ROWS, D))
        ys_dram = dram("expert_outputs", (MC * P, D))

        X = sb("X", NT * D)
        Hb = sb("Hb", NT * D)
        ACC = sb("ACC", NT * D)
        ring = sb("ring", 4 * QW)
        pick = sb("pick", 2 * QW)
        REC = sb("REC", NCH * 4)
        TTS = [sb(f"TT{b}", NCH, i32) for b in range(2)]
        WA = sb("WA", 2 * 2 * D)
        VEC = sb("VEC", 4 * D)
        B1C = sb("B1C", 2)
        EPS1 = sb("EPS1", 1)
        STG = sb("STG", ROUND * 4)
        IDX = sb("IDX", ROUND, u32)
        LOT = sb("LOT", 2 * ROUND * 4)
        iota = sb("iota", P)
        ident = sb("ident", P)
        tri = sb("tri", P)
        trii = sb("trii", P)
        ones = sb("ones", P)
        onesl = sb("onesl", P)
        RIN = sb("RIN", NT)
        ROUT = sb("ROUT", NT)
        CNT = sb("CNT", NR + 2)
        OFF = sb("OFF", NR + 2)
        col = sb("col", 8)
        coli = sb("coli", 2, i32)
        nchb = sb("nchb", P)
        FLAG = sb("FLAG", 1, i32)
        ST = sb("ST", QT * 6)
        MV = sb("MV", QT * 2)
        SM = sb("SM", QT * 6)
        WG = sb("WG", 2 * NE)
        BG = sb("BG", NE)
        IM = sb("IM", NE)
        iotam = sb("iotam", MC)
        DUMP = sb("DUMP", 2 * NT)
        G12 = sb("G12", 2 * NT)
        ET = TTS[0][:, 0:MC]
        PS = ctx.enter_context(nc.psum_tensor("PS", [P, 8 * 512], f32))

        def bank(b, w=512, off=0):
            return PS[:, b * 512 + off:b * 512 + off + w]

        Z = ring[:, 0:2 * QW]
        ZT = ring[:, 2 * QW:4 * QW]
        M1T = pick[:, 0:QW]
        U = pick[:, QW:2 * QW]

        s_const = sem("constants_made")
        s_clean = sem("buffers_cleared")
        s_in = sem("edges_loaded")
        s_x = sem("x_loaded")
        s_w = sem("weights_loaded")
        s_wt = sem("weights_transposed")
        s_wtc = sem("weight_transposes_copied")
        s_init = [sem(f"records_initialised{b}") for b in range(2)]
        s_zero = sem("expert_inputs_zeroed")
        s_dve = sem("vector_steps")
        s_act = sem("scalar_steps")
        s_raw = sem("edge_rows_loaded")
        s_order = sem("order_violations_counted")
        s_ordp = sem("order_violations_summed")
        s_flag = sem("order_flag_made")
        s_fstep = sem("row_steps")
        s_sel = sem("row_selections_made")
        s_fprod = sem("row_products_done")
        s_sorta = sem("first_sort_steps")
        s_ready = sem("first_records_ready")
        s_cnt = [sem(f"tile_counts_made{b}") for b in range(2)]
        s_psort = [sem(f"sort_products_done{b}") for b in range(2)]
        s_dump = sem("spare_rows_numbered")
        s_pos = [sem(f"edge_positions_made{b}") for b in range(2)]
        s_staged = sem("scatters_staged")
        s_scat = [sem(f"scatter_half{h}_done") for h in range(2)]
        s_stage = sem("indices_staged")
        s_slot = [sem(f"slot{j}_moved") for j in range(ROUND)]
        s_pend = sem("records_by_source_kept")
        s_lot = [sem(f"record_lot{j}_loaded") for j in range(2)]
        s_win = [sem(f"record_lot{j}_scattered") for j in range(2)]
        s_rec = [sem(f"records_loaded{b}") for b in range(2)]
        s_oh = [sem(f"one_hots{n}_built") for n in range(4)]
        s_hist = [sem(f"histogram_halves{n}_done") for n in range(4)]
        s_deg = sem("degrees_made")
        s_degq = sem("degree_roots_made")
        s_pick = sem("pick_halves_built")
        s_prod = sem("product_halves_done")
        s_acc = sem("chunks_accumulated")
        s_vec = sem("vectors_prepared")
        s_prep = sem("operand_steps")
        s_z = sem("operands_ready")
        s_t = sem("operands_transposed")
        s_zt = sem("transposes_copied")
        s_mm1 = sem("first_products_done")
        s_m1 = sem("hidden_ready")
        s_mm = sem("layer_products_done")
        s_nrm = sem("norms_made")
        s_u = sem("products_consumed")
        s_var = sem("variances_ready")
        s_sd = sem("deviations_ready")
        s_rs = sem("scales_ready")
        s_ln = sem("rows_normalised")
        s_fin = sem("outputs_final")
        s_tab = sem("tables_stored")
        s_gate = sem("gate_inputs_copied")
        s_t2 = sem("gate_inputs_transposed")
        s_t2c = sem("gate_transposes_copied")
        s_lg = sem("logits_done")
        s_lgc = sem("logits_copied")
        s_gap = sem("gate_gaps_made")
        s_exp = sem("gate_exponentials_made")
        s_route = sem("route_steps_made")
        s_rk = sem("rank_products_done")
        s_rkc = sem("ranks_copied")
        s_xsc = sem("expert_inputs_scattered")
        s_wl = [sem(f"expert_weights{j}_loaded") for j in range(MB)]
        s_xl = [sem(f"expert_rows{j}_loaded") for j in range(MB)]
        s_et = sem("expert_inputs_transposed")
        s_xt = sem("expert_transposes_copied")
        s_h = sem("expert_hidden_done")
        s_g = sem("expert_gelu_done")
        s_y = sem("expert_products_done")
        s_yc = sem("expert_outputs_copied")
        s_ys = [sem(f"expert_outputs{j}_stored") for j in range(MB)]
        s_b1 = sem("expert_biases_loaded")
        s_b1t = sem("expert_biases_transposed")
        s_b1c = sem("expert_biases_copied")
        s_comb = [sem(f"combine_slot{j}_gathered") for j in range(8)]
        s_cu = sem("combined")
        s_bnv = sem("batch_vectors_loaded")
        s_cen = sem("rows_centred")
        s_csq = sem("centred_rows_squared")
        s_bnm = sem("batch_sums_done")
        s_bns = sem("batch_root_made")
        s_out = sem("output_stored")
        s_idle = sem("waits_that_stood_alone")

        def hcols(n, dt=f32):
            v = Hb[:, n * EW:(n + 1) * EW]
            return v.bitcast(dt) if dt != f32 else v

        SRC, DST, TMI = hcols(0, i32), hcols(1, i32), hcols(2, i32)
        WE, HI, LO, SHI, SLO, RK, TMP, OH, CUM = (hcols(n) for n in range(3, 12))
        TMJ = hcols(13, i32)
        POS = [hcols(12, u32), hcols(13, u32)]
        DNEXT = POS[0].bitcast(i32)
        EDUMP = [pick[:, 0:EW], CUM]
        IOTC = [t[:, :].bitcast(f32) for t in TTS]
        RECE = [v.rearrange("p (c f) -> p c f", f=4) for v in (ring[:, 0:EW * 4], Hb[:, 8 * EW:12 * EW])]
        RECV = REC[:, :].rearrange("p (c f) -> p c f", f=4)
        OHL = [hcols(n)[:, 0:HALF * P // 2].bitcast(bf16).rearrange("p (c m) -> p c m", c=HALF) for n in (0, 2, 12, 13)]
        OHH = [hcols(n)[:, 512:512 + (HALF * NT + 1) // 2].bitcast(bf16)[:, 0:HALF * NT].rearrange("p (c m) -> p c m", c=HALF)
               for n in (0, 2, 12, 13)]
        RAWS, RAWL, RAWW, RAWH = (ring[:, n * RW:(n + 1) * RW] for n in range(4))
        RAWF = (RAWS, RAWL, RAWW, RAWH)
        SEL = [Hb[:, 8 * EW + n * NCH:8 * EW + (n + 1) * NCH] for n in range(EB - 1)] + [pick[:, 0:NCH]]
        GE = pick[:, 1024:1024 + EB * NT].rearrange("p (b t) -> p b t", b=EB)

        GW = NT * NE
        LOG, OH1, OH2, MM = (Hb[:, n * GW:(n + 1) * GW] for n in range(4))
        W1B = [Hb[:, j * 2048:j * 2048 + 1024] for j in range(MB)]
        W2B = [Hb[:, j * 2048 + 1024:j * 2048 + 2048] for j in range(MB)]
        HT = [Hb[:, 8192 + j * 512:8704 + j * 512] for j in range(MB)]
        B1T0 = 10240
        B1T = Hb[:, B1T0:B1T0 + 256]
        B2B = [Hb[:, 10496 + j * 256:10752 + j * 256] for j in range(MB)]
        XSB, XTB, YB = ([ring[:, (m * MB + j) * 256:(m * MB + j + 1) * 256] for j in range(MB)] for m in range(3))
        B1R = pick[0:NE, 0:HID]
        RNK = ring[:, 0:GW]
        RT = ring[:, GW:GW + 4 * NT]
        SI = ring[:, GW + 4 * NT:GW + 6 * NT].bitcast(u32)
        GI = ring[:, GW + 6 * NT:GW + 8 * NT].bitcast(u32)
        RB = 448

        block = ctx.enter_context(nc.Block())

        def wait(e, s, value):
            e.wait_ge(s, value)
            if not isinstance(value, int):
                e.sem_inc(s_idle, 1)

        class Steps:

            def __init__(self, e, s):
                self.e, self.s, self.at, self.n, self.alone = e, s, 0, 0, False

            def link(self, ins):
                ins.then_inc(self.s, 1)
                self.at = self.at + 1
                self.n += 1
                wait(self.e, self.s, self.at) if self.alone else self.e.wait_ge(self.s, self.at)
                self.alone = False

            def count(self, ins):
                ins.then_inc(self.s, 1)
                self.at = self.at + 1
                self.n += 1

            def sync(self):
                self.e.wait_ge(self.s, self.at)

            def loop(self, start, end, per):
                base, n = self.at, self.n
                with self.e.Fori(start, end) as i:
                    self.at = (i - start) * per + base if per else base
                    yield i
                assert self.n - n == per, (self.n - n, per)
                self.at = base + (end - start) * per

        def groups(e, steps=None, per=0):
            last = NT - (NQ - 1) * QT
            yield 0, QT, QT
            if steps is None:
                with e.Fori(1, NQ - 2) as q:
                    yield q, QT, QT
            else:
                yield from ((q, QT, QT) for q in steps.loop(1, NQ - 2, per))
            yield NQ - 2, QT, last
            yield NQ - 1, last, 0

        def chunks(e):
            for j in range(MB):
                yield 0, j, j
            with e.Fori(1, MG - 1) as g:
                for j in range(MB):
                    yield g, j, g * MB + j
            for j in range(MB):
                yield MG - 1, j, (MG - 1) * MB + j

        def fixed(v):
            return isinstance(v, int)

        def at(buf, c, w=1):
            return buf[:, c:c + w] if fixed(c) else buf[:, DS(c, w)]

        def load_values(e, row, c, w, most):
            return nc.values_load_multi_w_load_instructions(
                row[0:1, c:c + w] if fixed(c) else row[0:1, DS(c, w)], engines=(e.engine,), min_val=0, max_val=most,
                skip_runtime_bounds_check_because="the row's numbers are clamped where it is made")[1]

        def part(buf, q, nt):
            return at(buf, q * QW, nt * D)

        def tiles(v, nt):
            return v.rearrange("p (t d) -> p t d", t=nt)

        def vec(n, nt):
            return VEC[:, n * D:(n + 1) * D].unsqueeze(1).broadcast_to((P, nt, D))

        def wmat(m, k):
            return WA[:, (m * 2 + k) * D:(m * 2 + k + 1) * D]

        def ln_count(k, q, second=0):
            base = {0: 0, 1: NQ, 2: 2 * NQ, 3: 3 * NQ, "bn": 5 * NQ, 5: 6 * NQ}[k]
            return base + (2 * q + second if k == 3 else q) + 1

        W_DMAS = [2, 7, 7, 7, 6, 3]

        def w_count(k):
            return 16 * sum(W_DMAS[:k + 1])

        def rounds(k, h):
            return (NR - h) * k

        def operands(k):
            return 2 if k in (0, 4) else 1

        def unsorted(e):
            e.wait_ge(s_flag, 1)
            return load_values(e, FLAG, 0, 1, 1)[0]

        w1_rows = a["L2_gnn_w1"].rearrange("e d h -> (e d) h")
        w2_rows = a["L2_gnn_w2"].rearrange("e h d -> (e h) d")
        SQ = VEC[:, 0:D]
        CMAP = Hb[:, 9 * EW:9 * EW + NCH]

        def expert_moves(pool, lot_rounds):
            pool.wait_ge(s_pend, 16)
            pool.wait_ge(s_init[1], 16)
            lot_rounds(0)
            pool.wait_ge(s_zero, 64)
            pool.wait_ge(s_route, 3)
            for n in range(2 * NT):
                t, s = n // 2, n % 2
                pool.indirect_dma_start(xs_dram, bass.IndirectOffsetOnAxis(ap=SI[:, s * NT + t:s * NT + t + 1], axis=0),
                                        ACC[:, t * D:(t + 1) * D], None).then_inc(s_xsc, 16)
            lot_rounds(1)
            for j in range(MB):
                pool.wait_ge(s_ys[j], 16 * MG)
            for n in range(2 * NT):
                t, s = n // 2, n % 2
                if n >= 8:
                    pool.wait_ge(s_cu, n - 7)
                pool.indirect_dma_start(ring[:, n % 8 * D:(n % 8 + 1) * D], None, ys_dram,
                                        bass.IndirectOffsetOnAxis(ap=GI[:, s * NT + t:s * NT + t + 1], axis=0)).then_inc(s_comb[n % 8], 16)

        def expert_products(pe):
            mm = nc.tensor.matmul
            pe.wait_ge(s_route, 1)
            for b in range(GW // RB):
                mm(bank(b, RB), tri[:, :], MM[:, b * RB:(b + 1) * RB], start=True, stop=False)
                mm(bank(b, RB), ones[:, :], LOG[:, b * RB:(b + 1) * RB], start=False, stop=True)
            mm(bank(7, 1)[0:NE, :], CNT[:, 0:NE], ones[:, 0:1], start=True, stop=True).then_inc(s_rk, 1)
            pe.wait_ge(s_route, 2)
            mm(bank(7, NE, 64), nchb[0:NE, :], tri[0:NE, 0:NE], start=True, stop=True)
            mm(bank(7, 1, 192)[0:NE, :], trii[0:NE, 0:NE], col[0:NE, 1:2], start=True, stop=True).then_inc(s_rk, 1)
            pe.wait_ge(s_gap, 2)
            mm(bank(7, MC, 256)[0:1, :], ones[0:NE, 0:1], pick[0:NE, 0:MC], start=True, stop=True).then_inc(s_rk, 1)
            pe.wait_ge(s_route, 3)
            pe.wait_ge(s_b1, 16)
            for m in range(4):
                last = nc.tensor.transpose(bank(2, NE, m * NE), B1R[:, m * P:(m + 1) * P], ident[0:NE, 0:NE])
            last.then_inc(s_b1t, 1)

            def transpose(g, j, c):
                pe.wait_ge(s_xl[j], g * 16 + 16)
                if not (fixed(c) and c == 0):
                    pe.wait_ge(s_xt, c)
                for b in range(2):
                    last = nc.tensor.transpose(bank(0, P, b * P), XSB[j][:, b * P:(b + 1) * P], ident[:, :])
                last.then_inc(s_et, 1)

            def hidden(g, j, c):
                pe.wait_ge(s_xt, c + 1)
                pe.wait_ge(s_wl[j], g * 48 + 48)
                if not (fixed(c) and c < MB):
                    pe.wait_ge(s_g, c - (MB - 1))
                for m in range(4):
                    for b in range(2):
                        last = mm(bank(3 + j, P, m * P), W1B[j][:, b * HID + m * P:b * HID + (m + 1) * P],
                                  XTB[j][:, b * P:(b + 1) * P], start=b == 0, stop=b == 1)
                last.then_inc(s_h, 1)

            def output(j, c):
                pe.wait_ge(s_g, c + 1)
                if not (fixed(c) and c == 0):
                    pe.wait_ge(s_yc, c)
                for m in range(4):
                    mm(bank(1, D), HT[j][:, m * P:(m + 1) * P], W2B[j][:, m * D:(m + 1) * D], start=m == 0, stop=False)
                mm(bank(1, D), ones[0:1, :], B2B[j][0:1, :], start=False, stop=True).then_inc(s_y, 1)

            transpose(0, 0, 0)
            for g, j, c in chunks(pe):
                if not (fixed(c) and c == MC - 1):
                    transpose(g + (j == MB - 1), (j + 1) % MB, c + 1)
                hidden(g, j, c)
                if not (fixed(c) and c == 0):
                    output((j + MB - 1) % MB, c - 1)
            output((MC - 1) % MB, MC - 1)

            pe.wait_ge(s_cu, 2 * NT)
            mm(bank(0, D), ones[:, :], ACC[:, 0:D], start=True, stop=False)
            with pe.Fori(1, NT - 1) as t:
                mm(bank(0, D), ones[:, :], ACC[:, DS(t * D, D)], start=False, stop=False, skip_group_check=True)
            mm(bank(0, D), onesl[:, :], ACC[:, (NT - 1) * D:NT * D], start=False, stop=True).then_inc(s_bnm, 1)
            for q, nt, nxt in groups(pe):
                pe.wait_ge(s_csq, q + 1)
                for t in range(nt):
                    last = mm(bank(1, D), ones[:, :] if nxt else onesl[:, :], Z[:, t * D:(t + 1) * D],
                              start=fixed(q) and q == 0 and t == 0, stop=not nxt, skip_group_check=True)
                last.then_inc(s_bnm, 1)

        def expert_scalar(act, S, normalise):
            fn = nc.scalar.activation
            act.wait_ge(s_gap, 1)
            fn(RT[:, 0:NT], RT[:, 0:NT], ACT.Exp).then_inc(s_exp, 1)
            act.wait_ge(s_rk, 1)
            for b in range(GW // RB):
                last = fn(RNK[:, b * RB:(b + 1) * RB], bank(b, RB), ACT.Copy)
            last.then_inc(s_rkc, 1)
            act.wait_ge(s_b1t, 1)
            fn(B1T, bank(2, 4 * NE), ACT.Copy).then_inc(s_b1c, 1)
            act.wait_ge(s_b1c, 1)
            for g, j, c in chunks(act):
                if j == 0:
                    experts = load_values(act, ET, c, MB, NE - 1)
                wait(act, s_h, c + 1)
                if not (fixed(c) and c < MB):
                    wait(act, s_y, c - (MB - 1))
                e = experts[j]
                for m in range(4):
                    last = fn(HT[j][:, m * P:(m + 1) * P], bank(3 + j, P, m * P), ACT.Gelu, bias=Hb[:, DS(e + (B1T0 + m * NE), 1)])
                last.then_inc(s_g, 1)
            for q, nt, _ in groups(act):
                wait(act, s_cen, q + 1)
                if not (fixed(q) and q == 0):
                    wait(act, s_bnm, q + 1)
                fn(Z[:, 0:nt * D], part(ACC, q, nt), ACT.Square).then_inc(s_csq, 1)
            act.wait_ge(s_bns, 1)
            fn(VEC[:, 2 * D:3 * D], VEC[:, 2 * D:3 * D], ACT.Sqrt).then_inc(s_bns, 1)
            for q, nt, _ in groups(act):
                normalise("bn", q, nt, part(X, q, nt)).then_inc(s_fin, 1)

        def expert_vector(dve, V, statistics):
            v = nc.vector
            dve.wait_ge(s_lgc, NQ)
            g3 = lambda b: b.rearrange("p (t e) -> p t e", e=NE)
            over_e = lambda c: c.unsqueeze(2).broadcast_to((P, NT, NE))
            over_t = lambda c: c.unsqueeze(1).broadcast_to((P, NT, NE))
            best, second, sel = RT[:, NT:2 * NT], RT[:, 2 * NT:3 * NT], RT[:, 3 * NT:4 * NT]

            def top(value, oh):
                V.link(v.tensor_reduce(value, g3(LOG), AX.X, ALU.max))
                V.link(v.tensor_tensor(g3(MM), g3(LOG), over_e(value), ALU.is_equal))
                V.link(v.tensor_tensor(g3(MM), g3(MM), over_t(IM[:, :]), ALU.mult))
                V.link(v.tensor_reduce(sel, g3(MM), AX.X, ALU.min))
                V.link(v.tensor_tensor(g3(oh), over_t(IM[:, :]), over_e(sel), ALU.is_equal))

            top(best, OH1)
            V.link(v.scalar_tensor_tensor(LOG, OH1, -BIG, LOG, ALU.mult, ALU.add))
            top(second, OH2)
            v.tensor_tensor(RT[:, 0:NT], second, best, ALU.subtract).then_inc(s_gap, 1)
            dve.wait_ge(s_exp, 1)
            V.link(v.tensor_scalar(G12[:, 0:NT], RT[:, 0:NT], 1.0, None, ALU.add))
            V.link(v.reciprocal(G12[:, 0:NT], G12[:, 0:NT]))
            V.link(v.tensor_tensor(G12[:, NT:2 * NT], G12[:, 0:NT], RT[:, 0:NT], ALU.mult))
            V.link(v.tensor_tensor(MM, OH1, OH2, ALU.add))
            v.tensor_scalar(MM[:, (NT - 1) * NE:], MM[:, (NT - 1) * NE:], onesl[:, 0:1], None, ALU.mult)
            V.link(v.memset(LOG[:, 0:NE], 0.0))
            for t in V.loop(1, NT, 1):
                V.link(v.tensor_tensor(Hb[:, DS(t * NE, NE)], Hb[:, DS(t * NE - NE, NE)], Hb[:, DS(t * NE + (3 * GW - NE), NE)], ALU.add))
            v.tensor_tensor(CNT[:, 0:NE], LOG[:, (NT - 1) * NE:], MM[:, (NT - 1) * NE:], ALU.add).then_inc(s_route, 1)
            dve.wait_ge(s_rk, 1)
            V.link(v.tensor_scalar(coli[0:NE, 0:1], bank(7, 1)[0:NE, :], float(CAP), float(P - 1), ALU.min, ALU.add))
            V.link(v.tensor_scalar(coli[0:NE, 1:2], coli[0:NE, 0:1], 7, None, ALU.arith_shift_right))
            V.link(v.tensor_copy(col[0:NE, 1:2], coli[0:NE, 1:2]))
            v.tensor_scalar(nchb[0:NE, :], ones[0:NE, :], col[0:NE, 1:2], float(P), ALU.mult, ALU.mult).then_inc(s_route, 1)
            dve.wait_ge(s_rk, 2)
            v.tensor_copy(OFF[:, 0:NE], bank(7, NE, 64))
            V.link(v.tensor_copy(col[0:NE, 2:3], bank(7, 1, 192)[0:NE, :]))
            v.tensor_scalar(pick[0:NE, 0:MC], iotam[0:NE, :], col[0:NE, 2:3], None, ALU.is_ge).then_inc(s_gap, 1)
            dve.wait_ge(s_rk, 3)
            V.link(v.tensor_scalar(ET[0:1, :], bank(7, MC, 256)[0:1, :], float(NE - 1), None, ALU.min))
            dve.wait_ge(s_rkc, 1)
            rank, ok = best, second
            for s, oh in enumerate((OH1, OH2)):
                c = slice(s * NT, (s + 1) * NT)
                V.link(v.tensor_tensor(LOG, oh, RNK, ALU.mult))
                V.link(v.tensor_reduce(rank, g3(LOG), AX.X, ALU.add))
                V.link(v.tensor_scalar(ok, rank, float(CAP), None, ALU.is_lt))
                V.link(v.tensor_scalar(ok[:, NT - 1:NT], ok[:, NT - 1:NT], onesl[:, 0:1], None, ALU.mult))
                V.link(v.tensor_tensor(g3(LOG), g3(oh), over_t(OFF[:, 0:NE]), ALU.mult))
                V.link(v.tensor_reduce(sel, g3(LOG), AX.X, ALU.add))
                V.link(v.tensor_tensor(sel, sel, rank, ALU.add))
                v.tensor_tensor(G12[:, c], G12[:, c], ok, ALU.mult)
                v.tensor_tensor(GI[:, c], sel, ok, ALU.mult)
                V.link(v.tensor_tensor(sel, sel, DUMP[:, c], ALU.subtract))
                V.link(v.tensor_tensor(sel, sel, ok, ALU.mult))
                last = v.tensor_tensor(SI[:, c], sel, DUMP[:, c], ALU.add)
                if s == 0:
                    V.link(last)
            last.then_inc(s_route, 1)

            def copy_in(g, j, c):
                dve.wait_ge(s_et, c + 1)
                if not (fixed(c) and c < MB):
                    dve.wait_ge(s_h, c - (MB - 1))
                v.tensor_copy(XTB[j], bank(0, D)).then_inc(s_xt, 1)

            dve.wait_ge(s_b1c, 1)
            copy_in(0, 0, 0)
            for g, j, c in chunks(dve):
                if not (fixed(c) and c == MC - 1):
                    copy_in(g + (j == MB - 1), (j + 1) % MB, c + 1)
                dve.wait_ge(s_y, c + 1)
                if not (fixed(g) and g == 0):
                    dve.wait_ge(s_ys[j], g * 16)
                v.tensor_copy(YB[j], bank(1, D)).then_inc(s_yc, 1)
            for n in range(2 * NT):
                t, s = n // 2, n % 2
                dve.wait_ge(s_comb[n % 8], 16 * (n // 8 + 1))
                if n:
                    dve.wait_ge(s_cu, n)
                acc = ACC[:, t * D:(t + 1) * D]
                v.scalar_tensor_tensor(acc, ring[:, n % 8 * D:(n % 8 + 1) * D], G12[:, s * NT + t:s * NT + t + 1], acc,
                                       ALU.mult, ALU.add).then_inc(s_cu, 1)
            dve.wait_ge(s_bnm, 1)
            V.link(v.tensor_scalar(VEC[:, 3 * D:4 * D], bank(0, D), 1.0 / N, None, ALU.mult))
            for q, nt, _ in groups(dve):
                acc = tiles(part(ACC, q, nt), nt)
                v.tensor_tensor(acc, acc, vec(3, nt), ALU.subtract).then_inc(s_cen, 1)
            dve.wait_ge(s_bnm, NQ + 1)
            dve.wait_ge(s_bnv, 32)
            v.tensor_scalar(VEC[:, 2 * D:3 * D], bank(1, D), 1.0 / N, LN_EPS, ALU.mult, ALU.add).then_inc(s_bns, 1)
            dve.wait_ge(s_bns, 2)
            V.link(v.reciprocal(VEC[:, 2 * D:3 * D], VEC[:, 2 * D:3 * D]))
            V.link(v.tensor_tensor(VEC[:, 2 * D:3 * D], VEC[:, 2 * D:3 * D], VEC[:, 0:D], ALU.mult))
            dve.wait_ge(s_cen, NQ)
            for q, nt, _ in groups(dve, V, 6):
                if not (fixed(q) and q == 0):
                    dve.wait_ge(s_fin, q + NQ * 4)
                u = tiles(U[:, 0:nt * D], nt)
                V.link(v.tensor_tensor(u, tiles(part(ACC, q, nt), nt), vec(2, nt), ALU.mult))
                V.link(v.tensor_tensor(u, u, vec(1, nt), ALU.add))
                V.link(v.tensor_tensor(U[:, 0:nt * D], U[:, 0:nt * D], part(X, q, nt), ALU.add))
                statistics("bn", q, nt)

        @block.sync
        def _(sp):
            sp.wait_ge(s_clean, 1)
            for dst, name in ((SRC, "src"), (DST, "dst"), (WE, "edge_weight")):
                sp.dma_start(dst[0:EP, 0:EC], a[name].rearrange("(p c) -> p c", c=EC)).then_inc(s_in, 16)
            def weights(k):
                def mat(slot, src):
                    sp.dma_start(WA[:, slot * 2 * D:(slot + 1) * 2 * D].rearrange("p (k n) -> p k n", k=2),
                                 src.rearrange("(k p) n -> p k n", p=P)).then_inc(s_w, 16)

                def row(slot, src):
                    sp.dma_start(VEC[:, slot * D:(slot + 1) * D], src.partition_broadcast(P)).then_inc(s_w, 16)

                if k == 0:
                    mat(0, a["L0_gnn_w_neigh"])
                    mat(1, a["L0_gnn_w_self"])
                elif k <= 3:
                    mat(0, a["L1_gnn_W1"][k - 1])
                    mat(1, a["L1_gnn_W2"][k - 1])
                    row(0, a["L1_gnn_b2"][k - 1])
                    row(1, a["L1_gnn_gamma"][k - 1])
                    row(2, a["L1_gnn_beta"][k - 1])
                    sp.dma_start(B1C[:, :], a["L1_gnn_b1"][k - 1].rearrange("(k p) -> p k", p=P),
                                 allow_slow_non_contiguous=True).then_inc(s_w, 16)
                    sp.dma_start(EPS1[:, :], a["L1_gnn_eps"][k - 1:k].partition_broadcast(P)).then_inc(s_w, 16)
                elif k == 4:
                    mat(0, a["L2_gnn_W_gc"])
                    mat(1, a["L2_gnn_W_res"])
                    row(0, a["L2_gnn_b_gc"])
                    row(1, a["L2_gnn_b_res"])
                    sp.dma_start(WG[:, :].rearrange("p (k n) -> p k n", k=2),
                                 a["L2_gnn_Wg"].rearrange("(k p) n -> p k n", p=P)).then_inc(s_w, 16)
                    sp.dma_start(BG[:, :], a["L2_gnn_bg"].partition_broadcast(P)).then_inc(s_w, 16)
                else:
                    mat(0, a["L3_gnn_weight"])
                    row(0, a["L3_gnn_bias"])
                    row(1, a["L3_gnn_learnable_diag"])

            nxt = a["dst"].rearrange("(o e) -> o e", o=1)
            sp.dma_start(DNEXT[0:EP - 1, 0:EC], nxt[0, 1:1 + (EP - 1) * EC].rearrange("(p c) -> p c", c=EC)).then_inc(s_in, 16)
            sp.dma_start(DNEXT[EP - 1:EP, 0:EC - 1], nxt[0:1, 1 + (EP - 1) * EC:E]).then_inc(s_in, 16)
            whole, left = E // P, E % P
            for raw, name in ((RAWS.bitcast(i32), "src"), (RAWL.bitcast(i32), "dst"), (RAWW, "edge_weight")):
                e1 = a[name].rearrange("(o e) -> o e", o=1)
                nb = whole // P
                sp.dma_start(raw[:, 0:nb * P].rearrange("p (b c) -> p b c", c=P),
                             e1[0, 0:nb * P * P].rearrange("(b p c) -> p b c", p=P, c=P)).then_inc(s_raw, 16)
                sp.dma_start(raw[0:whole - nb * P, nb * P:RW], e1[0, nb * P * P:whole * P].rearrange("(p c) -> p c", c=P)).then_inc(s_raw, 16)
                sp.dma_start(raw[whole - nb * P:whole - nb * P + 1, nb * P:nb * P + left], e1[0:1, whole * P:E]).then_inc(s_raw, 16)
            weights(0)
            sp.dma_start(tiles(X[:, 0:(NT - 1) * D], NT - 1),
                         a["x"][0:(NT - 1) * P, :].rearrange("(t p) d -> p t d", p=P)).then_inc(s_x, 16)
            sp.dma_start(X[0:LAST, (NT - 1) * D:NT * D], a["x"][(NT - 1) * P:N, :]).then_inc(s_x, 16)
            sp.wait_ge(s_clean, 2)
            rows = [rec[0:NCH * P, :].rearrange("(p c) f -> p (c f)", p=P) for rec in recs]
            sp.dma_start(rows[1], REC[:, :]).then_inc(s_init[1], 16)
            with sp.If(unsorted(sp) == 1):
                sp.dma_start(rows[0], REC[:, :]).then_inc(s_init[0], 16)
                for h in range(2):
                    sp.wait_ge(s_scat[h], 16 * HALF * ER)
                sp.wait_ge(s_init[0], 16)
                sp.dma_start(REC[:, :], rows[0]).then_inc(s_rec[0], 16)

            def store_rows(k):
                for q, nt, _ in groups(sp):
                    src = Z[:, QW:QW + nt * D] if k == 3 else part(Hb if k in (1, 2) else X, q, nt)
                    sp.wait_ge(s_fin, q + NQ * k + 1)
                    if k == PASSES - 1 and fixed(q) and q == NQ - 1:
                        sp.dma_start(out[(NT - 1) * P:N, :], src[0:LAST, :]).then_inc(s_out, 16)
                        continue
                    table, s = (out, s_out) if k == PASSES - 1 else (tables[k + 1], s_tab)
                    rows = table[q * QT * P:(q * QT + nt) * P, :] if fixed(q) else table[DS(q * (QT * P), nt * P), :]
                    sp.dma_start(rows.rearrange("(t p) d -> p t d", p=P), tiles(src, nt)).then_inc(s, 16)

            for k in range(4):
                store_rows(k)
                weights(k + 1)
                if k == 0:
                    sp.wait_ge(s_pos[1], 1)
                    sp.dma_start(pend, Hb[:, 8 * EW:12 * EW]).then_inc(s_pend, 16)
                if k == 1:
                    xz = xs_dram[0:MC * P, :].rearrange("(p r) d -> p r d", p=P)
                    for r in range(0, MC, NT):
                        w = min(NT, MC - r)
                        sp.dma_start(xz[:, r:r + w, :], VEC[:, 3 * D:4 * D].unsqueeze(1).broadcast_to((P, w, D))).then_inc(s_zero, 16)
            sp.wait_ge(s_xsc, 16 * 2 * NT)
            sp.wait_ge(s_route, 3)
            sp.dma_start(B1R, a["L2_gnn_b1"]).then_inc(s_b1, 16)

            def store_outputs(j, c):
                rows = ys_dram[c * P:(c + 1) * P, :] if fixed(c) else ys_dram[DS(c * P, P), :]
                sp.dma_start(rows, YB[j]).then_inc(s_ys[j], 16)

            for g, j, c in chunks(sp):
                if j == 0:
                    experts = load_values(sp, ET, c, MB, NE - 1)
                e = experts[j]
                if not (fixed(g) and g == 0):
                    sp.wait_ge(s_et, c - (MB - 1))
                sp.dma_start(XSB[j], xs_dram[c * P:(c + 1) * P, :] if fixed(c) else xs_dram[DS(c * P, P), :]).then_inc(s_xl[j], 16)
                if not (fixed(g) and g == 0):
                    sp.wait_ge(s_yc, c - (MB - 1))
                    store_outputs(j, c - MB)
                sp.dma_start(W1B[j].rearrange("p (k n) -> p k n", k=2),
                             w1_rows[DS(e * D, D), :].rearrange("(k p) n -> p k n", p=P)).then_inc(s_wl[j], 16)
                sp.dma_start(W2B[j].rearrange("p (k n) -> p k n", k=4),
                             w2_rows[DS(e * HID, HID), :].rearrange("(k p) n -> p k n", p=P)).then_inc(s_wl[j], 16)
                sp.dma_start(B2B[j][0:1, :], a["L2_gnn_b2"][DS(e, 1), :]).then_inc(s_wl[j], 16)
            for j in range(MB):
                sp.wait_ge(s_yc, MC - MB + j + 1)
                store_outputs(j, MC - MB + j)
            for j in range(2):
                sp.wait_ge(s_win[j], 16 * ROUND * sum(LOTS) // 2)
            sp.wait_ge(s_acc, 5 * NCH)
            sp.wait_ge(s_stage, 5 * NH)
            sp.dma_start(REC[:, :], rows[1]).then_inc(s_rec[1], 16)
            sp.wait_ge(s_mm, 5 * NQ)
            sp.dma_start(VEC[:, 0:D], a["L2_gnn_gamma"].partition_broadcast(P)).then_inc(s_bnv, 16)
            sp.dma_start(VEC[:, D:2 * D], a["L2_gnn_beta"].partition_broadcast(P)).then_inc(s_bnv, 16)
            store_rows(4)
            weights(5)
            store_rows(5)
            sp.wait_ge(s_out, 16 * NQ)

        @block.gpsimd
        def _(pool):
            imprecise = dict(allow_small_or_imprecise_dtypes=True)
            pool.iota(iota[:, :], pattern=[[1, P]], base=0, channel_multiplier=0, **imprecise)
            pool.iota(iotam[:, :], pattern=[[1, MC]], base=0, channel_multiplier=0, **imprecise)
            pool.iota(IM[:, :], pattern=[[1, NE]], base=-NE, channel_multiplier=0, **imprecise)
            for t in range(2):
                pool.iota(IOTC[t], pattern=[[1, NCH]], base=0, channel_multiplier=0, **imprecise)
            pool.iota(EDUMP[0], pattern=[[1, EW]], base=NCH * P, channel_multiplier=EW, **imprecise)
            pool.iota(DUMP[:, :], pattern=[[P, 2 * NT]], base=MC * P, channel_multiplier=1, **imprecise)
            pool.memset(ident[:, :], 0.0)
            pool.memset(ones[:, :], 1.0).then_inc(s_const, 1)
            pool.wait_ge(s_const, 1)
            pool.affine_select(out=ident[:, :], in_=ident[:, :], compare_op=ALU.not_equal, fill=1.0, base=0,
                               pattern=[[-1, P]], channel_multiplier=1)
            pool.affine_select(out=tri[:, :], in_=ones[:, :], compare_op=ALU.is_gt, fill=0.0, base=0,
                               pattern=[[1, P]], channel_multiplier=-1)
            pool.affine_select(out=trii[:, :], in_=ones[:, :], compare_op=ALU.is_ge, fill=0.0, base=0,
                               pattern=[[1, P]], channel_multiplier=-1)
            pool.affine_select(out=onesl[:, :], in_=ones[:, :], compare_op=ALU.is_ge, fill=0.0, base=LAST - 1,
                               pattern=[[0, P]], channel_multiplier=-1).then_inc(s_const, 1)

            def scatter_half(i, h):
                wait(pool, s_staged, i * 2 + h + 1)
                for j in range(h * HALF, (h + 1) * HALF):
                    pool.indirect_dma_start(recs[0], bass.IndirectOffsetOnAxis(ap=IDX[:, j:j + 1], axis=0),
                                            STG[:, j * 4:j * 4 + 4], None).then_inc(s_scat[h], 16)

            with pool.If(unsorted(pool) == 1):
                pool.wait_ge(s_init[0], 16)
                with pool.Fori(0, ER) as i:
                    for h in range(2):
                        scatter_half(i, h)
            pool.wait_ge(s_ready, 1)

            def lot_round(k, i):
                r = i * 2 + sum(LOTS[:k])
                for b in range(2):
                    if not (fixed(r) and r == 0):
                        wait(pool, s_win[b], (i + sum(LOTS[:k]) // 2) * (16 * ROUND))
                    src = pend[:, (r + b) * W:(r + b + 1) * W] if fixed(r) else pend[:, DS((r + b) * W, W)]
                    pool.dma_start(LOT[:, b * W:(b + 1) * W], src).then_inc(s_lot[b], 16)
                for b in range(2):
                    wait(pool, s_lot[b], (i + sum(LOTS[:k]) // 2) * 16 + 16)
                    for j in range(ROUND):
                        o = b * W + j * 4
                        pool.indirect_dma_start(recs[1], bass.IndirectOffsetOnAxis(ap=LOT[:, o + 3:o + 4].bitcast(u32), axis=0),
                                                LOT[:, o:o + 4], None).then_inc(s_win[b], 16)

            W = ROUND * 4

            def lot_rounds(k):
                lot_round(k, 0)
                with pool.Fori(1, LOTS[k] // 2) as i:
                    lot_round(k, i)

            def gather_half(k, i, h, first):
                n = i * 2 + NH * k + h
                wait(pool, s_stage, n + 1)
                if not (first and k == 0):
                    wait(pool, s_prod, n - 1)
                for j in range(h * HALF, (h + 1) * HALF):
                    pool.indirect_dma_start(ring[:, j * D:(j + 1) * D], None, tables[k],
                                            bass.IndirectOffsetOnAxis(ap=IDX[:, j:j + 1], axis=0)).then_inc(s_slot[j], 16)

            prep = Steps(pool, s_prep)

            def prepare(k, q, nt):
                if not (fixed(q) and q == 0):
                    wait(pool, s_t, q + NQ * k)
                acc, x = part(ACC, q, nt), part(X, q, nt)
                tt = nc.gpsimd.tensor_tensor
                z, z2 = Z[:, 0:nt * D], Z[:, QW:QW + nt * D]
                prep.alone = True
                if k == 0:
                    pool.tensor_copy(z, acc)
                    last = pool.tensor_copy(z2, x)
                elif k <= 3:
                    prep.link(tt(z, x if k == 1 else part(Hb, q, nt), EPS1[:, :].broadcast_to((P, nt * D)), ALU.mult))
                    last = tt(z, z, acc, ALU.add)
                elif k == 4:
                    prep.link(tt(tiles(z, nt), tiles(acc, nt), at(RIN, q * QT, nt).unsqueeze(2).broadcast_to((P, nt, D)), ALU.mult))
                    last = pool.tensor_copy(z2, x)
                else:
                    prep.link(tt(tiles(z, nt), tiles(acc, nt), vec(1, nt), ALU.mult))
                    last = tt(z, x, z, ALU.subtract)
                last.then_inc(s_z, 1)

            for k in range(PASSES):
                if k == 5:
                    expert_moves(pool, lot_rounds)
                if k:
                    wait(pool, s_tab, 16 * NQ * k)
                for h in range(2):
                    gather_half(k, 0, h, True)
                with pool.Fori(1, NR - 1) as i:
                    for h in range(2):
                        gather_half(k, i, h, False)
                gather_half(k, NR - 1, 0, False)
                if k == 0:
                    pool.wait_ge(s_cnt[1], 1)
                    pool.iota(EDUMP[1], pattern=[[1, EW]], base=NCH * P, channel_multiplier=EW, **imprecise).then_inc(s_dump, 1)
                pool.wait_ge(s_acc, NCH * (k + 1))
                if k == 0:
                    pool.wait_ge(s_x, 32)
                else:
                    pool.wait_ge(s_vec, k)
                if k == 4:
                    pool.wait_ge(s_deg, 2)
                for q, nt, _ in groups(pool, prep, 1 if k else 0):
                    prepare(k, q, nt)

        @block.tensor
        def _(pe):
            mm = nc.tensor.matmul
            pe.wait_ge(s_const, 2)

            def sort_products(b):
                pe.wait_ge(s_cnt[b], 1)
                mm(bank(0, 1)[0:NT, :], CNT[:, 0:NT], ones[:, 0:1], start=True, stop=True).then_inc(s_psort[b], 1)
                pe.wait_ge(s_cnt[b], 2)
                mm(bank(1, NT), tri[:, :], CNT[:, 0:NT], start=True, stop=False)
                mm(bank(1, NT), nchb[0:NT, :], tri[0:NT, 0:NT], start=False, stop=True)
                mm(bank(2, 1)[0:NT, :], trii[0:NT, 0:NT], col[0:NT, 1:2], start=True, stop=True).then_inc(s_psort[b], 1)
                pe.wait_ge(s_cnt[b], 3)
                for c in range(2):
                    last = mm(bank(3 + c, NCH // 2)[0:1, :], ones[0:NT, 0:1], CMAP[0:NT, c * (NCH // 2):(c + 1) * (NCH // 2)],
                              start=True, stop=True)
                last.then_inc(s_psort[b], 1)

            pe.wait_ge(s_w, w_count(0))
            for m in range(2):
                for k in range(2):
                    for o in range(2):
                        last = nc.tensor.transpose(bank(m, P, k * D + o * P), wmat(m, o)[:, k * P:(k + 1) * P], ident[:, :])
            last.then_inc(s_wt, 1)
            pe.wait_ge(s_wtc, 1)

            pe.wait_ge(s_order, 1)
            mm(bank(5, 1)[0:1, :], col[:, 4:5], ones[:, 0:1], start=True, stop=True).then_inc(s_ordp, 1)
            flag = unsorted(pe)
            with pe.If(flag == 1):
                sort_products(0)
            with pe.Else():
                pe.wait_ge(s_sel, 1)
                for b in range(EB):
                    last = mm(bank(0, 1)[0:NT, :], GE[:, b, :], ones[:, 0:1], start=b == 0, stop=b == EB - 1)
                last.then_inc(s_fprod, 1)
                pe.wait_ge(s_sel, 2)
                for c in range(2):
                    last = mm(bank(1 + c, NCH // 2), ones[0:NT, :], CMAP[0:NT, c * (NCH // 2):(c + 1) * (NCH // 2)], start=True, stop=True)
                last.then_inc(s_fprod, 1)
                for b in range(EB):
                    pe.wait_ge(s_sel, 3 + b)
                    for f, raw in enumerate(RAWF):
                        for c in range(2):
                            last = mm(bank(2 * f + c, NCH // 2), raw[:, b * P:(b + 1) * P], SEL[b][:, c * (NCH // 2):(c + 1) * (NCH // 2)],
                                      start=b == 0, stop=b == EB - 1)
                last.then_inc(s_fprod, 1)

            def hist_half(b, i, h, first):
                pe.wait_ge(s_oh[2 * b + h], i)
                for j in range(HALF):
                    last = mm(bank(6 + b, NT), OHL[2 * b + h][:, j, :], OHH[2 * b + h][:, j, :], start=first and j == 0, stop=False,
                              skip_group_check=True)
                last.then_inc(s_hist[2 * b + h], 1)

            def prod_half(k, i, h, first):
                n = i * 2 + NH * k + h
                pe.wait_ge(s_pick, n + 1)
                if not (first and k == 0):
                    pe.wait_ge(s_acc, n * HALF - HALF)
                for j in range(h * HALF, (h + 1) * HALF):
                    pe.wait_ge(s_slot[j], i * 16 + 16 * (rounds(k, h) + 1))
                    last = mm(PS[:, j * D:(j + 1) * D], pick[:, j * P:(j + 1) * P], ring[:, j * D:(j + 1) * D],
                              start=True, stop=True)
                last.then_inc(s_prod, 1)

            def transposes(k, q, nt):
                pe.wait_ge(s_z, q + NQ * k + 1)
                if not (fixed(q) and q == 0 and k == 0):
                    pe.wait_ge(s_zt, q + NQ * k)
                for o in range(operands(k)):
                    for b in range(2):
                        for t in range(nt):
                            last = nc.tensor.transpose(bank(2 * o + b, P, t * P), Z[:, o * QW + t * D + b * P:o * QW + t * D + (b + 1) * P],
                                                       ident[:, :])
                last.then_inc(s_t, 1)

            def layer(k, q, nt, nxt):
                if k in (1, 2, 3):
                    pe.wait_ge(s_zt, q + NQ * k + 1)
                    if not (fixed(q) and q == 0 and k == 1):
                        pe.wait_ge(s_m1, q + NQ * (k - 1))
                    for b in range(2):
                        for d in range(2):
                            last = mm(bank(2 + b, nt * P), wmat(0, d)[:, b * P:(b + 1) * P], ZT[:, d * 512:d * 512 + nt * P],
                                      start=d == 0, stop=d == 1)
                    last.then_inc(s_mm1, 1)
                    if nxt:
                        transposes(k, q + 1, nxt)
                    pe.wait_ge(s_m1, q + NQ * (k - 1) + 1)
                    pairs = [(M1T, 0, 1, b) for b in range(2)]
                else:
                    pe.wait_ge(s_zt, q + NQ * k + 1)
                    if nxt:
                        transposes(k, q + 1, nxt)
                    pairs = [(ZT, o * 1024, o, b) for o in range(operands(k)) for b in range(2)]
                if not (fixed(q) and q == 0 and k == 0):
                    pe.wait_ge(s_u, q + NQ * k)
                biases = 1 if k == 4 else 0
                for t in range(nt):
                    o = bank(4 + t // 2, D, t % 2 * D)
                    for n, (src, base, m, b) in enumerate(pairs):
                        last = mm(o, src[:, base + b * 512 + t * P:base + b * 512 + (t + 1) * P], wmat(m, b), start=n == 0,
                                  stop=n == len(pairs) - 1 and not biases)
                    for v in range(biases):
                        last = mm(o, ones[0:1, :], VEC[0:1, v * D:(v + 1) * D], start=False, stop=v == biases - 1)
                last.then_inc(s_mm, 1)
                if k == 4:
                    pe.wait_ge(s_gate, q + 1)
                    if not (fixed(q) and q == 0):
                        pe.wait_ge(s_lgc, q)
                    for b in range(2):
                        for t in range(nt):
                            last = nc.tensor.transpose(bank(6 + b, P, t * P), U[:, t * D + b * P:t * D + (b + 1) * P], ident[:, :])
                    last.then_inc(s_t2, 1)
                    pe.wait_ge(s_t2c, q + 1)
                    for t in range(nt):
                        o = bank(6, NE, t * NE)
                        for b in range(2):
                            mm(o, M1T[:, b * 512 + t * P:b * 512 + (t + 1) * P], WG[:, b * NE:(b + 1) * NE], start=b == 0, stop=False)
                        last = mm(o, ones[0:1, :], BG[0:1, :], start=False, stop=True)
                    last.then_inc(s_lg, 1)

            for k in range(PASSES):
                if k == 5:
                    expert_products(pe)
                for h in range(2):
                    prod_half(k, 0, h, True)
                if k < 2:
                    for h in range(2):
                        prod_half(k, 1, h, False)
                    for n in range(3 if k else 1):
                        hist_half((k + n) // 2, 1, (k + n) % 2, k + n in (0, 2))
                with pe.Fori(1 + (k < 2), NR - 1) as i:
                    for h in range(2):
                        prod_half(k, i, h, False)
                    if k < 2:
                        for n in range(3 if k else 1):
                            hist_half((k + n) // 2, i, (k + n) % 2, False)
                prod_half(k, NR - 1, 0, False)
                if k < 2:
                    for n in range(3 if k else 1):
                        hist_half((k + n) // 2, NR - 1, (k + n) % 2, False)
                if k == 0:
                    pe.wait_ge(s_acc, NCH)
                    sort_products(1)
                    pe.wait_ge(s_cnt[1], 4)
                pe.wait_ge(s_w, w_count(k))
                if k == 4:
                    pe.wait_ge(s_vec, 4)
                transposes(k, 0, QT)
                for q, nt, nxt in groups(pe):
                    layer(k, q, nt, nxt)

        @block.scalar
        def _(act):
            S = Steps(act, s_act)
            fn = nc.scalar.activation

            def stage_scatter(i, h):
                if not (fixed(i) and i == 0):
                    wait(act, s_scat[h], i * (16 * HALF))
                c = i * ROUND + h * HALF
                fn(IDX[:, h * HALF:(h + 1) * HALF], at(POS[0], c, HALF), ACT.Copy)
                src = ring[:, c * 4:(c + HALF) * 4] if fixed(c) else ring[:, DS(c * 4, HALF * 4)]
                fn(STG[:, h * HALF * 4:(h + 1) * HALF * 4], src, ACT.Copy).then_inc(s_staged, 1)

            act.wait_ge(s_wt, 1)
            for m in range(2):
                last = fn(WA[:, m * 512:(m + 1) * 512], bank(m), ACT.Copy)
            last.then_inc(s_wtc, 1)

            with act.If(unsorted(act) == 1):
                act.wait_ge(s_pos[0], 1)
                for h in range(2):
                    stage_scatter(0, h)
                with act.Fori(1, ER) as i:
                    for h in range(2):
                        stage_scatter(i, h)

            act.wait_ge(s_ready, 1)

            def stage_gather(k, i, h, first):
                if not (first and k == 0):
                    wait(act, s_prod, i * 2 + NH * k + h - 1)
                c = i * ROUND + h * HALF
                src = RECV[:, c:c + HALF, 0] if fixed(c) else RECV[:, DS(c, HALF), 0]
                fn(IDX[:, h * HALF:(h + 1) * HALF], src, ACT.Copy).then_inc(s_stage, 1)

            def copy_transposes(k, q, nt):
                act.wait_ge(s_t, q + NQ * k + 1)
                if not (fixed(q) and q == 0):
                    if k in (1, 2, 3):
                        act.wait_ge(s_mm1, q + NQ * (k - 1))
                    else:
                        act.wait_ge(s_mm, q + NQ * k)
                for b in range(2 * operands(k)):
                    last = fn(ZT[:, b * 512:b * 512 + nt * P], bank(b, nt * P), ACT.Copy)
                last.then_inc(s_zt, 1)

            def normalise(key, q, nt, dst, second=0):
                n = ln_count(key, q, second)
                act.wait_ge(s_var, n)
                fn(SM[:, 4:4 + nt], SM[:, 0:nt], ACT.Sqrt).then_inc(s_sd, 1)
                wait(act, s_rs, n)
                for t in range(nt):
                    last = fn(dst[:, t * D:(t + 1) * D], U[:, t * D:(t + 1) * D], ACT.Identity, bias=SM[:, 12 + t:13 + t],
                              scale=SM[:, 8 + t:9 + t])
                return last

            def early(k, q, nt, nxt):
                if k == 0:
                    act.wait_ge(s_mm, q + 1)
                    if not (fixed(q) and q == 0):
                        act.wait_ge(s_u, q)
                    for t in range(nt):
                        last = fn(SQ[:, 0:D], bank(4 + t // 2, D, t % 2 * D), ACT.Square, accum_out=SM[:, 16 + t:17 + t])
                        S.link(last)
                    fn(SM[:, 20:20 + nt], SM[:, 16:16 + nt], ACT.Sqrt).then_inc(s_nrm, 1)
                if k in (1, 2, 3):
                    act.wait_ge(s_mm1, q + NQ * (k - 1) + 1)
                    if not (fixed(q) and q == 0 and k == 1):
                        act.wait_ge(s_mm, q + NQ * k)
                    for b in range(2):
                        last = fn(M1T[:, b * 512:b * 512 + nt * P], bank(2 + b, nt * P), ACT.Relu, bias=B1C[:, b:b + 1])
                    last.then_inc(s_m1, 1)
                if k == 4:
                    act.wait_ge(s_mm, q + NQ * 4 + 1)
                    if not (fixed(q) and q == 0):
                        act.wait_ge(s_t2, q)
                        act.wait_ge(s_u, q + NQ * 4)
                    for b in range(-(-nt // 2)):
                        w = min(2, nt - 2 * b) * D
                        last = fn(U[:, b * 512:b * 512 + w], bank(4 + b, w), ACT.Copy)
                    last.then_inc(s_gate, 1)
                if nxt:
                    copy_transposes(k, q + 1, nxt)
                if k == 4:
                    act.wait_ge(s_t2, q + 1)
                    for b in range(2):
                        last = fn(M1T[:, b * 512:b * 512 + nt * P], bank(6 + b, nt * P), ACT.Copy)
                    last.then_inc(s_t2c, 1)

            def late(k, q, nt):
                if k in (0, 5):
                    normalise(k, q, nt, part(X, q, nt)).then_inc(s_fin, 1)
                elif k < 4:
                    normalise(k, q, nt, U).then_inc(s_ln, 1)
                    if k == 3:
                        S.link(normalise(3, q, nt, part(X, q, nt), 1))
                        if not (fixed(q) and q == 0):
                            wait(act, s_tab, q * 16 + 16 * NQ * 3)
                        for t in range(nt):
                            last = fn(Z[:, QW + t * D:QW + (t + 1) * D], at(X, q * QW + t * D, D), ACT.Copy,
                                      scale=at(ROUT, q * QT + t))
                        last.then_inc(s_fin, 1)

            for k in range(PASSES):
                if k == 5:
                    expert_scalar(act, S, normalise)
                    act.wait_ge(s_rec[1], 16)
                for h in range(2):
                    stage_gather(k, 0, h, True)
                with act.Fori(1, NR - 1) as i:
                    for h in range(2):
                        stage_gather(k, i, h, False)
                stage_gather(k, NR - 1, 0, False)
                if k == 1:
                    act.wait_ge(s_deg, 1)
                    fn(RIN[:, :], RIN[:, :], ACT.Sqrt)
                    fn(ROUT[:, :], ROUT[:, :], ACT.Sqrt).then_inc(s_degq, 1)
                act.wait_ge(s_w, w_count(k))
                if k == 3:
                    act.wait_ge(s_deg, 2)
                copy_transposes(k, 0, QT)
                for q, nt, nxt in groups(act, S, {0: QT, 3: 1}.get(k, 0)):
                    early(k, q, nt, nxt)
                    if not (fixed(q) and q == 0):
                        late(k, q - 1, QT)
                late(k, NQ - 1, NT - (NQ - 1) * QT)

        @block.vector
        def _(dve):
            V = Steps(dve, s_dve)
            v = nc.vector
            v.memset(Hb[:, 0:2 * EW].bitcast(i32), -1)
            v.memset(DNEXT, 1 << 30)
            v.memset(RAWS, 0.0)
            v.memset(RAWL.bitcast(i32), -1)
            v.memset(RAWW, 0.0)
            v.memset(WE, 0.0)
            v.memset(X[:, (NT - 1) * D:NT * D], 0.0).then_inc(s_clean, 1)
            v.memset(ACC[:, :], 0.0)
            v.memset(VEC[:, 3 * D:4 * D], 0.0)
            V.link(v.memset(REC[:, :], 0.0))
            v.memset(RECV[:, :, 1], -1.0).then_inc(s_clean, 1)
            v.memset(OFF[:, :], 0.0)
            dve.wait_ge(s_const, 2)
            dve.wait_ge(s_in, 80)

            for src, hi, lo in ((DST, HI, LO), (SRC, SHI, SLO)):
                V.link(v.tensor_scalar(TMI, src, 7, None, ALU.arith_shift_right))
                V.link(v.tensor_copy(hi, TMI))
                V.link(v.tensor_scalar(TMI, src, P - 1, None, ALU.bitwise_and))
                V.link(v.tensor_copy(lo, TMI))

            V.link(v.tensor_scalar(TMI, DNEXT, 7, None, ALU.arith_shift_right))
            V.link(v.tensor_copy(TMP, TMI))
            V.link(v.tensor_tensor(OH, TMP, HI, ALU.is_lt))
            v.tensor_reduce(col[:, 4:5], OH, AX.X, ALU.add).then_inc(s_order, 1)
            dve.wait_ge(s_ordp, 1)
            v.tensor_scalar(FLAG[0:1, :], bank(5, 1)[0:1, :], 1.0, None, ALU.min).then_inc(s_flag, 1)

            def rank_step(V, hi, h, n):
                V.sync()
                if n == 0:
                    V.count(v.tensor_scalar(OH[:, 0:EC], hi[:, 0:EC], at(iota, h), None, ALU.is_equal))
                if n == 1:
                    V.count(v.tensor_tensor_scan(CUM[:, 0:EC], OH[:, 0:EC], OH[:, 0:EC], 0.0, ALU.add, ALU.max))
                if n == 2:
                    v.tensor_copy(at(CNT, h), CUM[:, EC - 1:EC])
                    V.count(v.tensor_tensor(TMP[:, 0:EC], OH[:, 0:EC], CUM[:, 0:EC], ALU.mult))
                if n == 3:
                    V.count(v.tensor_tensor(RK[:, 0:EC], RK[:, 0:EC], TMP[:, 0:EC], ALU.add))

            def offset_step(V, hi, h, n):
                V.sync()
                if n == 0:
                    V.count(v.tensor_scalar(OH[:, 0:EC], hi[:, 0:EC], at(iota, h), at(OFF, h), ALU.is_equal, ALU.mult))
                if n == 1:
                    V.count(v.tensor_tensor(RK[:, 0:EC], RK[:, 0:EC], OH[:, 0:EC], ALU.add))

            def chunk_tiles(V, b):
                V.sync()
                v.memset(col[:, 0:1], 0.0).then_inc(s_cnt[b], 1)
                dve.wait_ge(s_psort[b], 1)
                V.link(v.tensor_scalar(coli[0:NT, 0:1], bank(0, 1)[0:NT, :], float(P - 1), None, ALU.add))
                V.link(v.tensor_scalar(coli[0:NT, 1:2], coli[0:NT, 0:1], 7, None, ALU.arith_shift_right))
                V.link(v.tensor_copy(col[0:NT, 1:2], coli[0:NT, 1:2]))
                v.tensor_scalar(nchb[0:NT, :], ones[0:NT, :], col[0:NT, 1:2], float(P), ALU.mult, ALU.mult).then_inc(s_cnt[b], 1)
                dve.wait_ge(s_psort[b], 2)
                v.tensor_copy(OFF[:, 0:NT], bank(1, NT))
                V.link(v.tensor_copy(col[0:NT, 2:3], bank(2, 1)[0:NT, :]))
                v.tensor_scalar(CMAP[0:NT, :], IOTC[b][0:NT, :], col[0:NT, 2:3], None, ALU.is_ge).then_inc(s_cnt[b], 1)
                dve.wait_ge(s_psort[b], 3)
                for c in range(2):
                    w = NCH // 2
                    V.link(v.tensor_scalar(TTS[b][0:1, c * w:(c + 1) * w], bank(3 + c, w)[0:1, :], float(NT - 1), float(D),
                                           ALU.min, ALU.mult))

                v.memset(col[:, 0:1], 0.0).then_inc(s_cnt[b], 1)

            def slots(V, b, hi):
                V.sync()
                V.link(v.tensor_scalar(TMI, RK, -1.0, 0.0, ALU.add, ALU.max))
                V.link(v.tensor_scalar(TMJ, TMI, 7, None, ALU.arith_shift_right))
                V.link(v.tensor_copy(TMP, TMJ))
                V.link(v.tensor_scalar(TMJ, TMI, P - 1, None, ALU.bitwise_and))
                V.link(v.tensor_copy(OH, TMJ))
                V.link(v.scalar_tensor_tensor(RK, OH, float(NCH), TMP, ALU.mult, ALU.add))
                V.link(v.tensor_tensor(RK, RK, EDUMP[b], ALU.subtract))
                V.link(v.tensor_scalar(OH, hi, 0.0, None, ALU.is_ge))
                V.link(v.tensor_tensor(RK, RK, OH, ALU.mult))
                V.link(v.tensor_tensor(POS[b], RK, EDUMP[b], ALU.add))

            def records(b, other, lo):
                v.tensor_copy(RECE[b][:, :, 0], other)
                v.tensor_copy(RECE[b][:, :, 1], lo)
                if b:
                    v.tensor_copy(Hb[:, 8 * EW:12 * EW].bitcast(u32).rearrange("p (c f) -> p c f", f=4)[:, :, 3], POS[b])
                v.tensor_copy(RECE[b][:, :, 2], WE).then_inc(s_pos[b], 1)

            flag = unsorted(dve)
            with dve.If(flag == 1):
                A = Steps(dve, s_sorta)
                dve.wait_ge(s_raw, 144)
                v.memset(ring[:, :], 0.0)
                A.link(v.memset(RK, 0.0))
                for h in A.loop(0, NT, 4):
                    for n in range(4):
                        rank_step(A, HI, h, n)
                chunk_tiles(A, 0)
                for h in A.loop(0, NT, 2):
                    for n in range(2):
                        offset_step(A, HI, h, n)
                slots(A, 0, HI)
                records(0, SRC, LO)
                dve.wait_ge(s_rec[0], 16)
                v.memset(col[:, 0:1], 0.0).then_inc(s_ready, 1)
            with dve.Else():
                F = Steps(dve, s_fstep)
                dve.wait_ge(s_raw, 144)
                F.link(v.tensor_scalar(RAWH.bitcast(i32), RAWL.bitcast(i32), 7, None, ALU.arith_shift_right))
                F.link(v.tensor_copy(RAWH, RAWH.bitcast(i32)))
                ends = RAWH.rearrange("p (b c) -> p b c", c=P)[:, :, P - 1]
                F.link(v.tensor_scalar(CNT[:, 0:EB], ends, 0.0, 1000.0, ALU.is_lt, ALU.mult))
                F.link(v.tensor_tensor(CNT[:, 0:EB], CNT[:, 0:EB], ends, ALU.add))
                v.tensor_tensor(GE, iota[:, 0:NT].unsqueeze(1).broadcast_to((P, EB, NT)),
                                CNT[:, 0:EB].unsqueeze(2).broadcast_to((P, EB, NT)), ALU.is_ge).then_inc(s_sel, 1)
                F.link(v.tensor_scalar(RAWL.bitcast(i32), RAWL.bitcast(i32), P - 1, None, ALU.bitwise_and))
                v.tensor_copy(RAWL, RAWL.bitcast(i32))
                v.tensor_copy(RAWS, RAWS.bitcast(i32))
                dve.wait_ge(s_fprod, 1)
                lane = DUMP[:, 0:1]
                F.link(v.tensor_scalar(col[0:NT, 1:2], bank(0, 1)[0:NT, :], lane[0:NT, :], float(1 - MC * P), ALU.add, ALU.add))
                v.tensor_scalar(CMAP[0:NT, :], IOTC[0][0:NT, :], col[0:NT, 1:2], None, ALU.is_ge).then_inc(s_sel, 1)
                dve.wait_ge(s_fprod, 2)
                dve.wait_ge(s_init[1], 16)
                w = NCH // 2
                for c in range(2):
                    F.link(v.tensor_scalar(RECV[:, c * w:(c + 1) * w, 3], bank(1 + c, w), float(NT - 1), None, ALU.min))
                F.link(v.tensor_tensor(IOTC[0], IOTC[0], RECV[:, :, 3], ALU.subtract))
                for n in range(EB):
                    v.tensor_scalar(SEL[n], IOTC[0], lane, float(n * P - MC * P), ALU.subtract, ALU.is_equal).then_inc(s_sel, 1)
                dve.wait_ge(s_sel, 2 + EB)
                F.link(v.tensor_scalar(TTS[0][0:1, :], RECV[0:1, :, 3], float(D), None, ALU.mult))
                dve.wait_ge(s_fprod, 3)
                for c in range(2):
                    s = slice(c * w, (c + 1) * w)
                    v.tensor_copy(RECV[:, s, 0], bank(c, w))
                    v.tensor_copy(RECV[:, s, 2], bank(4 + c, w))
                    F.link(v.tensor_tensor(RECV[:, s, 1], bank(6 + c, w), RECV[:, s, 3], ALU.is_equal))
                    F.link(v.scalar_tensor_tensor(RECV[:, s, 1], bank(2 + c, w), 1.0, RECV[:, s, 1], ALU.add, ALU.mult))
                    last = v.tensor_scalar(RECV[:, s, 1], RECV[:, s, 1], -1.0, None, ALU.add)
                    F.link(last) if c == 0 else last.then_inc(s_ready, 1)
            dve.wait_ge(s_ready, 1)
            V.link(v.memset(RK, 0.0))

            def one_hot(b, i, h, n):
                hi, lo = ((HI, LO), (SHI, SLO))[b]
                c = (i - 1) * ROUND + h * HALF
                if n == 0:
                    if not (fixed(i) and i == 1):
                        dve.wait_ge(s_hist[2 * b + h], i - 1)
                    l3 = at(lo, c, HALF).unsqueeze(2).broadcast_to((P, HALF, P))
                    v.tensor_tensor(OHL[2 * b + h], iota[:, :].unsqueeze(1).broadcast_to((P, HALF, P)), l3, ALU.is_equal)
                else:
                    h3 = at(hi, c, HALF).unsqueeze(2).broadcast_to((P, HALF, NT))
                    v.tensor_tensor(OHH[2 * b + h], iota[:, 0:NT].unsqueeze(1).broadcast_to((P, HALF, NT)), h3,
                                    ALU.is_equal).then_inc(s_oh[2 * b + h], 1)

            def pick_one(k, i, h, j):
                c = i * ROUND + h * HALF + j
                p = pick[:, (h * HALF + j) * P:(h * HALF + j + 1) * P]
                lo = RECV[:, c, 1:2] if fixed(c) else REC[:, DS(c * 4 + 1, 1)]
                we = RECV[:, c, 2:3] if fixed(c) else REC[:, DS(c * 4 + 2, 1)]
                if k in (0, 5):
                    last = v.tensor_scalar(p, iota[:, :], lo, we, ALU.is_equal, ALU.mult)
                else:
                    last = v.tensor_scalar(p, iota[:, :], lo, None, ALU.is_equal)
                if j == HALF - 1:
                    last.then_inc(s_pick, 1)

            def add_half(k, i, h, more=True):
                n = i * 2 + NH * k + h
                c = i * ROUND + h * HALF
                at_tile = load_values(dve, TTS[k == 5], c, HALF, (NT - 1) * D)
                dve.wait_ge(s_prod, n + 1)
                for j, t in enumerate(at_tile):
                    if more:
                        pick_one(k, i + 1, h, j)
                    if not (fixed(n) and n + j == 0):
                        dve.wait_ge(s_acc, n * HALF + j)
                    slot = h * HALF + j
                    v.tensor_tensor(ACC[:, DS(t, D)], ACC[:, DS(t, D)], PS[:, slot * D:(slot + 1) * D], ALU.add).then_inc(s_acc, 1)
                    if k > 1 or (fixed(i) and i == NR - 1):
                        continue
                    if k == 0:
                        if j in (1, 3):
                            rank_step(V, SHI, i, h * 2 + j // 2)
                        if j == 5:
                            one_hot(0, i + 1, 0, h)
                    else:
                        if j == 1:
                            offset_step(V, SHI, i, h)
                        if j in (2, 3):
                            one_hot(1, i + 1, h, j - 2)
                        if j == 5:
                            one_hot(0, i + 1, 1, h)

            def statistics(key, q, nt, second=0):
                for t in range(nt):
                    last = v.bn_stats(ST[:, t * 6:(t + 1) * 6], U[:, t * D:(t + 1) * D])
                V.alone = True
                V.link(last)
                for t in range(nt):
                    last = v.bn_aggr(MV[:, t * 2:t * 2 + 2], ST[:, t * 6:(t + 1) * 6])
                V.link(last)
                mv = MV[:, 0:2 * nt].rearrange("p (t s) -> p t s", s=2)
                v.tensor_scalar(SM[:, 0:nt], mv[:, :, 1], LN_EPS, None, ALU.add).then_inc(s_var, 1)
                n = ln_count(key, q, second)
                dve.wait_ge(s_sd, n)
                V.link(v.reciprocal(SM[:, 8:8 + nt], SM[:, 4:4 + nt]))
                v.scalar_tensor_tensor(SM[:, 12:12 + nt], mv[:, :, 0], -1.0, SM[:, 8:8 + nt], ALU.mult, ALU.mult).then_inc(s_rs, 1)

            def consume(k, q, nt):
                dve.wait_ge(s_mm, q + NQ * k + 1)
                if k == 4:
                    dve.wait_ge(s_gate, q + 1)
                    v.tensor_copy(part(ACC, q, nt), U[:, 0:nt * D]).then_inc(s_u, 1)
                    dve.wait_ge(s_lg, q + 1)
                    v.tensor_copy(at(Hb, q * (QT * NE), nt * NE), bank(6, nt * NE)).then_inc(s_lgc, 1)
                    return
                if not (fixed(q) and q == 0):
                    dve.wait_ge(s_fin, q + NQ * k)
                if k == 0:
                    dve.wait_ge(s_nrm, q + 1)
                    V.link(v.tensor_scalar(SM[:, 20:20 + nt], SM[:, 20:20 + nt], 1e-12, None, ALU.max))
                    V.link(v.reciprocal(SM[:, 20:20 + nt], SM[:, 20:20 + nt]))
                    for t in range(nt):
                        last = v.scalar_tensor_tensor(U[:, t * D:(t + 1) * D], bank(4 + t // 2, D, t % 2 * D), SM[:, 20 + t:21 + t],
                                                      at(X, q * QW + t * D, D), ALU.mult, ALU.add)
                else:
                    last = v.tensor_tensor(U[:, 0:nt * D], PS[:, 2048:2048 + nt * D], part(Hb if k in (2, 3) else X, q, nt), ALU.add)
                last.then_inc(s_u, 1)
                dve.wait_ge(s_u, q + NQ * k + 1)
                if k:
                    V.link(v.tensor_tensor(tiles(U[:, 0:nt * D], nt), tiles(U[:, 0:nt * D], nt), vec(0, nt), ALU.add))
                statistics(k, q, nt)
                if k in (1, 2, 3):
                    dve.wait_ge(s_ln, q + NQ * (k - 1) + 1)
                    u = tiles(U[:, 0:nt * D], nt)
                    V.link(v.tensor_tensor(u, u, vec(1, nt), ALU.mult))
                    V.link(v.tensor_tensor(u, u, vec(2, nt), ALU.add))
                    if k < 3:
                        v.tensor_scalar(part(Hb, q, nt), U[:, 0:nt * D], 0.0, None, ALU.max).then_inc(s_fin, 1)
                    else:
                        V.link(v.scalar_tensor_tensor(U[:, 0:nt * D], U[:, 0:nt * D], 0.0, part(X, q, nt), ALU.max, ALU.add))
                        statistics(3, q, nt, 1)

            PER = {0: 5, 1: 6, 2: 6, 3: 10, 4: 0, 5: 4}
            for k in range(PASSES):
                if k == 5:
                    expert_vector(dve, V, statistics)
                    dve.wait_ge(s_rec[1], 16)
                if k:
                    dve.wait_ge(s_fin, NQ * k)
                    V.link(v.memset(ACC[:, :], 0.0))
                for h in range(2):
                    for j in range(HALF):
                        pick_one(k, 0, h, j)
                for h in range(2):
                    add_half(k, 0, h)
                if k < 2:
                    for i in V.loop(1, NR - 2, 4 - 2 * k):
                        for h in range(2):
                            add_half(k, i, h)
                else:
                    with dve.Fori(1, NR - 2) as i:
                        for h in range(2):
                            add_half(k, i, h)
                add_half(k, NR - 2, 0)
                add_half(k, NR - 2, 1, False)
                add_half(k, NR - 1, 0, False)
                dve.wait_ge(s_acc, NCH * (k + 1))
                if k == 0:
                    dve.wait_ge(s_hist[0], NR - 1)
                    chunk_tiles(V, 1)
                if k == 1:
                    for n in range(1, 4):
                        dve.wait_ge(s_hist[n], NR - 1)
                    v.tensor_scalar(RIN[:, :], bank(6, NT), 1.0, None, ALU.max)
                    v.tensor_scalar(ROUT[:, :], bank(7, NT), 1.0, None, ALU.max).then_inc(s_deg, 1)
                    dve.wait_ge(s_dump, 1)
                    slots(V, 1, SHI)
                    records(1, DST, SLO)
                    dve.wait_ge(s_degq, 1)
                    V.link(v.reciprocal(RIN[:, :], RIN[:, :]))
                    v.reciprocal(ROUT[:, :], ROUT[:, :]).then_inc(s_deg, 1)
                    dve.wait_ge(s_pend, 16)
                dve.wait_ge(s_w, w_count(k))
                if k == 0:
                    dve.wait_ge(s_x, 32)
                if k in (1, 2, 3):
                    v.tensor_scalar(EPS1[:, :], EPS1[:, :], 1.0, None, ALU.add).then_inc(s_vec, 1)
                if k == 4:
                    v.tensor_tensor(VEC[:, 0:D], VEC[:, 0:D], VEC[:, D:2 * D], ALU.add).then_inc(s_vec, 1)
                if k == 5:
                    v.tensor_scalar(VEC[:, D:2 * D], VEC[:, D:2 * D], 1.0, None, ALU.add).then_inc(s_vec, 1)
                for q, nt, nxt in groups(dve, V, PER[k]):
                    consume(k, q, nt)


_INS = [
    "x", "src", "dst", "edge_weight", "L0_gnn_w_self", "L0_gnn_w_neigh", "L1_gnn_W1", "L1_gnn_b1",
    "L1_gnn_W2", "L1_gnn_b2", "L1_gnn_eps", "L1_gnn_gamma", "L1_gnn_beta", "L2_gnn_W_gc", "L2_gnn_b_gc",
    "L2_gnn_W_res", "L2_gnn_b_res", "L2_gnn_Wg", "L2_gnn_bg", "L2_gnn_w1", "L2_gnn_b1", "L2_gnn_w2",
    "L2_gnn_b2", "L2_gnn_gamma", "L2_gnn_beta", "L3_gnn_weight", "L3_gnn_learnable_diag", "L3_gnn_bias",
]


def kernel(**inputs):
    import numpy as np
    import concourse.bacc as bacc
    from concourse.bass_utils import run_bass_kernel_spmd as run

    nc = bacc.Bacc("TRN2", target_bir_lowering=False, num_devices=1)
    arrays, aps = {}, {}
    for name in _INS:
        v = np.ascontiguousarray(inputs[name])
        arrays[f"in_{name}"] = v
        aps[name] = nc.dram_tensor(f"in_{name}", v.shape, mybir.dt.from_np(v.dtype), kind="ExternalInput").ap()
    out = nc.dram_tensor("out", (N, D), mybir.dt.float32, kind="ExternalOutput").ap()
    gnn(nc, aps, out)
    return run(nc, [arrays], core_ids=[0]).results[0]["out"]
```
